# Optimizing a Trainium2 kernel written in Bass

```python
import numpy as np
import jax
import jax.numpy as jnp

def _softmax(x, axis=-1):
    return jax.nn.softmax(x, axis=axis)

def _gelu(x):
    return jax.nn.gelu(x, approximate=True)

def _silu(x):
    return jax.nn.silu(x)

def _sigmoid(x):
    return jax.nn.sigmoid(x)

def _layernorm(x, axis=-1, eps=1e-05):
    m = jnp.mean(x, axis=axis, keepdims=True)
    v = jnp.var(x, axis=axis, keepdims=True)
    return (x - m) / jnp.sqrt(v + eps)

def _scatter_add(tgt, idx, src, axis=0):
    return tgt.at[idx].add(src)

def _segment_sum(src, seg, n):
    return jax.ops.segment_sum(src, seg, n)
kernel_name = 'mk_xattn_ffn_d4_seqx_r8_bd645d'

def setup_inputs(seed: int=0):
    np.random.seed(seed)
    _w = jnp.asarray

    def _rec_inputs():
        import jax
        import jax.numpy as jnp
        _rk = jax.random.key(seed)
        x = 7.22e-05 + 1 * jax.random.normal(jax.random.fold_in(_rk, 1), (8, 256, 128), jnp.float32)
        _lenS = 256 - jax.random.randint(jax.random.fold_in(_rk, 7), (8,), 0, max(1, 256 // 4) + 1, jnp.int32)
        _lenS2 = 256 - jax.random.randint(jax.random.fold_in(_rk, 8), (8,), 0, max(1, 256 // 4) + 1, jnp.int32)
        _ctx_1024P = jax.random.normal(jax.random.fold_in(_rk, 11), (8, 16, 128), jnp.float32)
        _ctx_1024c = jax.random.dirichlet(jax.random.fold_in(_rk, 511), 0.3 * jnp.ones((16,), jnp.float32), (8, 256))
        _ctx_1024t = jnp.einsum('bsk,bkd->bsd', _ctx_1024c, _ctx_1024P)
        _ctx_1024t = _ctx_1024t * jax.lax.rsqrt(jnp.mean(jnp.square(_ctx_1024t)) + 1e-12) * 0.953939
        ctx_1024 = 4.13588e-05 + 0.999923 * (_ctx_1024t + 0.3 * jax.random.normal(jax.random.fold_in(_rk, 611), (8, 256, 128), jnp.float32))
        _validS = jnp.arange(256)[None, :] < _lenS[:, None]
        _validS2 = jnp.arange(256)[None, :] < _lenS2[:, None]
        _causal = jnp.tril(jnp.ones((256, 256), dtype=bool))
        mask_BxS_ik0 = jnp.where(jnp.broadcast_to(_validS[:, :], (8, 256)), 0, 1).astype(jnp.int32)
        mask_Bx1x1xS2_ff0 = jnp.where(jnp.ones((8, 1, 1, 256), dtype=bool), 0.0, -1000000000.0).astype(jnp.float32)
        return (x, ctx_1024, mask_BxS_ik0, mask_Bx1x1xS2_ff0)
    x, ctx_1024, mask_BxS_ik0, mask_Bx1x1xS2_ff0 = _rec_inputs()

    def _L0_xattn_setup():
        import jax, jax.numpy as jnp
        import numpy as np
        NUM_HEADS = 16
        key = jax.random.key(seed)
        kq, kk, kv = jax.random.split(key, 3)
        B, S, E = (4, 256, 128)
        Q = jax.random.normal(kq, (B, S, E), dtype=jnp.float32)
        K = jax.random.normal(kk, (B, S, E), dtype=jnp.float32)
        V = jax.random.normal(kv, (B, S, E), dtype=jnp.float32)
        return {'Q': Q, 'K': K, 'V': V}
    _L0_xattn_all = _L0_xattn_setup()
    _L0_xattn_in = {k: v for k, v in _L0_xattn_all.items() if k in ()}
    del _L0_xattn_all

    def _L0_ffn_setup():
        import jax, jax.numpy as jnp
        import numpy as np
        EMB = 128
        FF = 4 * EMB

        def _ternary(w):
            scale = jnp.maximum(jnp.mean(jnp.abs(w)), 1e-08)
            w_t = jnp.clip(jnp.round(w / scale), -1.0, 1.0)
            return w + jax.lax.stop_gradient(w_t - w)
        key = jax.random.key(seed)
        kx, k1, k2, kb1, kb2 = jax.random.split(key, 5)
        x = jax.random.normal(kx, (4, 256, EMB), dtype=jnp.float32)
        lim1 = 1.0 / np.sqrt(EMB)
        lim2 = 1.0 / np.sqrt(FF)
        W1 = jax.random.uniform(k1, (FF, EMB), jnp.float32, -lim1, lim1)
        b1 = jax.random.uniform(kb1, (FF,), jnp.float32, -lim1, lim1)
        W2 = jax.random.uniform(k2, (EMB, FF), jnp.float32, -lim2, lim2)
        b2 = jax.random.uniform(kb2, (EMB,), jnp.float32, -lim2, lim2)
        return {'x': x, 'W1': W1, 'b1': b1, 'W2': W2, 'b2': b2}
    _L0_ffn_all = _L0_ffn_setup()
    _L0_ffn_in = {k: v for k, v in _L0_ffn_all.items() if k in ('W1', 'b1', 'W2', 'b2')}
    del _L0_ffn_all

    def _L1_xattn_setup():
        import jax, jax.numpy as jnp
        import numpy as np
        HEADS = 16
        DIM_HEAD = 64
        SCALE = DIM_HEAD ** (-0.5)
        MASK_NEG = 1000000.0

        def _split_heads(t):
            b, n, _ = t.shape
            return t.reshape(b, n, HEADS, DIM_HEAD).transpose(0, 2, 1, 3)
        key = jax.random.key(seed)
        ks = jax.random.split(key, 6)
        B, N, M, D = (2, 256, 256, 128)
        inner = HEADS * DIM_HEAD
        x = jax.random.normal(ks[0], (B, N, D), dtype=jnp.float32)
        context = jax.random.normal(ks[1], (B, M, D), dtype=jnp.float32)
        mask = jax.random.randint(ks[2], (B, N), 0, 2, dtype=jnp.int32)
        Wq = jax.random.normal(ks[3], (D, inner), dtype=jnp.float32) * D ** (-0.5)
        Wkv = jax.random.normal(ks[4], (D, 2 * inner), dtype=jnp.float32) * D ** (-0.5)
        Wout = jax.random.normal(ks[5], (inner, D), dtype=jnp.float32) * inner ** (-0.5)
        bout = jnp.zeros((D,), dtype=jnp.float32)
        return {'x': x, 'context': context, 'mask': mask, 'Wq': Wq, 'Wkv': Wkv, 'Wout': Wout, 'bout': bout}
    _L1_xattn_all = _L1_xattn_setup()
    _L1_xattn_in = {k: v for k, v in _L1_xattn_all.items() if k in ('Wq', 'Wkv', 'Wout', 'bout')}
    del _L1_xattn_all

    def _L1_ffn_setup():
        import jax, jax.numpy as jnp
        import numpy as np
        B, S, H = (2, 128, 128)
        KD, NH, K = (128, 8, 8)
        NE = 8192
        NK = 32
        EPS = 1e-05
        key = jax.random.key(seed)
        ks = jax.random.split(key, 5)
        inputs = jax.random.normal(ks[0], (B, S, H), jnp.float32)
        bn_gamma = jnp.ones((H,), jnp.float32)
        bn_beta = jnp.zeros((H,), jnp.float32)
        w_q = jax.random.normal(ks[1], (2 * NH * KD, H), jnp.float32) * (1.0 / np.sqrt(H))
        keys_p = jax.random.normal(ks[2], (NH, NK, 2, KD), jnp.float32) * 0.02
        lim = float(np.sqrt(6.0 / (NE + H)))
        down = jax.random.uniform(ks[3], (NE, H), jnp.float32, -lim, lim)
        up = jax.random.uniform(ks[4], (NE, H), jnp.float32, -lim, lim)
        return {'inputs': inputs, 'bn_gamma': bn_gamma, 'bn_beta': bn_beta, 'w_q': w_q, 'keys_p': keys_p, 'down': down, 'up': up}
    _L1_ffn_all = _L1_ffn_setup()
    _L1_ffn_in = {k: v for k, v in _L1_ffn_all.items() if k in ('bn_gamma', 'bn_beta', 'w_q', 'keys_p', 'down', 'up')}
    del _L1_ffn_all

    def _L2_xattn_setup():
        import jax, jax.numpy as jnp
        import numpy as np
        B, L_Q, L_KV, D, H = (4, 256, 256, 128, 16)
        key = jax.random.key(seed)
        ks = jax.random.split(key, 11)
        s = 0.02
        return {'kv': jax.random.normal(ks[0], (B, L_KV, D), dtype=jnp.float32), 'q': jax.random.normal(ks[1], (B, L_Q, D), dtype=jnp.float32), 'Wq': jax.random.normal(ks[2], (D, D), dtype=jnp.float32) * s, 'bq': jnp.zeros((D,), dtype=jnp.float32), 'Wk': jax.random.normal(ks[3], (D, D), dtype=jnp.float32) * s, 'bk': jnp.zeros((D,), dtype=jnp.float32), 'Wv': jax.random.normal(ks[4], (D, D), dtype=jnp.float32) * s, 'bv': jnp.zeros((D,), dtype=jnp.float32), 'Wo': jax.random.normal(ks[5], (D, D), dtype=jnp.float32) * s, 'bo': jnp.zeros((D,), dtype=jnp.float32)}
    _L2_xattn_all = _L2_xattn_setup()
    _L2_xattn_in = {k: v for k, v in _L2_xattn_all.items() if k in ('Wq', 'bq', 'Wk', 'bk', 'Wv', 'bv', 'Wo', 'bo')}
    del _L2_xattn_all

    def _L2_ffn_setup():
        import jax, jax.numpy as jnp
        import numpy as np
        B, T, E, C, H, G = (2, 256, 8, 128, 256, 16)
        key = jax.random.key(seed)
        ks = jax.random.split(key, 7)
        return {'hidden_states': jax.random.normal(ks[0], (B, T, C), jnp.float32), 'w_red': jax.random.normal(ks[1], (C, G), jnp.float32) * 0.02, 'wg': jax.random.normal(ks[2], (E, G), jnp.float32), 'W1': jax.random.normal(ks[3], (E, C, H), jnp.float32) * 0.02, 'b1': jax.random.normal(ks[4], (E, H), jnp.float32) * 0.02, 'W2': jax.random.normal(ks[5], (E, H, C), jnp.float32) * 0.02, 'b2': jax.random.normal(ks[6], (E, C), jnp.float32) * 0.02}
    _L2_ffn_all = _L2_ffn_setup()
    _L2_ffn_in = {k: v for k, v in _L2_ffn_all.items() if k in ('w_red', 'wg', 'W1', 'b1', 'W2', 'b2')}
    del _L2_ffn_all

    def _L3_xattn_setup():
        import jax, jax.numpy as jnp
        import numpy as np
        D_MODEL = 128
        N_HEADS = 16
        D_KV = 64
        B, S = (2, 256)

        def _split_heads(x):
            b, s, _ = x.shape
            return x.reshape(b, s, N_HEADS, D_KV).transpose(0, 2, 1, 3)
        key = jax.random.key(seed)
        ks = jax.random.split(key, 7)
        scale = 1.0 / np.sqrt(D_MODEL)
        return {'query': jax.random.normal(ks[0], (B, S, D_MODEL), jnp.float32), 'key': jax.random.normal(ks[1], (B, S, D_MODEL), jnp.float32), 'value': jax.random.normal(ks[2], (B, S, D_MODEL), jnp.float32), 'mask': jnp.zeros((B, 1, 1, S), jnp.float32), 'Wq': jax.random.normal(ks[3], (D_MODEL, N_HEADS * D_KV), jnp.float32) * scale, 'Wk': jax.random.normal(ks[4], (D_MODEL, N_HEADS * D_KV), jnp.float32) * scale, 'Wv': jax.random.normal(ks[5], (D_MODEL, N_HEADS * D_KV), jnp.float32) * scale, 'Wo': jax.random.normal(ks[6], (N_HEADS * D_KV, D_MODEL), jnp.float32) * scale}
    _L3_xattn_all = _L3_xattn_setup()
    _L3_xattn_in = {k: v for k, v in _L3_xattn_all.items() if k in ('Wq', 'Wk', 'Wv', 'Wo')}
    del _L3_xattn_all

    def _L3_ffn_setup():
        import math
        import jax, jax.numpy as jnp
        import numpy as np
        B, S, H = (4, 256, 128)
        E, K, I = (8, 2, 128)
        NSH = 2
        CF, RSF = (1.25, 1.0)
        key = jax.random.key(seed)
        ks = jax.random.split(key, 8)
        w = lambda k, sh: jax.random.normal(k, sh, dtype=jnp.float32) * 0.02
        return {'hidden_states': jax.random.normal(ks[0], (B, S, H), dtype=jnp.float32), 'gate_w': w(ks[1], (E, H)), 'we_gate': w(ks[2], (E, I, H)), 'we_up': w(ks[3], (E, I, H)), 'we_down': w(ks[4], (E, H, I)), 'ws_gate': w(ks[5], (NSH * I, H)), 'ws_up': w(ks[6], (NSH * I, H)), 'ws_down': w(ks[7], (H, NSH * I))}
    _L3_ffn_all = _L3_ffn_setup()
    _L3_ffn_in = {k: v for k, v in _L3_ffn_all.items() if k in ('gate_w', 'we_gate', 'we_up', 'we_down', 'ws_gate', 'ws_up', 'ws_down')}
    del _L3_ffn_all
    return {'x': x, 'ctx_1024': ctx_1024, 'mask_BxS_ik0': mask_BxS_ik0, 'mask_Bx1x1xS2_ff0': mask_Bx1x1xS2_ff0, 'L0_ffn_W1': _L0_ffn_in['W1'], 'L0_ffn_b1': _L0_ffn_in['b1'], 'L0_ffn_W2': _L0_ffn_in['W2'], 'L0_ffn_b2': _L0_ffn_in['b2'], 'L1_xattn_Wq': _L1_xattn_in['Wq'], 'L1_xattn_Wkv': _L1_xattn_in['Wkv'], 'L1_xattn_Wout': _L1_xattn_in['Wout'], 'L1_xattn_bout': _L1_xattn_in['bout'], 'L1_ffn_bn_gamma': _L1_ffn_in['bn_gamma'], 'L1_ffn_bn_beta': _L1_ffn_in['bn_beta'], 'L1_ffn_w_q': _L1_ffn_in['w_q'], 'L1_ffn_keys_p': _L1_ffn_in['keys_p'], 'L1_ffn_down': _L1_ffn_in['down'], 'L1_ffn_up': _L1_ffn_in['up'], 'L2_xattn_Wq': _L2_xattn_in['Wq'], 'L2_xattn_bq': _L2_xattn_in['bq'], 'L2_xattn_Wk': _L2_xattn_in['Wk'], 'L2_xattn_bk': _L2_xattn_in['bk'], 'L2_xattn_Wv': _L2_xattn_in['Wv'], 'L2_xattn_bv': _L2_xattn_in['bv'], 'L2_xattn_Wo': _L2_xattn_in['Wo'], 'L2_xattn_bo': _L2_xattn_in['bo'], 'L2_ffn_w_red': _L2_ffn_in['w_red'], 'L2_ffn_wg': _L2_ffn_in['wg'], 'L2_ffn_W1': _L2_ffn_in['W1'], 'L2_ffn_b1': _L2_ffn_in['b1'], 'L2_ffn_W2': _L2_ffn_in['W2'], 'L2_ffn_b2': _L2_ffn_in['b2'], 'L3_xattn_Wq': _L3_xattn_in['Wq'], 'L3_xattn_Wk': _L3_xattn_in['Wk'], 'L3_xattn_Wv': _L3_xattn_in['Wv'], 'L3_xattn_Wo': _L3_xattn_in['Wo'], 'L3_ffn_gate_w': _L3_ffn_in['gate_w'], 'L3_ffn_we_gate': _L3_ffn_in['we_gate'], 'L3_ffn_we_up': _L3_ffn_in['we_up'], 'L3_ffn_we_down': _L3_ffn_in['we_down'], 'L3_ffn_ws_gate': _L3_ffn_in['ws_gate'], 'L3_ffn_ws_up': _L3_ffn_in['ws_up'], 'L3_ffn_ws_down': _L3_ffn_in['ws_down']}

def reference(x, ctx_1024, mask_BxS_ik0, mask_Bx1x1xS2_ff0, L0_ffn_W1, L0_ffn_b1, L0_ffn_W2, L0_ffn_b2, L1_xattn_Wq, L1_xattn_Wkv, L1_xattn_Wout, L1_xattn_bout, L1_ffn_bn_gamma, L1_ffn_bn_beta, L1_ffn_w_q, L1_ffn_keys_p, L1_ffn_down, L1_ffn_up, L2_xattn_Wq, L2_xattn_bq, L2_xattn_Wk, L2_xattn_bk, L2_xattn_Wv, L2_xattn_bv, L2_xattn_Wo, L2_xattn_bo, L2_ffn_w_red, L2_ffn_wg, L2_ffn_W1, L2_ffn_b1, L2_ffn_W2, L2_ffn_b2, L3_xattn_Wq, L3_xattn_Wk, L3_xattn_Wv, L3_xattn_Wo, L3_ffn_gate_w, L3_ffn_we_gate, L3_ffn_we_up, L3_ffn_we_down, L3_ffn_ws_gate, L3_ffn_ws_up, L3_ffn_ws_down):
    import jax
    import jax.numpy as jnp

    def _L0_xattn_ref(Q, K, V):
        import jax, jax.numpy as jnp
        import numpy as np
        NUM_HEADS = 16
        B, S, E = Q.shape
        H = NUM_HEADS
        d_k = E // H
        q = Q.reshape(B, S, H, d_k).transpose(0, 2, 1, 3)
        k = K.reshape(B, S, H, d_k).transpose(0, 2, 1, 3)
        v = V.reshape(B, S, H, d_k).transpose(0, 2, 1, 3)
        scale = 1.0 / np.sqrt(d_k).astype(np.float32)
        scores = jnp.einsum('bhqd,bhkd->bhqk', q, k) * scale
        causal_mask = jnp.tril(jnp.ones((S, S), dtype=bool))
        scores = jnp.where(causal_mask, scores, jnp.finfo(scores.dtype).min)
        attn = jax.nn.softmax(scores, axis=-1)
        out = jnp.einsum('bhqk,bhkd->bhqd', attn, v)
        return out.transpose(0, 2, 1, 3).reshape(B, S, E)

    def _L0_ffn_ref(x, W1, b1, W2, b2):
        import jax, jax.numpy as jnp
        import numpy as np
        EMB = 128
        FF = 4 * EMB

        def _ternary(w):
            scale = jnp.maximum(jnp.mean(jnp.abs(w)), 1e-08)
            w_t = jnp.clip(jnp.round(w / scale), -1.0, 1.0)
            return w + jax.lax.stop_gradient(w_t - w)
        h = jnp.einsum('bsd,fd->bsf', x, _ternary(W1)) + b1
        h = jax.nn.gelu(h, approximate=False)
        out = jnp.einsum('bsf,df->bsd', h, _ternary(W2)) + b2
        return out

    def _L1_xattn_ref(x, context, mask, Wq, Wkv, Wout, bout):
        import jax, jax.numpy as jnp
        import numpy as np
        HEADS = 16
        DIM_HEAD = 64
        SCALE = DIM_HEAD ** (-0.5)
        MASK_NEG = 1000000.0

        def _split_heads(t):
            b, n, _ = t.shape
            return t.reshape(b, n, HEADS, DIM_HEAD).transpose(0, 2, 1, 3)
        kv = context @ Wkv
        k, v = jnp.split(kv, 2, axis=-1)
        q = x @ Wq
        q, k, v = (_split_heads(q), _split_heads(k), _split_heads(v))
        dots = jnp.einsum('bhnd,bhmd->bhnm', q, k) * SCALE
        dots = dots - (1.0 - mask.astype(jnp.float32))[:, None, :, None] * MASK_NEG
        attn = jax.nn.softmax(dots, axis=-1)
        out = jnp.einsum('bhnm,bhmd->bhnd', attn, v)
        b, h, n, d = out.shape
        out = out.transpose(0, 2, 1, 3).reshape(b, n, h * d)
        return out @ Wout + bout

    def _L1_ffn_ref(inputs, bn_gamma, bn_beta, w_q, keys_p, down, up):
        import jax, jax.numpy as jnp
        import numpy as np
        B, S, H = (2, 128, 128)
        KD, NH, K = (128, 8, 8)
        NE = 8192
        NK = 32
        EPS = 1e-05
        b, s, d = inputs.shape
        x = inputs.reshape(b * s, d)
        mean = x.mean(axis=0)
        var = x.var(axis=0)
        xn = (x - mean) * jax.lax.rsqrt(var + EPS) * bn_gamma + bn_beta
        xn = xn.reshape(b, s, d)
        q = (xn @ w_q.T).reshape(b, s, 2, NH, KD).transpose(2, 0, 1, 3, 4)
        sim = jnp.einsum('pbnhd,hkpd->pbnhk', q, keys_p)
        scores, idx = jax.lax.top_k(sim, K)
        all_scores = (scores[0][..., :, None] + scores[1][..., None, :]).reshape(b, s, NH, K * K)
        all_idx = (idx[0][..., :, None] * NK + idx[1][..., None, :]).reshape(b, s, NH, K * K)
        sc, pk = jax.lax.top_k(all_scores, K)
        indices = jnp.take_along_axis(all_idx, pk, axis=-1)
        wd = down[indices]
        hmid = jnp.einsum('bnd,bnhkd->bnhk', inputs, wd)
        hmid = jax.nn.sigmoid(sc) * jax.nn.gelu(hmid, approximate=False)
        wu = up[indices]
        return jnp.einsum('bnhk,bnhkd->bnd', hmid, wu)

    def _L2_xattn_ref(kv, q, Wq, bq, Wk, bk, Wv, bv, Wo, bo):
        import jax, jax.numpy as jnp
        import numpy as np
        B, L_Q, L_KV, D, H = (4, 256, 256, 128, 16)
        Bb, Lkv, Dm = kv.shape
        Lq = q.shape[1]
        hd = Dm // H
        scale = hd ** (-0.5)
        qh = (q @ Wq.T + bq).reshape(Bb, Lq, H, hd).transpose(0, 2, 1, 3)
        kh = (kv @ Wk.T + bk).reshape(Bb, Lkv, H, hd).transpose(0, 2, 1, 3)
        vh = (kv @ Wv.T + bv).reshape(Bb, Lkv, H, hd).transpose(0, 2, 1, 3)
        scores = jnp.einsum('bhqd,bhkd->bhqk', qh, kh) * scale
        mask = jnp.arange(Lkv)[None, :] <= jnp.arange(Lq)[:, None]
        scores = jnp.where(mask[None, None], scores, -jnp.inf)
        attn = jax.nn.softmax(scores, axis=-1)
        out = jnp.einsum('bhqk,bhkd->bhqd', attn, vh)
        out = out.transpose(0, 2, 1, 3).reshape(Bb, Lq, Dm)
        return out @ Wo.T + bo

    def _L2_ffn_ref(hidden_states, w_red, wg, W1, b1, W2, b2):
        import jax, jax.numpy as jnp
        import numpy as np
        B, T, E, C, H, G = (2, 256, 8, 128, 256, 16)
        b, t, c = hidden_states.shape
        x = hidden_states.reshape(-1, c)
        x_red = x @ w_red
        wg_n = wg / jnp.maximum(jnp.linalg.norm(wg, axis=1, keepdims=True), 0.0001)
        logits = x_red @ wg_n.T
        gates = jax.nn.softmax(logits, axis=1)
        scores = jnp.max(gates, axis=1)
        idx = jnp.argmax(gates, axis=1)
        h = jnp.einsum('nc,ech->neh', x, W1) + b1[None]
        h = jnp.take_along_axis(h, idx[:, None, None], axis=1)[:, 0, :]
        h = jax.nn.gelu(h, approximate=False)
        o = jnp.einsum('nh,ehc->nec', h, W2) + b2[None]
        o = jnp.take_along_axis(o, idx[:, None, None], axis=1)[:, 0, :]
        o = o * scores[:, None]
        return o.reshape(b, t, c)

    def _L3_xattn_ref(query, key, value, mask, Wq, Wk, Wv, Wo):
        import jax, jax.numpy as jnp
        import numpy as np
        D_MODEL = 128
        N_HEADS = 16
        D_KV = 64
        B, S = (2, 256)

        def _split_heads(x):
            b, s, _ = x.shape
            return x.reshape(b, s, N_HEADS, D_KV).transpose(0, 2, 1, 3)
        q = _split_heads(query @ Wq)
        k = _split_heads(key @ Wk)
        v = _split_heads(value @ Wv)
        scores = jnp.einsum('bhqd,bhkd->bhqk', q, k) / jnp.sqrt(jnp.asarray(D_KV, (scores_dtype := q.dtype)))
        scores = scores + mask
        attn = jax.nn.softmax(scores, axis=-1)
        ctx = jnp.einsum('bhqk,bhkd->bhqd', attn, v)
        ctx = ctx.transpose(0, 2, 1, 3).reshape(query.shape[0], -1, N_HEADS * D_KV)
        hidden = ctx @ Wo
        return hidden

    def _L3_ffn_ref(hidden_states, gate_w, we_gate, we_up, we_down, ws_gate, ws_up, ws_down):
        import math
        import jax, jax.numpy as jnp
        import numpy as np
        B, S, H = (4, 256, 128)
        E, K, I = (8, 2, 128)
        NSH = 2
        CF, RSF = (1.25, 1.0)
        orig_shape = hidden_states.shape
        x = hidden_states.reshape(-1, H)
        N = x.shape[0]
        logits = x.astype(jnp.float32) @ gate_w.astype(jnp.float32).T
        scores = jax.nn.softmax(logits, axis=-1)
        topk_w, topk_idx = jax.lax.top_k(scores, K)
        topk_w = topk_w / (topk_w.sum(-1, keepdims=True) + 1e-20) * RSF
        capacity = math.ceil(CF * N * K / E)
        flat = topk_idx.reshape(-1)
        one_hot = jax.nn.one_hot(flat, E, dtype=jnp.int32)
        pos = jnp.cumsum(one_hot, axis=0) - 1
        pos_tok = jnp.take_along_axis(pos, flat[:, None], axis=1)[:, 0]
        keep = (pos_tok < capacity).reshape(N, K)
        topk_w = topk_w * keep.astype(topk_w.dtype)
        comb = jnp.zeros((N, E), jnp.float32).at[jnp.arange(N)[:, None], topk_idx].add(topk_w)
        g = jnp.einsum('nh,eih->nei', x, we_gate)
        u = jnp.einsum('nh,eih->nei', x, we_up)
        eo = jnp.einsum('nei,ehi->neh', jax.nn.silu(g) * u, we_down)
        y = jnp.einsum('neh,ne->nh', eo, comb)
        sh = jax.nn.silu(x @ ws_gate.T) * (x @ ws_up.T) @ ws_down.T
        return (y + sh).reshape(orig_shape)
    x = x + _L0_xattn_ref(_layernorm(x, axis=-1), ctx_1024, ctx_1024)
    x = x + _L0_ffn_ref(_layernorm(x, axis=-1), L0_ffn_W1, L0_ffn_b1, L0_ffn_W2, L0_ffn_b2)
    x = x + _L1_xattn_ref(_layernorm(x, axis=-1), ctx_1024, mask_BxS_ik0, L1_xattn_Wq, L1_xattn_Wkv, L1_xattn_Wout, L1_xattn_bout)
    x = x + _L1_ffn_ref(_layernorm(x, axis=-1), L1_ffn_bn_gamma, L1_ffn_bn_beta, L1_ffn_w_q, L1_ffn_keys_p, L1_ffn_down, L1_ffn_up)
    x = x + _L2_xattn_ref(ctx_1024, _layernorm(x, axis=-1), L2_xattn_Wq, L2_xattn_bq, L2_xattn_Wk, L2_xattn_bk, L2_xattn_Wv, L2_xattn_bv, L2_xattn_Wo, L2_xattn_bo)
    x = x + _L2_ffn_ref(_layernorm(x, axis=-1), L2_ffn_w_red, L2_ffn_wg, L2_ffn_W1, L2_ffn_b1, L2_ffn_W2, L2_ffn_b2)
    x = x + _L3_xattn_ref(_layernorm(x, axis=-1), ctx_1024, ctx_1024, mask_Bx1x1xS2_ff0, L3_xattn_Wq, L3_xattn_Wk, L3_xattn_Wv, L3_xattn_Wo)
    x = x + _L3_ffn_ref(_layernorm(x, axis=-1), L3_ffn_gate_w, L3_ffn_we_gate, L3_ffn_we_up, L3_ffn_we_down, L3_ffn_ws_gate, L3_ffn_ws_up, L3_ffn_ws_down)
    return x

_drawn_inputs = setup_inputs


def setup_inputs(seed=0):
    import zlib

    import numpy as np

    out = dict(_drawn_inputs(seed))
    spreads = {'L1_xattn_bout': (0.0, 2.0),
     'L1_ffn_bn_gamma': (1.0, 0.6),
     'L1_ffn_bn_beta': (0.0, 2.0),
     'L2_xattn_bq': (0.0, 2.0),
     'L2_xattn_bk': (0.0, 2.0),
     'L2_xattn_bv': (0.0, 2.0),
     'L2_xattn_bo': (0.0, 2.0)}
    factors = {'L0_ffn_b1': 8.0,
     'L0_ffn_b2': 34.484,
     'L1_xattn_Wq': 8.0,
     'L1_xattn_Wkv': 8.0,
     'L1_xattn_Wout': 8.0,
     'L1_ffn_w_q': 26.112,
     'L1_ffn_keys_p': 25.274,
     'L1_ffn_down': 28.092,
     'L1_ffn_up': 25.303,
     'L2_xattn_Wq': 8.0,
     'L2_xattn_Wk': 8.0,
     'L2_xattn_Wv': 8.0,
     'L2_xattn_Wo': 8.0,
     'L2_ffn_w_red': 8.0,
     'L2_ffn_wg': 8.0,
     'L2_ffn_W1': 8.0,
     'L2_ffn_b1': 64.0,
     'L2_ffn_W2': 8.0,
     'L2_ffn_b2': 64.0,
     'L3_xattn_Wq': 8.0,
     'L3_xattn_Wk': 8.0,
     'L3_xattn_Wv': 5.356,
     'L3_xattn_Wo': 5.329,
     'L3_ffn_gate_w': 34.674,
     'L3_ffn_we_gate': 33.361,
     'L3_ffn_we_up': 29.406,
     'L3_ffn_we_down': 29.338,
     'L3_ffn_ws_gate': 26.046,
     'L3_ffn_ws_up': 23.048,
     'L3_ffn_ws_down': 23.179}
    for name, (base, spread) in spreads.items():
        noise = np.random.default_rng([zlib.crc32(name.encode()), seed]).standard_normal(out[name].shape)
        drawn = base * np.exp(spread * noise) if base else spread * noise
        out[name] = jnp.asarray(drawn.astype(out[name].dtype))
    for name, factor in factors.items():
        out[name] = (out[name] * factor).astype(out[name].dtype)
    return out
```

```python
from contextlib import ExitStack

import concourse.bass as bass
from concourse import mybir
from concourse.alu_op_type import AluOpType as ALU

ACT = mybir.ActivationFunctionType
AX = mybir.AxisListType.X
F32 = mybir.dt.float32
BF16 = mybir.dt.bfloat16
I32 = mybir.dt.int32
U32 = mybir.dt.uint32

P = 128
D = 128
BATCH, SEQ = 8, 256
TOKENS = BATCH * SEQ
TILES = TOKENS // P
TPB = SEQ // P
HEADS = 16
PAIRS = HEADS // 2
GROUP = 512
GROUPS = TOKENS // GROUP
TPG = GROUP // P
EPS = 1e-5
PENALTY = 1.0e6
RSQRT_SEED = float(0x5F3759DF)
NEWTON = 3
LN_CHAIN = 4 * NEWTON


LAYERS = ["raw", "ffn0", "rows", "ffn1", "bias", "ffn2", "keys", "ffn3"]


def take_counts(layer, c):
    layer.scores, layer.exp, layer.rawmax, layer.negmax = c["scores"], c["exp"], c["rawmax"], c["negmax"]
    layer.rinv, layer.norm, layer.tp, layer.pt, layer.av = c["rinv"], c["norm"], c["tp"], c["pt"], c["av"]
    layer.ot, layer.km, layer.qt, layer.vc, layer.ctx = c["ot"], c["km"], c["qt"], c["vc"], c["ctx"]
    layer.xn, layer.ln, layer.stat, layer.nat = c["xn"], c["ln"], c["stat"], c["nat"]
    layer.stages = c["stages"]


class Attention:

    def __init__(self, kind, base):
        self.kind = kind
        self.wide = kind in ("rows", "keys")
        self.causal = not self.wide
        self.scale = 1.0 if self.wide else 8 ** -0.5
        self.slabs = PAIRS if self.wide else 1
        take_counts(self, base)
        self.uses = {part: [u for t in range(PAIRS) for slot in "ABC" for u in self.bank_uses(part, t, slot)]
                     for part in ("first", "loop", "last")}
        if self.wide:
            self.uses["pre"] = ["ln", "qk0", "v0", "qk1", "qk2", "v1", "qk3"]
        else:
            self.uses["pre"] = {"raw": ["ln"], "bias": ["ln", "k", "q"]}[kind]
        self.uses["epi"] = ["back"] if kind == "raw" else ["out", "back"]
        self.fill0, self.drain0 = {}, {}
        fills, drains = base["fill"], base["drain"]
        for part, times in (("pre", 1), ("first", 1), ("loop", BATCH - 2), ("last", 1), ("epi", 1)):
            self.fill0[part], self.drain0[part] = fills, drains
            fills += times * len(self.uses[part])
            drains += times * sum(self.drains_of(u) for u in self.uses[part])
        per = dict(scores=2, exp=2, rawmax=2, negmax=2, rinv=2, norm=2, tp=2, pt=2, av=1)
        self.after = {k: base[k] + v * BATCH * PAIRS for k, v in per.items()}
        self.after.update(
            ot=base["ot"] + (BATCH * PAIRS if self.wide else BATCH),
            km=base["km"] + (0 if self.wide else BATCH * PAIRS),
            qt=base["qt"] + (0 if self.wide else BATCH),
            vc=base["vc"] + (2 * BATCH if kind == "raw" else 0),
            ctx=base["ctx"] + BATCH, xn=base["xn"] + TPB * BATCH, ln=base["ln"] + BATCH,
            stat=base["stat"] + 7 * BATCH, nat=base["nat"] + (BATCH if kind == "raw" else 0),
            stages=base["stages"] + 1, fill=fills, drain=drains)

    def bank_uses(self, part, t, slot):
        before, after = part != "first", part != "last"
        out = []
        if self.wide:
            if slot == ("B" if t == 2 else "A") and (t < 4 or after):
                out.append(f"qk{(t + 4) % PAIRS}")
            if slot == "B" and t in (0, 1):
                out.append(f"v{t + 2}")
            if slot == "B" and t == 3 and after:
                out.append("ln")
            if slot == "B" and t in (4, 6) and after:
                out.append(f"v{(t - 4) // 2}")
            if slot == "B" and t == 5 and before:
                out.append("back")
        elif self.kind == "bias":
            if (t, slot) == (1, "B"):
                out.append("v")
            if (t, slot) == (2, "C") and after:
                out.append("k")
            if (t, slot) == (6, "B") and after:
                out.append("q")
        if (t, slot) == (5, "C") and after and not self.wide:
            out.append("ln")
        if (t, slot) == (2, "A") and before and self.kind != "raw":
            out.append("out")
        if (t, slot) == (4, "C") and before and not self.wide:
            out.append("back")
        return out

    def drains_of(self, use):
        if use.startswith("qk"):
            return 3
        return 2 if use.startswith("v") else 1

    def fills(self, part, b, use):
        n = self.fill0[part] + self.uses[part].index(use) + 1
        return n + (b - 1) * len(self.uses["loop"]) if part == "loop" else n

    def drained(self, part, b, use, whole=True):
        names = self.uses[part]
        n = self.drain0[part] + sum(self.drains_of(u) for u in names[:names.index(use) + whole])
        return n + (b - 1) * sum(self.drains_of(u) for u in names_loop(self)) if part == "loop" else n


def names_loop(A):
    return A.uses["loop"]


def known_below(g, n):
    return isinstance(g, int) and g < n


def build(nc, w, out, layers):
    with ExitStack() as ctx:
        def sb(name, shape, dt=F32):
            return ctx.enter_context(nc.sbuf_tensor("sb_" + name, shape, dt))

        def sem(name):
            return ctx.enter_context(nc.semaphore(name))

        x = sb("x", [P, TILES, D])
        xn_all = sb("xn_all", [P, TILES, D])
        xnT_all = sb("xnT_all", [P, TOKENS])
        ident = sb("ident", [P, P])
        identB = sb("identB", [P, P], BF16)
        triB = sb("triB", [P, 2, P], BF16)
        onesB = sb("onesB", [P, P], BF16)
        headmask = sb("headmask", [P, HEADS])
        stats = sb("stats", [P, TILES, 6])
        mv = sb("mv", [P, TILES, 2])
        veps = sb("veps", [P, TILES])
        vhalf = sb("vhalf", [P, TILES])
        vbits = sb("vbits", [P, TILES], U32)
        c15 = sb("c15", [P, TILES])
        scratch = sb("scratch", [P, 2])
        rstd = sb("rstd", [P, TILES])
        ntmp = sb("ntmp", [P, TILES])
        ctxT_in = sb("ctxT_in", [P, SEQ])
        ctxT = sb("ctxT", [P, SEQ])
        xn = sb("xn", [P, TPB, D])
        xnT = sb("xnT", [P, SEQ])
        QT = sb("QT", [P, PAIRS, SEQ])
        KM = sb("KM", [P, PAIRS, 2, SEQ])
        VP = sb("VP", [P, TPB, HEADS, P])
        both = sb("both", [P, 4096])
        PR = both[:, 0:2048].rearrange("p (g i h k) -> p g i h k", g=2, i=TPB, h=2)
        PT = both[:, 2048:4096].rearrange("p (g h i q) -> p g h i q", g=2, h=2, i=TPB)
        rawmax = sb("rawmax", [P, 2, TPB, 2])
        negmax = sb("negmax", [P, 2, TPB, 2])
        rowsum = sb("rowsum", [P, 2, TPB, 2])
        rinv = sb("rinv", [P, 2, TPB, 2])
        OT = sb("OT", [P, PAIRS, SEQ])
        kT_all = OT[:, 1, :]
        qT_next = OT[:, 2, :]
        ctxN = OT[:, 3, :].rearrange("p (i d) -> p i d", i=TPB)
        outT = sb("outT", [P, GROUP])
        rowmask = sb("rowmask", [P, TILES], I32)
        rowpen = sb("rowpen", [P, TILES])
        keymask = xn_all[:].rearrange("p a b -> p (a b)")
        WQ1, WK1, WV1 = (sb(n, [P, 1024]) for n in ("WQ1", "WK1", "WV1"))
        WO1 = sb("WO1", [P, PAIRS, D])
        WQ3, WK3, WV3 = (sb(n, [P, 1024]) for n in ("WQ3", "WK3", "WV3"))
        WO3 = sb("WO3", [P, PAIRS, D])
        WQ2, WK2, WV2, WO2 = (sb(n, [P, D]) for n in ("WQ2", "WK2", "WV2", "WO2"))
        bq2, bk2, bo2, bo1 = (sb(n, [P, 1]) for n in ("bq2", "bk2", "bo2", "bo1"))
        bv2 = sb("bv2", [P, D])
        bank = [ctx.enter_context(nc.psum_tensor(f"bank{i}", [P, GROUP], F32)) for i in range(8)]
        shared = bank[7]

        x_in = sem("x_in")
        const_in = sem("const_in")
        rowmask_in, keymask_in = sem("rowmask_in"), sem("keymask_in")
        rowpen_ready = sem("rowpen_ready")
        masked = sem("masked")
        w_in = [sem(f"w_in{i}") for i in range(8)]
        ctx_in, nat_in = sem("ctx_in"), sem("nat_in")
        out_done = sem("out_done")
        setup_done = sem("setup_done")
        zeros_done = sem("zeros_done")
        stage_done = sem("stage_done")
        stat_step = sem("stat_step")
        seed_ready = sem("seed_ready")
        newton_step = sem("newton_step")
        xn_ready = sem("xn_ready")
        ctx_ready = sem("ctx_ready")
        fill_done, drain_done = sem("fill_done"), sem("drain_done")
        scores_ready = sem("scores_ready")
        rawmax_done, negmax_ready = sem("rawmax_done"), sem("negmax_ready")
        exp_done = sem("exp_done")
        rinv_ready = sem("rinv_ready")
        probs_ready = sem("probs_ready")
        tp_done = sem("tp_done")
        pt_ready = sem("pt_ready")
        av_done = sem("av_done")
        ot_ready = sem("ot_ready")
        km_ready = sem("km_ready")
        qt_ready = sem("qt_ready")
        vc_ready = sem("vc_ready")
        def own_wait(dve, cell=0):
            dve.memset(scratch[:, cell:cell + 1], 0.0)

        def seed(dve, variance, n, at):
            dve.tensor_scalar(veps[:, 0:n], variance, EPS, None, ALU.add).then_inc(stat_step, 1)
            dve.tensor_scalar(vhalf[:, 0:n], variance, EPS, -0.5, ALU.add, ALU.mult).then_inc(stat_step, 1)
            dve.wait_ge(stat_step, at + 2)
            dve.tensor_scalar(vbits[:, 0:n], veps[:, 0:n].bitcast(U32), 1, None,
                              ALU.logical_shift_right).then_inc(stat_step, 1)
            dve.wait_ge(stat_step, at + 3)
            dve.tensor_scalar(rstd[:, 0:n].bitcast(I32), vbits[:, 0:n], -1.0, RSQRT_SEED,
                              ALU.mult, ALU.add).then_inc(seed_ready, 1)

        S = dict(
            x=x, xn_all=xn_all, xnT_all=xnT_all, ident=ident, identB=identB, bank=bank, outT=outT, QT=QT, OT=OT,
            both=both, KM=KM, VP=VP, stats=stats, mv=mv, veps=veps, vbits=vbits, rstd=rstd,
            onesB=onesB, w_in=w_in, const_in=const_in, stat_step=stat_step,
            seed_ready=seed_ready, newton_step=newton_step, xn_ready=xn_ready, stage_done=stage_done,
            setup_done=setup_done, seed=seed, own_wait=own_wait)

        zero = {k: 0 for k in ("scores", "exp", "rawmax", "negmax", "rinv", "norm", "tp", "pt", "av", "ot",
                               "km", "qt", "vc", "ctx", "xn", "ln", "stat", "nat", "stages", "fill", "drain")}
        kinds = LAYERS
        plan, now = [], zero
        for kind in kinds[:layers]:
            plan.append(Attention(kind, now) if not kind.startswith("ffn") else FeedForward(kind, now))
            now = plan[-1].after
        zeros, narrow = 1, 0
        for A in plan:
            if isinstance(A, Attention):
                A.narrow = narrow
                narrow += 0 if A.wide else A.after["rawmax"] - A.rawmax
                zeros += 2 if A.wide else 1
                A.zeros = zeros
        ctxT_v = w["ctxT"]
        ctxN_v = w["ctx"]
        ffn = feed_forward(nc, ctx, sb, sem, S, w)
        block = ctx.enter_context(nc.Block())
        layer_of = {k: i for i, k in enumerate(kinds)}
        weights = {"rows": (WQ1, WK1, WV1, WO1), "keys": (WQ3, WK3, WV3, WO3), "bias": (WQ2, WK2, WV2, WO2)}

        @block.sync
        def _(sp):
            sp.dma_start(x[:], w["x"]).then_inc(x_in, 16)
            for dst, name in ((ident, "ident"), (identB, "identB"), (triB, "triB"), (headmask, "headmask")):
                sp.dma_start(dst[:], w[name]).then_inc(const_in, 16)
            sp.dma_start(ctxT_in[:], ctxT_v[:, 0:SEQ]).then_inc(ctx_in, 16)
            sp.dma_start(ctxN, ctxN_v[0]).then_inc(nat_in, 16)
            ffn.loads(sp, "ffn0")
            sp.dma_start(rowmask[:], w["rowmask"]).then_inc(rowmask_in, 16)
            layer_weights = (
                ("rows", ((WQ1, "WQ1"), (WK1, "WK1"), (WV1, "WV1"), (WO1, "WO1"), (bo1, "bo1"))),
                ("ffn1", ()),
                ("bias", ((WQ2, "WQ2"), (WK2, "WK2"), (WV2, "WV2"), (WO2, "WO2"), (bq2, "bq2"),
                          (bk2, "bk2"), (bo2, "bo2"), (bv2, "bv2"))),
                ("ffn2", ()),
                ("keys", ((WQ3, "WQ3"), (WK3, "WK3"), (WV3, "WV3"), (WO3, "WO3"))),
                ("ffn3", ()))
            layers_attn = [A for A in plan if isinstance(A, Attention)]
            for A in layers_attn:
                more = A is not layers_attn[-1]
                if A.kind == "keys":
                    sp.wait_ge(ffn.lnT_done, 3 * GROUPS)
                    sp.dma_start(keymask, w["keymask"].broadcast_to([P, TOKENS])).then_inc(keymask_in, 16)
                with sp.Fori(0, BATCH - 1) as b:
                    sp.wait_ge(ctx_ready, A.ctx + b + 1)
                    sp.dma_start(ctxT_in[:], ctxT_v[:, bass.ts(b + 1, SEQ)]).then_inc(ctx_in, 16)
                    if A.kind == "raw":
                        sp.wait_ge(vc_ready, A.vc + 2 * b + 2)
                        sp.dma_start(ctxN, ctxN_v[b + 1]).then_inc(nat_in, 16)
                if more:
                    sp.wait_ge(ctx_ready, A.ctx + BATCH)
                    sp.dma_start(ctxT_in[:], ctxT_v[:, 0:SEQ]).then_inc(ctx_in, 16)
                if A is layers_attn[0]:
                    for kind, pairs in layer_weights:
                        if kind.startswith("ffn"):
                            ffn.loads(sp, kind)
                        for dst, name in pairs:
                            sp.dma_start(dst[:], w[name]).then_inc(w_in[layer_of[kind]], 16)
            for kind, pairs in layer_weights:
                sp.wait_ge(w_in[layer_of[kind]], 16 * (len(pairs) or ffn.n_loads(kind)))
            sp.wait_ge(w_in[1], 16 * ffn.n_loads("ffn0"))
            sp.wait_ge(rowmask_in, 16)
            if len(plan) > layer_of["keys"]:
                sp.wait_ge(keymask_in, 16)
            sp.wait_ge(stage_done, len(plan))
            sp.dma_start(out, x[:]).then_inc(out_done, 16)
            sp.wait_ge(out_done, 16)

        def attention_tensor(pe, A):
            WQ, WK, WV, WO = weights.get(A.kind, (None,) * 4)

            def wait_bank(part, b, use):
                if not (part == "pre" and A.drained(part, b, use, False) == 0):
                    pe.wait_ge(drain_done, A.drained(part, b, use, False))

            def put(part, b, use):
                wait_bank(part, b, use)
                if use == "ln":
                    nxt = 0 if part == "pre" else b + 1
                    pe.wait_ge(xn_ready, A.xn + TPB * nxt + TPB)
                    for i in range(TPB):
                        last = pe.transpose(shared[:, i * P:(i + 1) * P], xn[:, i, :], ident[:])
                elif use.startswith("qk"):
                    j = int(use[2:])
                    if j == 0:
                        pe.wait_ge(ctx_ready, A.ctx + (1 if part == "pre" else b + 2))
                    pe.matmul(shared[:, 0:SEQ], WQ[:, j * P:(j + 1) * P], xnT[:], start=True, stop=True)
                    last = pe.matmul(shared[:, SEQ:2 * SEQ], WK[:, j * P:(j + 1) * P], ctxT[:],
                                     start=True, stop=True)
                elif use == "q":
                    last = pe.matmul(shared[:, 0:SEQ], WQ[:], xnT[:], start=True, stop=True)
                elif use == "k":
                    pe.wait_ge(ctx_ready, A.ctx + (1 if part == "pre" else b + 2))
                    last = pe.matmul(shared[:, 0:SEQ], WK[:], ctxT[:], start=True, stop=True)
                elif use == "v":
                    for kt in range(TPB):
                        last = pe.matmul(shared[:, kt * D:(kt + 1) * D], ctxT[:, kt * P:(kt + 1) * P], WV[:],
                                         start=True, stop=True)
                elif use.startswith("v"):
                    m = int(use[1:])
                    for kt in range(TPB):
                        last = pe.matmul(shared[:, kt * 256:(kt + 1) * 256], ctxT[:, kt * P:(kt + 1) * P],
                                         WV[:, m * 256:(m + 1) * 256], start=True, stop=True)
                elif use == "out":
                    if A.wide:
                        pe.wait_ge(ot_ready, A.ot + PAIRS * b)
                    else:
                        pe.wait_ge(ot_ready, A.ot + b)
                    for j in range(A.slabs):
                        wo = WO[:, j, :] if A.wide else WO[:]
                        last = pe.matmul(shared[:, 0:SEQ], wo, OT[:, j, :], start=(j == 0),
                                         stop=(j == A.slabs - 1))
                elif use == "back":
                    if A.kind == "raw":
                        pe.wait_ge(ot_ready, A.ot + b)
                    for i in range(TPB):
                        last = pe.transpose(shared[:, i * P:(i + 1) * P], outT[:, i * P:(i + 1) * P], ident[:])
                last.then_inc(fill_done, 1)

            def scores(b, t):
                g = PAIRS * b + t
                if not known_below(g, 2):
                    pe.wait_ge(exp_done, A.exp + 2 * g - 2)
                if not A.wide:
                    pe.wait_ge(km_ready, A.km + g + 1)
                    if t == 0:
                        pe.wait_ge(qt_ready, A.qt + b + 1)
                for qt in range(TPB):
                    keys = P if A.causal and qt == 0 else SEQ
                    s = bank[2 * (t % 2) + qt][:].rearrange("p (h k) -> p h k", h=2)
                    q = QT[:, t if A.wide else 0, qt * P:(qt + 1) * P]
                    last = pe.matmul(s[:, :, 0:keys], q, KM[:, t, :, 0:keys], start=True, stop=not A.causal)
                    if A.causal:
                        last = pe.matmul(s[:, :, qt * P:(qt + 1) * P], identB[:], triB[:], start=False, stop=True)
                    last.then_inc(scores_ready, 1)

            def transposes(b, t):
                g = PAIRS * b + t
                for qt in range(TPB):
                    pe.wait_ge(probs_ready, A.norm + 2 * g + qt + 1)
                    if not known_below(g, 1):
                        pe.wait_ge(pt_ready, A.pt + 2 * g - 2 + qt + 1)
                    for h in range(2):
                        for kt in range(qt + 1 if A.causal else TPB):
                            n = h * TPB + kt
                            last = pe.transpose(bank[4 + qt][:, n * P:(n + 1) * P],
                                                PR[:, t % 2, qt, h, kt * P:(kt + 1) * P], ident[:])
                    last.then_inc(tp_done, 1)

            def weighted(part, b, t):
                g = PAIRS * b + t
                pe.wait_ge(pt_ready, A.pt + 2 * g + 2)
                if A.wide and not known_below(g, 1):
                    pe.wait_ge(ot_ready, A.ot + g)
                if not A.wide and t == 0:
                    if not known_below(b, 1):
                        pe.wait_ge(ot_ready, A.ot + b)
                    if A.kind == "raw":
                        pe.wait_ge(vc_ready, A.vc + 2 * b + 2)
                    else:
                        pe.wait_ge(drain_done, A.drained(part, b, "v"))
                rows = slice(0, P) if A.wide else slice(32 * (t // 2), 32 * (t // 2) + 32)
                for h in range(2):
                    for kt in range(TPB):
                        lo = P if A.causal and kt == 1 else 0
                        first = h == 0 and kt == 0 and (A.wide or t % 2 == 0)
                        final = h == 1 and kt == 1 and (A.wide or t % 2 == 1)
                        last = pe.matmul(bank[6][rows, lo:SEQ], VP[:, kt, 2 * t + h, rows],
                                         PT[:, t % 2, h, kt, lo:SEQ], start=first, stop=final)
                last.then_inc(av_done, 1)

            def step(part, b, t):
                g = PAIRS * b + t
                scores(b, t)
                for use in A.bank_uses(part, t, "A"):
                    put(part, b, use)
                if not known_below(g, 2):
                    weighted(part, b if t >= 2 else b - 1, (t - 2) % PAIRS)
                for use in A.bank_uses(part, t, "B"):
                    put(part, b, use)
                if not known_below(g, 1):
                    transposes(b if t >= 1 else b - 1, (t - 1) % PAIRS)
                for use in A.bank_uses(part, t, "C"):
                    put(part, b, use)

            if A.stages:
                pe.wait_ge(stage_done, A.stages)
            else:
                pe.wait_ge(const_in, 16 * 4)
            if A.kind != "raw":
                n = {"rows": 5, "bias": 8, "keys": 4}[A.kind]
                pe.wait_ge(w_in[layer_of[A.kind]], 16 * n)
            pe.wait_ge(zeros_done, A.zeros)
            for use in A.uses["pre"]:
                put("pre", 0, use)
            for t in range(PAIRS):
                step("first", 0, t)
            with pe.Fori(1, BATCH - 1) as b:
                for t in range(PAIRS):
                    step("loop", b, t)
            for t in range(PAIRS):
                step("last", BATCH - 1, t)
            weighted("last", BATCH - 1, PAIRS - 2)
            transposes(BATCH - 1, PAIRS - 1)
            weighted("last", BATCH - 1, PAIRS - 1)
            for use in A.uses["epi"]:
                put("epi", BATCH, use)

        @block.tensor
        def _(pe):
            for A in plan:
                if isinstance(A, Attention):
                    attention_tensor(pe, A)
                else:
                    ffn.tensor(pe, A)

        def attention_scalar(act, A):
            def take(part, b, use):
                if use not in ("ln", "q", "k", "out") and not use.startswith("qk"):
                    return
                act.wait_ge(fill_done, A.fills(part, b, use))
                if use == "ln":
                    dst = qT_next if A.kind == "raw" else xnT[:]
                    if A.kind == "raw" and part != "pre":
                        act.wait_ge(qt_ready, A.qt + b + 1)
                    act.activation(dst, shared[:, 0:SEQ], ACT.Copy).then_inc(drain_done, 1)
                elif use == "q":
                    if part != "pre":
                        act.wait_ge(qt_ready, A.qt + b + 1)
                    act.activation(qT_next, shared[:, 0:SEQ], ACT.Identity, bias=bq2[:]).then_inc(drain_done, 1)
                elif use == "k":
                    if part != "pre":
                        act.wait_ge(km_ready, A.km + PAIRS * b + PAIRS)
                    act.activation(kT_all, shared[:, 0:SEQ], ACT.Identity, bias=bk2[:]).then_inc(drain_done, 1)
                elif use.startswith("qk"):
                    act.activation(QT[:, int(use[2:]), :], shared[:, 0:SEQ], ACT.Copy,
                                   scale=64 ** -0.5).then_inc(drain_done, 1)
                    for h in range(2):
                        act.activation(KM[64 * h:64 * h + 64, int(use[2:]), h, :],
                                       shared[64 * h:64 * h + 64, SEQ:2 * SEQ], ACT.Copy).then_inc(drain_done, 1)
                elif use == "out":
                    bias = {"rows": bo1, "bias": bo2}.get(A.kind)
                    if bias is None:
                        act.activation(outT[:, 0:SEQ], shared[:, 0:SEQ], ACT.Copy).then_inc(drain_done, 1)
                    else:
                        act.activation(outT[:, 0:SEQ], shared[:, 0:SEQ], ACT.Identity,
                                       bias=bias[:]).then_inc(drain_done, 1)

            def spread_keys(part, b, t):
                if A.kind == "raw":
                    act.wait_ge(ctx_ready, A.ctx + b + 1)
                else:
                    if isinstance(b, int) and b == 0:
                        act.wait_ge(drain_done, A.drained("pre", 0, "k"))
                    elif t >= PAIRS - 3:
                        pass
                    else:
                        act.wait_ge(drain_done, A.drained(part, b - 1, "k"))
                src = ctxT[:] if A.kind == "raw" else kT_all
                act.activation(KM[:, t, 0, :], src, ACT.Copy, scale=headmask[:, 2 * t:2 * t + 1])
                act.activation(KM[:, t, 1, :], src, ACT.Copy,
                               scale=headmask[:, 2 * t + 1:2 * t + 2]).then_inc(km_ready, 1)

            def exps(b, t):
                g = PAIRS * b + t
                for qt in range(TPB):
                    act.wait_ge(negmax_ready, A.negmax + 2 * g + qt + 1)
                    if not known_below(g, 2):
                        act.wait_ge(tp_done, A.tp + 2 * g - 4 + qt + 1)
                    keys = P if A.causal and qt == 0 else SEQ
                    s = bank[2 * (t % 2) + qt][:].rearrange("p (h k) -> p h k", h=2)
                    for h in range(2):
                        last = act.activation(PR[:, t % 2, qt, h, 0:keys], s[:, h, 0:keys], ACT.Exp,
                                              bias=negmax[:, t % 2, qt, h:h + 1], scale=A.scale,
                                              accum_out=rowsum[:, t % 2, qt, h:h + 1])
                    last.then_inc(exp_done, 1)

            def heads_out(part, b, t):
                g = PAIRS * b + t
                if not A.wide and t != PAIRS - 1:
                    return
                act.wait_ge(av_done, A.av + g + 1)
                if A.kind == "raw":
                    act.activation(outT[:, 0:SEQ], bank[6][:, 0:SEQ], ACT.Copy).then_inc(ot_ready, 1)
                else:
                    act.activation(OT[:, t if A.wide else 0, :], bank[6][:, 0:SEQ], ACT.Copy).then_inc(ot_ready, 1)

            def step(part, b, t):
                g = PAIRS * b + t
                for use in A.bank_uses(part, t, "A"):
                    take(part, b, use)
                exps(b, t)
                if not known_below(g, 2):
                    heads_out(part, b if t >= 2 else b - 1, (t - 2) % PAIRS)
                for use in A.bank_uses(part, t, "B"):
                    take(part, b, use)
                if not A.wide and (t < 3 or part != "last"):
                    spread_keys(part, b if t < 3 else b + 1, (t + 5) % PAIRS)
                for use in A.bank_uses(part, t, "C"):
                    take(part, b, use)

            if A.stages:
                act.wait_ge(stage_done, A.stages)
            else:
                act.wait_ge(const_in, 16 * 4)
            if A.kind != "raw":
                n = {"rows": 5, "bias": 8, "keys": 4}[A.kind]
                act.wait_ge(w_in[layer_of[A.kind]], 16 * n)
            act.wait_ge(zeros_done, A.zeros)
            for use in A.uses["pre"]:
                take("pre", 0, use)
            if not A.wide:
                for t in range(PAIRS - 3):
                    spread_keys("pre", 0, t)
            for t in range(PAIRS):
                step("first", 0, t)
            with act.Fori(1, BATCH - 1) as b:
                for t in range(PAIRS):
                    step("loop", b, t)
            for t in range(PAIRS):
                step("last", BATCH - 1, t)
            heads_out("last", BATCH - 1, PAIRS - 2)
            heads_out("last", BATCH - 1, PAIRS - 1)
            for use in A.uses["epi"]:
                take("epi", BATCH, use)

        @block.scalar
        def _(act):
            for A in plan:
                if isinstance(A, Attention):
                    attention_scalar(act, A)
                else:
                    ffn.scalar(act, A)

        def attention_vector(dve, A):
            def norm_stats(b):
                base = A.stat + 7 * b
                for i in range(TPB):
                    dve.bn_stats(stats[:, i, :], x[:, TPB * b + i, :]).then_inc(stat_step, 1)
                dve.wait_ge(stat_step, base + 2)
                own_wait(dve)
                for i in range(TPB):
                    dve.bn_aggr(mv[:, i, :], stats[:, i, :]).then_inc(stat_step, 1)
                dve.wait_ge(stat_step, base + 4)
                seed(dve, mv[:, 0:TPB, 1], TPB, base + 4)

            def normalise(b):
                dve.wait_ge(newton_step, LN_CHAIN * (A.ln + b + 1))
                for i in range(TPB):
                    dve.tensor_scalar(xn[:, i, :], x[:, TPB * b + i, :], mv[:, i, 0:1], rstd[:, i:i + 1],
                                      ALU.subtract, ALU.mult).then_inc(xn_ready, 1)

            def take_context(b):
                dve.wait_ge(ctx_in, 16 * (A.ctx + b + 1))
                dve.tensor_copy(ctxT[:], ctxT_in[:]).then_inc(ctx_ready, 1)

            def take(part, b, use):
                if not (use == "back" or use in ("v", "v0", "v1", "v2", "v3")):
                    return
                dve.wait_ge(fill_done, A.fills(part, b, use))
                if use == "v":
                    for kt in range(TPB):
                        dve.tensor_tensor(diagonal(kt), shared[:, kt * D:(kt + 1) * D].rearrange(
                            "p (h c) -> p h c", h=HEADS), bv2[:].rearrange("p (h c) -> p h c", h=HEADS),
                            ALU.add).then_inc(drain_done, 1)
                elif use.startswith("v"):
                    m = int(use[1:])
                    src = shared[:].rearrange("p (kt pp h c) -> p kt pp h c", kt=TPB, pp=2, h=2)
                    for h in range(2):
                        dst = VP[:, :, 4 * m + h:4 * m + 4:2, 64 * h:64 * h + 64]
                        dve.tensor_copy(dst, src[:, :, :, h, :]).then_inc(drain_done, 1)
                elif use == "back":
                    xb = x[:, bass.ds(TPB * (b - 1), TPB), :]
                    last = dve.tensor_tensor(xb, shared[:, 0:SEQ].rearrange("p (i d) -> p i d", i=TPB), xb, ALU.add)
                    last.then_inc(drain_done, 1)

            def diagonal(kt):
                flat = VP[:, kt, :, :].rearrange("p h c -> p (h c)")
                return bass.AP(tensor=flat.tensor, offset=flat.offset, ap=[list(flat.ap[0]), [P + 8, HEADS], [1, 8]])

            def values_raw(b):
                if not known_below(b, 1):
                    dve.wait_ge(av_done, A.av + PAIRS * b)
                dve.wait_ge(nat_in, 16 * (A.nat + b + 1))
                for kt in range(TPB):
                    dve.tensor_copy(diagonal(kt), ctxN[:, kt, :].rearrange("p (h c) -> p h c", h=HEADS))\
                       .then_inc(vc_ready, 1)

            def maxima(b, t):
                g = PAIRS * b + t
                for qt in range(TPB):
                    keys = P if A.causal and qt == 0 else SEQ
                    s = bank[2 * (t % 2) + qt][:].rearrange("p (h k) -> p h k", h=2)
                    dve.wait_ge(scores_ready, A.scores + 2 * g + qt + 1)
                    if A.wide:
                        if A.kind == "rows":
                            mask = rowpen[:, bass.ds(TPB * b + qt, 1)].unsqueeze(2).broadcast_to([P, 2, SEQ])
                        else:
                            mask = keymask[:, bass.ds(b * SEQ, SEQ)].unsqueeze(1).broadcast_to([P, 2, SEQ])
                        dve.tensor_tensor(s, s, mask, ALU.add).then_inc(masked, 1)
                        dve.wait_ge(masked, A.rawmax - A.narrow + 2 * g + qt + 1)
                    dve.tensor_reduce(rawmax[:, t % 2, qt, :], s[:, :, 0:keys], AX, ALU.max).then_inc(rawmax_done, 1)
                    dve.wait_ge(rawmax_done, A.rawmax + 2 * g + qt + 1)
                    dve.tensor_scalar(negmax[:, t % 2, qt, :], rawmax[:, t % 2, qt, :], -A.scale, None,
                                      ALU.mult).then_inc(negmax_ready, 1)

            def copy_pt(b, t, qts=range(TPB)):
                g = PAIRS * b + t
                for qt in qts:
                    if not known_below(g, 2):
                        dve.wait_ge(av_done, A.av + g - 1)
                    dve.wait_ge(tp_done, A.tp + 2 * g + qt + 1)
                    kts = qt + 1 if A.causal else TPB
                    src = bank[4 + qt][:].rearrange("p (h kt q) -> p h kt q", h=2, kt=TPB)
                    dve.tensor_copy(PT[:, t % 2, :, 0:kts, qt * P:(qt + 1) * P], src[:, :, 0:kts, :])\
                       .then_inc(pt_ready, 1)

            def inverses(b, t, qts=range(TPB)):
                g = PAIRS * b + t
                for qt in qts:
                    dve.wait_ge(exp_done, A.exp + 2 * g + qt + 1)
                    dve.reciprocal(rinv[:, t % 2, qt, :], rowsum[:, t % 2, qt, :]).then_inc(rinv_ready, 1)

            def step(part, b, t):
                g = PAIRS * b + t
                more = part != "last"
                for qt in range(TPB):
                    if not known_below(g, 1):
                        inverses(b if t >= 1 else b - 1, (t - 1) % PAIRS, [qt])
                    if not known_below(g, 2):
                        copy_pt(b if t >= 2 else b - 1, (t - 2) % PAIRS, [qt])
                maxima(b, t)
                if t == 0 and more:
                    norm_stats(b + 1)
                if t == 4 - A.wide and more:
                    normalise(b + 1)
                if A.kind == "bias" and t == 2 and more:
                    take_context(b + 1)
                if A.kind == "raw" and t == 3 and more:
                    dve.wait_ge(km_ready, A.km + PAIRS * b + PAIRS)
                    take_context(b + 1)
                if t == PAIRS - 1 and more and not A.wide:
                    dve.wait_ge(drain_done, A.drained(part, b, "ln" if A.kind == "raw" else "q"))
                    dve.tensor_copy(QT[:, 0, :], qT_next).then_inc(qt_ready, 1)
                for use in A.bank_uses(part, t, "A"):
                    take(part, b, use)
                if t == 3 and more and A.wide:
                    dve.wait_ge(fill_done, A.fills(part, b, "qk7"))
                    take_context(b + 1)
                if t == 1 and A.kind == "raw":
                    values_raw(b)
                for use in A.bank_uses(part, t, "B"):
                    take(part, b, use)
                for use in A.bank_uses(part, t, "C"):
                    take(part, b, use)

            if not A.stages:
                dve.wait_ge(x_in, 16)
            if A.kind != "raw":
                n = {"rows": 5, "bias": 8, "keys": 4}[A.kind]
                dve.wait_ge(w_in[layer_of[A.kind]], 16 * n)
            dve.wait_ge(zeros_done, A.zeros)
            if A.kind == "rows":
                dve.wait_ge(rowmask_in, 16)
                dve.tensor_scalar(rowpen[:], rowmask[:], -1.0, PENALTY, ALU.add, ALU.mult).then_inc(rowpen_ready, 1)
                dve.wait_ge(rowpen_ready, 1)
            if A.kind == "keys":
                dve.wait_ge(keymask_in, 16)
            take_context(0)
            norm_stats(0)
            normalise(0)
            for use in A.uses["pre"]:
                take("pre", 0, use)
            if not A.wide:
                dve.wait_ge(drain_done, A.drained("pre", 0, "ln" if A.kind == "raw" else "q"))
                dve.tensor_copy(QT[:, 0, :], qT_next).then_inc(qt_ready, 1)
            for t in range(PAIRS):
                step("first", 0, t)
            with dve.Fori(1, BATCH - 1) as b:
                for t in range(PAIRS):
                    step("loop", b, t)
            for t in range(PAIRS):
                step("last", BATCH - 1, t)
            inverses(BATCH - 1, PAIRS - 1)
            copy_pt(BATCH - 1, PAIRS - 2)
            copy_pt(BATCH - 1, PAIRS - 1)
            for use in A.uses["epi"]:
                take("epi", BATCH, use)
            dve.wait_ge(drain_done, A.after["drain"])
            dve.nop().then_inc(stage_done, 1)

        @block.vector
        def _(dve):
            ffn.setup_vector(dve)
            for A in plan:
                if isinstance(A, Attention):
                    attention_vector(dve, A)
                else:
                    ffn.vector(dve, A)

        def rsqrt(pool, n, ln, rounds=range(NEWTON)):
            step = LN_CHAIN * ln
            if 0 in rounds:
                pool.wait_ge(seed_ready, ln + 1)
            y, a = rstd[:, 0:n], ntmp[:, 0:n]
            for k in rounds:
                if k:
                    pool.wait_ge(newton_step, step + 4 * k)
                pool.tensor_tensor(a, y, y, ALU.mult).then_inc(newton_step, 1)
                pool.wait_ge(newton_step, step + 4 * k + 1)
                pool.tensor_tensor(a, a, vhalf[:, 0:n], ALU.mult).then_inc(newton_step, 1)
                pool.wait_ge(newton_step, step + 4 * k + 2)
                pool.tensor_tensor(a, a, c15[:, 0:n], ALU.add).then_inc(newton_step, 1)
                pool.wait_ge(newton_step, step + 4 * k + 3)
                pool.tensor_tensor(y, y, a, ALU.mult).then_inc(newton_step, 1)

        def attention_pool(pool, A):
            def step(part, b, t):
                g = PAIRS * b + t
                for qt in range(TPB):
                    keys = P if A.causal and qt == 0 else SEQ
                    pool.wait_ge(rinv_ready, A.rinv + 2 * g + qt + 1)
                    p = PR[:, t % 2, qt, :, 0:keys]
                    pool.tensor_tensor(p, p, rinv[:, t % 2, qt, :].unsqueeze(2).broadcast_to([P, 2, keys]),
                                       ALU.mult).then_inc(probs_ready, 1)
                if t < NEWTON and part != "last":
                    rsqrt(pool, TPB, A.ln + b + 1, [t])

            if A.stages:
                pool.wait_ge(stage_done, A.stages)
            else:
                pool.memset(c15[:], 1.5).then_inc(zeros_done, 1)
                pool.wait_ge(zeros_done, 1)
                clear(pool, A)
            rsqrt(pool, TPB, A.ln)
            for t in range(PAIRS):
                step("first", 0, t)
            with pool.Fori(1, BATCH - 1) as b:
                for t in range(PAIRS):
                    step("loop", b, t)
            for t in range(PAIRS):
                step("last", BATCH - 1, t)

        def clear(pool, A):
            pool.memset(VP[:], 0.0).then_inc(zeros_done, 1)
            if A.wide:
                pool.memset(KM[:], 0.0).then_inc(zeros_done, 1)

        @block.gpsimd
        def _(pool):
            for A, following in zip(plan, plan[1:] + [None]):
                if isinstance(A, Attention):
                    attention_pool(pool, A)
                else:
                    ffn.pool(pool, A, rsqrt)
                    if following:
                        clear(pool, following)


class FeedForward:

    def __init__(self, kind, base):
        self.kind = kind
        take_counts(self, base)
        self.index = int(kind[3:])
        norms = 2 if kind == "ffn1" else 1
        self.after = dict(base, xn=base["xn"] + TILES, ln=base["ln"] + norms,
                          stat=base["stat"] + 2 * TILES + 3 + (GROUPS + 4 if norms == 2 else 0),
                          stages=base["stages"] + 1)


NE_USED = 1024
CHUNKS = NE_USED // P
PK_HEADS, NK, TOPK = 8, 32, 8
EXPERTS = 8
CAPACITY = 640


def feed_forward(nc, ctx, sb, sem, S, w):
    x, xn_all, xnT_all, ident, identB = (S[n] for n in ("x", "xn_all", "xnT_all", "ident", "identB"))
    bank, outT, QT, OT, both, KM, VP = (S[n] for n in ("bank", "outT", "QT", "OT", "both", "KM", "VP"))
    stats, mv, veps, vbits, rstd = (S[n] for n in ("stats", "mv", "veps", "vbits", "rstd"))
    onesB, w_in, const_in = S["onesB"], S["w_in"], S["const_in"]
    stat_step, seed_ready, newton_step, xn_ready = (S[n] for n in ("stat_step", "seed_ready", "newton_step", "xn_ready"))
    stage_done, setup_done = S["stage_done"], S["setup_done"]

    W1T, W2T = sb("W1T", [P, 512]), sb("W2T", [P, 512])
    b1c, b2c = sb("b1c", [P, 4]), sb("b2c", [P, 1])
    abssum = sb("abssum", [P, 2])
    onesF = sb("onesF", [P, P])
    half, neghalf = sb("half", [P, 2]), sb("neghalf", [P, 2])
    above, below = OT[:, 0:2, :].rearrange("p a b -> p (a b)"), OT[:, 2:4, :].rearrange("p a b -> p (a b)")
    absjunk = OT[:, 4:6, :].rearrange("p a b -> p (a b)")
    hidden = QT[:].rearrange("p a b -> p (a b)").rearrange("p (s n) -> p s n", s=4)
    WKQ, keysT = sb("WKQ", [P, 16, P]), sb("keysT", [P, 512])
    AK = QT[:, 0:2, :].rearrange("p a b -> p (a b)")
    downT, up = sb("downT", [P, NE_USED]), sb("up", [P, CHUNKS, D])
    gamma, beta = sb("gamma", [P, 1]), sb("beta", [P, 1])
    bnstats, bnmv = sb("bnstats", [P, GROUPS, 6]), sb("bnmv", [P, 2])
    bn_a, bn_c = sb("bn_a", [P, 1]), sb("bn_c", [P, 1])
    xbT = QT[:, 2, :].rearrange("p (a b) -> p a b", a=2)
    sims = OT[:].rearrange("p a b -> p (a b)").rearrange("p (g n) -> p g n", g=4)
    top = sb("top", [P, 2, 16, TOPK])
    combos = QT[:, 4:6, :].rearrange("p a b -> p (a b)")
    best = sb("best", [P, 2, PK_HEADS, TOPK])
    pairsum = KM[:].rearrange("p a b c -> p (a b c)").rearrange("p (r n) -> p r n", r=4)
    gated = VP[:].rearrange("p a b c -> p (a b c)").rearrange("p (r n) -> p r n", r=4)
    HG = both[:, 0:2048].rearrange("p (r c n) -> p r c n", r=2, c=CHUNKS)
    F1, F2 = sb("F1", [P, EXPERTS, 256]), sb("F2", [P, 16, D])
    f1b = sb("f1b", [P, 16])
    b2pad = sb("b2pad", [P, D])
    b2parts = sb("b2parts", [P, 3, D], BF16)
    wredT, wg = sb("wredT", [16, P]), sb("wg", [8, 16])
    wgn, wgnT = sb("wgn", [8, 16]), sb("wgnT", [16, 8])
    wsq, wnorm = sb("wsq", [8, 16]), sb("wnorm", [8, 4])
    gateW = sb("gateW", [P, 2, EXPERTS])
    WG, WU, WD = (sb(n, [P, EXPERTS, P]) for n in ("WG", "WU", "WD"))
    SG, SU, SD = (sb(n, [P, 2, P]) for n in ("SG", "SU", "SD"))
    sel = sb("sel", [P, EXPERTS, P], BF16)
    iota8 = sb("iota8", [P, EXPERTS])
    before = sb("before", [P, P], BF16)
    lgT = OT[0:8].rearrange("p a b -> p (a b)")
    gt = {n: sb("g_" + n, [P, TILES, EXPERTS]) for n in ("lg", "m8", "e8", "idxf", "oh1", "oh2", "comb", "t1", "pre", "r")}
    idx8 = sb("idx8", [P, TILES, EXPERTS], U32)
    gs = {n: sb("gs_" + n, [P, TILES]) for n in ("z", "zi", "p1", "p2", "den", "di", "w1", "w2")}
    picks = sb("picks", [P, TILES, EXPERTS], BF16)
    parts = QT[:].rearrange("p a b -> p (a b)").bitcast(BF16)[:, 0:TILES * P].rearrange("p (t c) -> p t c", t=TILES)
    gT = sb("gT", [P, TOKENS], BF16)
    ring = KM[:].rearrange("p a b c -> p (a b c)")
    act_ring = ring[:, 0:2048].rearrange("p (r n) -> p r n", r=4)
    gated_ring = ring[:, 2048:4096].rearrange("p (r n) -> p r n", r=4)
    shared_u = VP[:].rearrange("p a b c -> p (a b c)")[:, 0:2048].rearrange("p (r n) -> p r n", r=4)

    abs_ready, abs_sum, scale_ready = sem("abs_ready"), sem("abs_sum"), sem("scale_ready")
    tern_step = sem("tern_step")
    lnT_done, xnT_ready = sem("lnT_done"), sem("xnT_ready")
    up_done = [sem(f"up_done{i}") for i in range(4)]
    act_ready = [sem(f"act_ready{i}") for i in range(4)]
    out_ready = [sem(f"out_ready{i}") for i in range(4)]
    outT_ready = [sem(f"outT_ready{i}") for i in range(4)]
    back_done = [sem(f"back_done{i}") for i in range(4)]
    added = [sem(f"added{i}") for i in range(4)]
    ak_done, ak_ready = sem("ak_done"), sem("ak_ready")
    bn_step, bn_ready = sem("bn_step"), sem("bn_ready")
    xb_ready, sim_done, sims_ready = sem("xb_ready"), sem("sim_done"), sem("sims_ready")
    top_done, combos_done, best_done = sem("top_done"), sem("combos_done"), sem("best_done")
    sum_ready = sem("sum_ready")
    sig_ready, gated_ready, wT_done = sem("sig_ready"), sem("gated_ready"), sem("wT_done")
    mixed = sem("mixed")
    gate_w_step = sem("gate_w_step")
    lg_done, lg_ready = [sem("lg_done2"), sem("lg_done3")], [sem("lg_ready2"), sem("lg_ready3")]
    gate_step = sem("gate_step")
    gexp_go, gexp_done = sem("gexp_go"), sem("gexp_done")
    count_done = sem("count_done")
    parts_ready, gT_done, gT_ready = sem("parts_ready"), sem("gT_done"), sem("gT_ready")
    b2_step = sem("b2_step")
    bc_done = [sem("bc_done2"), sem("bc_done3")]
    prod_step = sem("prod_step")
    gated_done = [sem("gated_done2"), sem("gated_done3")]
    down_done = [sem("down_done2"), sem("down_done3")]

    class Layers:
        pass

    F = Layers()
    F.lnT_done = lnT_done
    lists = {
        "ffn0": ((W1T, "W1T"), (W2T, "W2T"), (b1c, "b1c"), (b2c, "b2c")),
        "ffn1": ((WKQ, "WKQ"), (keysT, "keysT"), (downT, "downT"), (up, "up"), (gamma, "gamma"), (beta, "beta")),
        "ffn2": ((F1, "F1"), (F2, "F2"), (f1b, "f1b"), (b2pad, "b2pad"), (wredT, "wredT"), (wg, "wg"),
                 (sel, "sel"), (iota8, "iota8")),
        "ffn3": ((gateW[:, 1, :], "gateW3"), (WG, "WG"), (WU, "WU"), (WD, "WD"), (SG, "SG"), (SU, "SU"), (SD, "SD"),
                 (before, "before")),
    }
    layer_no = {"ffn0": 1, "ffn1": 3, "ffn2": 5, "ffn3": 7}

    def loads(sp, kind):
        for dst, name in lists[kind]:
            sp.dma_start(dst if name == "gateW3" else dst[:], w[name]).then_inc(w_in[layer_no[kind]], 16)

    def weights_in(eng, A):
        eng.wait_ge(w_in[layer_no[A.kind]], 16 * len(lists[A.kind]))

    def norm_vector(dve, A, between=None):
        for i in range(TILES):
            dve.bn_stats(stats[:, i, :], x[:, i, :]).then_inc(stat_step, 1)
        dve.wait_ge(stat_step, A.stat + TILES)
        for i in range(TILES):
            dve.bn_aggr(mv[:, i, :], stats[:, i, :]).then_inc(stat_step, 1)
        dve.wait_ge(stat_step, A.stat + 2 * TILES)
        S["seed"](dve, mv[:, :, 1], TILES, A.stat + 2 * TILES)
        if between:
            between()
        dve.wait_ge(newton_step, LN_CHAIN * (A.ln + 1))
        for i in range(TILES):
            dve.tensor_scalar(xn_all[:, i, :], x[:, i, :], mv[:, i, 0:1], rstd[:, i:i + 1],
                              ALU.subtract, ALU.mult).then_inc(xn_ready, 1)

    def norm_tensor(pe, A):
        for g in range(GROUPS):
            pe.wait_ge(xn_ready, A.xn + TPG * (g + 1))
            for i in range(TPG):
                last = pe.transpose(bank[g][:, i * P:(i + 1) * P], xn_all[:, TPG * g + i, :], ident[:])
            last.then_inc(lnT_done, 1)

    def norm_scalar(act, A):
        for g in range(GROUPS):
            act.wait_ge(lnT_done, GROUPS * A.index + g + 1)
            act.activation(xnT_all[:, g * GROUP:(g + 1) * GROUP], bank[g][:], ACT.Copy).then_inc(xnT_ready, 1)

    def back_tensor(pe, A, g, home):
        pe.wait_ge(outT_ready[A.index], g + 1)
        if not known_zero(g):
            pe.wait_ge(added[A.index], g)
        for i in range(TPG):
            last = pe.transpose(home[:, i * P:(i + 1) * P], outT[:, i * P:(i + 1) * P], ident[:])
        last.then_inc(back_done[A.index], 1)

    def out_scalar(act, A, g, home, bias=None):
        act.wait_ge(out_ready[A.index], g + 1)
        if bias is None:
            act.activation(outT[:], home[:], ACT.Copy).then_inc(outT_ready[A.index], 1)
        else:
            act.activation(outT[:], home[:], ACT.Identity, bias=bias).then_inc(outT_ready[A.index], 1)

    def add_vector(dve, A, g, home):
        dve.wait_ge(back_done[A.index], g + 1)
        xg = x[:, bass.ds(TPG * g, TPG), :]
        dve.tensor_tensor(xg, home[:].rearrange("p (i d) -> p i d", i=TPG), xg, ALU.add).then_inc(added[A.index], 1)

    def known_zero(g):
        return isinstance(g, int) and g == 0

    def groups(eng, body):
        body(0)
        with eng.Fori(1, GROUPS) as g:
            body(g)

    def tensor0(pe, A):
        pe.wait_ge(setup_done, 2)
        pe.wait_ge(abs_ready, 2)
        pe.matmul(bank[6][:, 0:2], onesF[:], abssum[:], start=True, stop=True).then_inc(abs_sum, 1)
        norm_tensor(pe, A)
        pe.wait_ge(tern_step, 10)

        def body(g):
            if known_zero(g):
                pe.wait_ge(xnT_ready, GROUPS * A.index + GROUPS)
            for s in range(4):
                if not known_zero(g):
                    pe.wait_ge(act_ready[0], 4 * g - 4 + s + 1)
                pe.matmul(bank[s][:], W1T[:, s * P:(s + 1) * P], xnT_all[:, bass.ts(g, GROUP)],
                          start=True, stop=True).then_inc(up_done[0], 1)
            if not known_zero(g):
                pe.wait_ge(outT_ready[0], g)
            for s in range(4):
                pe.wait_ge(act_ready[0], 4 * g + s + 1)
                last = pe.matmul(bank[4][:], W2T[:, s * P:(s + 1) * P], hidden[:, s, :], start=(s == 0), stop=(s == 3))
            last.then_inc(out_ready[0], 1)
            back_tensor(pe, A, g, bank[5])

        groups(pe, body)

    def scalar0(act, A):
        weights_in(act, A)
        act.activation(absjunk, W1T[:], ACT.Abs, accum_out=abssum[:, 0:1]).then_inc(abs_ready, 1)
        act.wait_ge(abs_ready, 1)
        act.activation(absjunk, W2T[:], ACT.Abs, accum_out=abssum[:, 1:2]).then_inc(abs_ready, 1)
        norm_scalar(act, A)

        def body(g):
            for s in range(4):
                act.wait_ge(up_done[0], 4 * g + s + 1)
                if not known_zero(g):
                    act.wait_ge(out_ready[0], g)
                act.activation(hidden[:, s, :], bank[s][:], ACT.Gelu, bias=b1c[:, s:s + 1]).then_inc(act_ready[0], 1)
            if not known_zero(g):
                act.wait_ge(back_done[0], g)
            out_scalar(act, A, g, bank[4], b2c[:])

        groups(act, body)

    def vector0(dve, A):
        def ternary():
            dve.wait_ge(abs_sum, 1)
            dve.tensor_scalar(half[:], bank[6][:, 0:2], 1.0 / (512 * D), 1e-8, ALU.mult, ALU.max)\
               .then_inc(scale_ready, 1)
            dve.wait_ge(scale_ready, 1)
            dve.tensor_scalar(neghalf[:], half[:], -0.5, None, ALU.mult).then_inc(scale_ready, 1)
            dve.wait_ge(scale_ready, 2)
            dve.tensor_scalar(half[:], half[:], 0.5, None, ALU.mult).then_inc(scale_ready, 1)
            dve.wait_ge(scale_ready, 3)
            for n, wt in enumerate((W1T, W2T)):
                dve.tensor_scalar(above, wt[:], half[:, n:n + 1], None, ALU.is_gt).then_inc(tern_step, 1)
                dve.tensor_scalar(below, wt[:], neghalf[:, n:n + 1], None, ALU.is_lt).then_inc(tern_step, 1)
                dve.wait_ge(tern_step, 5 * n + 2)
                dve.tensor_tensor(above, above, below, ALU.subtract).then_inc(tern_step, 1)
                dve.wait_ge(tern_step, 5 * n + 3)
                dve.tensor_tensor(below, above, wt[:], ALU.subtract).then_inc(tern_step, 1)
                dve.wait_ge(tern_step, 5 * n + 4)
                dve.tensor_tensor(wt[:], wt[:], below, ALU.add).then_inc(tern_step, 1)
                dve.wait_ge(tern_step, 5 * n + 5)

        norm_vector(dve, A, ternary)
        groups(dve, lambda g: add_vector(dve, A, g, bank[5]))

    def steps1(eng, step):
        far = TILES
        for t in range(TPG):
            step(t, far, t, t)
        with eng.Fori(1, GROUPS - 1) as g:
            for t in range(TPG):
                step(far, far, TPG * g + t, t)
        for t in range(TPG):
            step(far, TPG - 1 - t, TILES - TPG + t, t)

    def weight_bank(t, c):
        return bank[(2, 6)[t % 2] + c // 4][:, (c % 4) * P:(c % 4 + 1) * P]

    def tensor1(pe, A):
        weights_in(pe, A)
        for p in range(2):
            for h in range(PK_HEADS):
                c = (2 * h + p) * NK
                last = pe.matmul(bank[4][:, c:c + NK], WKQ[:, p * PK_HEADS + h, :], keysT[:, c:c + NK],
                                 start=True, stop=True)
        last.then_inc(ak_done, 1)
        norm_tensor(pe, A)
        pe.wait_ge(ak_ready, 1)

        def similar(first, i, t):
            pe.wait_ge(xb_ready, i + 1)
            if first > 0:
                pe.wait_ge(sims_ready, i)
            pe.matmul(bank[0][:], xbT[:, t % 2, :], AK, start=True, stop=True).then_inc(sim_done, 1)

        def lower(first, i):
            for half_ in range(2):
                if first > 0:
                    pe.wait_ge(act_ready[1], 2 * i + half_ - 1)
                for c in range(4):
                    last = pe.matmul(bank[4 + half_][:, c * P:(c + 1) * P],
                                     downT[:, (4 * half_ + c) * P:(4 * half_ + c + 1) * P],
                                     xnT_all[:, bass.ds(i * P, P)], start=True, stop=True)
                last.then_inc(up_done[1], 1)

        def upper(first, i, t):
            pe.wait_ge(mixed, 2 * i + 2)
            if first > 0:
                pe.wait_ge(added[1], i)
            for c in range(CHUNKS):
                last = pe.matmul(bank[1][:, 0:D], HG[:, t % 2, c, :], up[:, c, :],
                                 start=(c == 0), stop=(c == CHUNKS - 1))
            last.then_inc(back_done[1], 1)

        def step(first, last_, i, t):
            if first > 0:
                upper(first - 1, i - 1, t - 1)
            for h in range(PK_HEADS):
                pe.wait_ge(gated_ready, PK_HEADS * i + h + 1)
                if h == 0 and first > 1:
                    pe.wait_ge(mixed, 2 * i - 2)
                for c in range(CHUNKS):
                    last = pe.matmul(weight_bank(t, c), gated[:, h % 4, c * P:(c + 1) * P], ident[:],
                                     is_transpose=True, start=(h == 0 and c % 4 == 0),
                                     stop=(h == PK_HEADS - 1 and c % 4 == 3), skip_group_check=True)
                last.then_inc(wT_done, 1)
                if h == 1 and last_ > 1:
                    similar(first + 2, i + 2, t)
                if h == 3 and last_ > 0:
                    lower(first + 1, i + 1)

        similar(0, 0, 0)
        lower(0, 0)
        similar(1, 1, 1)
        steps1(pe, step)
        upper(TILES, TILES - 1, TPG - 1)

    def scalar1(act, A):
        weights_in(act, A)
        act.wait_ge(ak_done, 1)
        act.activation(AK, bank[4][:], ACT.Copy).then_inc(ak_ready, 1)
        norm_scalar(act, A)
        act.wait_ge(bn_ready, 1)

        def inputs(first, i, t):
            if first > 1:
                act.wait_ge(sim_done, i - 1)
            act.activation(xbT[:, t % 2, :], xnT_all[:, bass.ds(i * P, P)], ACT.Identity, bias=bn_c[:], scale=bn_a[:])\
               .then_inc(xb_ready, 1)

        def copy_sims(first, i, t):
            act.wait_ge(sim_done, i + 1)
            if first > 3:
                act.wait_ge(top_done, 16 * (i - 3))
                act.wait_ge(gated_ready, PK_HEADS * (i - 3))
            act.activation(sims[:, t % 4, :], bank[0][:], ACT.Copy).then_inc(sims_ready, 1)

        def step(first, last_, i, t):
            if last_ > 1:
                inputs(first + 2, i + 2, t)
            if last_ > 0:
                copy_sims(first + 1, i + 1, t + 1)
            for half_ in range(2):
                act.wait_ge(up_done[1], 2 * i + half_ + 1)
                if half_ == 0 and first > 1:
                    act.wait_ge(back_done[1], i - 1)
                act.activation(HG[:, t % 2, 4 * half_:4 * half_ + 4, :],
                               bank[4 + half_][:].rearrange("p (c n) -> p c n", c=4), ACT.Gelu).then_inc(act_ready[1], 1)
            for h in range(PK_HEADS):
                n = PK_HEADS * i + h
                act.wait_ge(sum_ready, n + 1)
                if first > 0 or h >= 4:
                    act.wait_ge(wT_done, n - 3)
                act.activation(gated[:, h % 4, :], pairsum[:, h % 4, :], ACT.Sigmoid).then_inc(sig_ready, 1)

        inputs(0, 0, 0)
        inputs(1, 1, 1)
        copy_sims(0, 0, 0)
        steps1(act, step)

    def pool1(pool, A):
        def step(first, last_, i, t):
            pool.wait_ge(sims_ready, i + 1)
            s = sims[:, t % 4, :].rearrange("p (h q k) -> p h q k", h=PK_HEADS, q=2)
            for h in range(PK_HEADS):
                if first > 0 or h >= 4:
                    pool.wait_ge(gated_ready, PK_HEADS * i + h - 3)
                dst = pairsum[:, h % 4, :].rearrange("p (i j) -> p i j", i=NK)
                pool.tensor_tensor(dst, s[:, h, 0, :].unsqueeze(2).broadcast_to([P, NK, NK]),
                                   s[:, h, 1, :].unsqueeze(1).broadcast_to([P, NK, NK]), ALU.add)\
                    .then_inc(sum_ready, 1)

        steps1(pool, step)

    def vector1(dve, A):
        norm_vector(dve, A)
        dve.wait_ge(xnT_ready, GROUPS * A.index + GROUPS)
        for g in range(GROUPS):
            dve.bn_stats(bnstats[:, g, :], xnT_all[:, g * GROUP:(g + 1) * GROUP]).then_inc(stat_step, 1)
        at = A.stat + 2 * TILES + 3
        dve.wait_ge(stat_step, at + GROUPS)
        dve.bn_aggr(bnmv[:], bnstats[:].rearrange("p g s -> p (g s)")).then_inc(stat_step, 1)
        dve.wait_ge(stat_step, at + GROUPS + 1)
        S["seed"](dve, bnmv[:, 1:2], 1, at + GROUPS + 1)
        dve.wait_ge(newton_step, LN_CHAIN * (A.ln + 2))
        weights_in(dve, A)
        dve.tensor_tensor(bn_a[:], rstd[:, 0:1], gamma[:], ALU.mult).then_inc(bn_step, 1)
        dve.wait_ge(bn_step, 1)
        dve.tensor_tensor(bn_c[:], bnmv[:, 0:1], bn_a[:], ALU.mult).then_inc(bn_step, 1)
        dve.wait_ge(bn_step, 2)
        dve.tensor_tensor(bn_c[:], beta[:], bn_c[:], ALU.subtract).then_inc(bn_ready, 1)

        def choose(i, t):
            dve.wait_ge(sims_ready, i + 1)
            S["own_wait"](dve)
            for n in range(16):
                last = dve.max(top[:, t % 2, n, :], sims[:, t % 4, n * NK:(n + 1) * NK])
                last.then_inc(top_done, 1)
            dve.wait_ge(top_done, 16 * i + 16)
            pair = top[:, t % 2].rearrange("p (h q) k -> p h q k", q=2)
            dve.tensor_tensor(combos.rearrange("p (h a b) -> p h a b", h=PK_HEADS, a=TOPK),
                              pair[:, :, 0, :].unsqueeze(3).broadcast_to([P, PK_HEADS, TOPK, TOPK]),
                              pair[:, :, 1, :].unsqueeze(2).broadcast_to([P, PK_HEADS, TOPK, TOPK]), ALU.add)\
               .then_inc(combos_done, 1)
            dve.wait_ge(combos_done, i + 1)
            S["own_wait"](dve, 1)
            for h in range(PK_HEADS):
                dve.max(best[:, t % 2, h, :], combos[:, h * 64:(h + 1) * 64]).then_inc(best_done, 1)

        def mix(i, t):
            dve.wait_ge(wT_done, PK_HEADS * i + PK_HEADS)
            dve.wait_ge(act_ready[1], 2 * i + 2)
            for half_ in range(2):
                hg = HG[:, t % 2, 4 * half_:4 * half_ + 4, :]
                wt = bank[(2, 6)[t % 2] + half_][:].rearrange("p (c n) -> p c n", c=4)
                dve.tensor_tensor(hg, wt, hg, ALU.mult).then_inc(mixed, 1)

        def add_tile(i):
            dve.wait_ge(back_done[1], i + 1)
            xi = x[:, bass.ds(i, 1), :].rearrange("p a d -> p (a d)")
            dve.tensor_tensor(xi, bank[1][:, 0:D], xi, ALU.add).then_inc(added[1], 1)

        def step(first, last_, i, t):
            if last_ > 0:
                choose(i + 1, t + 1)
            if first > 0:
                mix(i - 1, t - 1)
            dve.wait_ge(best_done, PK_HEADS * i + PK_HEADS)
            for h in range(PK_HEADS):
                dve.wait_ge(sig_ready, PK_HEADS * i + h + 1)
                dve.scalar_tensor_tensor(out=gated[:, h % 4, :], in0=pairsum[:, h % 4, :],
                                         scalar=best[:, t % 2, h, TOPK - 1:TOPK], in1=gated[:, h % 4, :],
                                         op0=ALU.is_ge, op1=ALU.mult).then_inc(gated_ready, 1)
                if h == 3 and first > 0:
                    add_tile(i - 1)

        choose(0, 0)
        steps1(dve, step)
        mix(TILES - 1, TPG - 1)
        add_tile(TILES - 1)

    def gate_tensor(pe, A):
        k = A.index - 2
        for g in range(GROUPS):
            if g == 0:
                pe.wait_ge(xnT_ready, GROUPS * A.index + GROUPS)
            if g >= 2:
                pe.wait_ge(lg_ready[k], g - 1)
            pe.matmul(bank[g % 2][0:8, :], gateW[:, k, :], xnT_all[:, g * GROUP:(g + 1) * GROUP],
                      start=True, stop=True).then_inc(lg_done[k], 1)
        pe.wait_ge(lg_ready[k], GROUPS)
        for i in range(TILES):
            last = pe.transpose(bank[2][:, i * 8:(i + 1) * 8], lgT[:, i * P:(i + 1) * P], ident[0:8, 0:8])
        last.then_inc(lg_done[k], 1)
        if k == 1:
            pe.wait_ge(count_done, 1)
            flat = picks[:].rearrange("p t e -> p (t e)")
            pe.matmul(bank[3][:, 0:P], before[:], flat, start=True, stop=True)
            pe.matmul(bank[3][:, P:2 * P], onesB[:], flat, start=True, stop=True).then_inc(count_done, 1)
        pe.wait_ge(parts_ready, k + 1)
        for i in range(TILES):
            home = bank[4 + i // 8][:].bitcast(BF16)
            last = pe.transpose(home[:, (i % 8) * P:(i % 8 + 1) * P], parts[:, i, :], identB[:])
            if i % 8 == 7:
                last.then_inc(gT_done, 1)
        pe.wait_ge(gT_ready, 2 * k + 2)

    def gate_scalar(act, A):
        k = A.index - 2
        for g in range(GROUPS):
            act.wait_ge(lg_done[k], g + 1)
            act.activation(lgT[:, g * GROUP:(g + 1) * GROUP], bank[g % 2][0:8, :], ACT.Copy).then_inc(lg_ready[k], 1)
        act.wait_ge(gexp_go, k + 1)
        act.activation(gt["e8"][:], gt["t1"][:], ACT.Exp).then_inc(gexp_done, 1)
        for half_ in range(2):
            act.wait_ge(gT_done, 2 * k + half_ + 1)
            act.activation(gT[:, half_ * 1024:(half_ + 1) * 1024], bank[4 + half_][:].bitcast(BF16), ACT.Copy)\
               .then_inc(gT_ready, 1)

    def gate_vector(dve, A):
        k = A.index - 2
        n = [gate_total[k]]

        def link(ins):
            n[0] += 1
            ins.then_inc(gate_step, 1)
            dve.wait_ge(gate_step, n[0])

        def wide(a):
            return a.unsqueeze(2).broadcast_to([P, TILES, EXPERTS])

        lg, m8, e8, oh1, oh2, comb, t1 = (gt[q] for q in ("lg", "m8", "e8", "oh1", "oh2", "comb", "t1"))
        link(dve.memset(parts, 0.0))
        dve.wait_ge(lg_done[k], GROUPS + 1)
        link(dve.tensor_copy(lg[:].rearrange("p t e -> p (t e)"), bank[2][:, 0:TILES * EXPERTS]))
        for i in range(TILES):
            ins = dve.max(m8[:, i, :], lg[:, i, :])
            n[0] += 1
            ins.then_inc(gate_step, 1)
        dve.wait_ge(gate_step, n[0])
        for i in range(TILES):
            ins = dve.max_index(idx8[:, i, :], m8[:, i, :], lg[:, i, :])
            n[0] += 1
            ins.then_inc(gate_step, 1)
        dve.tensor_tensor(t1[:], m8[:], wide(m8[:, :, 0]), ALU.subtract).then_inc(gexp_go, 1)
        dve.wait_ge(gate_step, n[0])
        link(dve.tensor_copy(gt["idxf"][:], idx8[:]))
        iota = iota8[:].unsqueeze(1).broadcast_to([P, TILES, EXPERTS])
        link(dve.tensor_tensor(oh1[:], wide(gt["idxf"][:, :, 0]), iota, ALU.is_equal))
        if k == 1:
            link(dve.tensor_tensor(oh2[:], wide(gt["idxf"][:, :, 1]), iota, ALU.is_equal))
            dve.tensor_tensor(picks[:], oh1[:], oh2[:], ALU.add).then_inc(count_done, 1)
        dve.wait_ge(gexp_done, k + 1)
        link(dve.tensor_reduce(gs["z"][:], e8[:], AX, ALU.add))
        link(dve.reciprocal(gs["zi"][:], gs["z"][:]))
        if k == 0:
            link(dve.tensor_tensor(comb[:], oh1[:], wide(gs["zi"][:]), ALU.mult))
        else:
            link(dve.tensor_tensor(gs["p1"][:], e8[:, :, 0], gs["zi"][:], ALU.mult))
            link(dve.tensor_tensor(gs["p2"][:], e8[:, :, 1], gs["zi"][:], ALU.mult))
            link(dve.tensor_tensor(gs["den"][:], gs["p1"][:], gs["p2"][:], ALU.add))
            link(dve.tensor_scalar(gs["den"][:], gs["den"][:], 1e-20, None, ALU.add))
            link(dve.reciprocal(gs["di"][:], gs["den"][:]))
            link(dve.tensor_tensor(gs["w1"][:], gs["p1"][:], gs["di"][:], ALU.mult))
            link(dve.tensor_tensor(gs["w2"][:], gs["p2"][:], gs["di"][:], ALU.mult))
            link(dve.tensor_tensor(oh1[:], oh1[:], wide(gs["w1"][:]), ALU.mult))
            link(dve.tensor_tensor(oh2[:], oh2[:], wide(gs["w2"][:]), ALU.mult))
            link(dve.tensor_tensor(comb[:], oh1[:], oh2[:], ALU.add))
            dve.wait_ge(count_done, 2)
            pre = gt["pre"]
            totals = bank[3][:, P:2 * P].rearrange("p (t e) -> p t e", t=TILES)
            link(dve.memset(pre[:, 0, :], 0.0))
            for i in range(1, TILES):
                link(dve.tensor_tensor(pre[:, i, :], totals[:, i - 1, :], pre[:, i - 1, :], ALU.add))
            link(dve.tensor_tensor(pre[:], bank[3][:, 0:P].rearrange("p (t e) -> p t e", t=TILES), pre[:], ALU.add))
            link(dve.tensor_scalar(pre[:], pre[:], float(CAPACITY), None, ALU.is_lt))
            link(dve.tensor_tensor(comb[:], comb[:], pre[:], ALU.mult))
        r = gt["r"]
        link(dve.tensor_copy(parts[:, :, 0:8], comb[:]))
        link(dve.tensor_tensor(r[:], comb[:], parts[:, :, 0:8], ALU.subtract))
        link(dve.tensor_copy(parts[:, :, 32:40], r[:]))
        link(dve.tensor_tensor(r[:], r[:], parts[:, :, 32:40], ALU.subtract))
        dve.tensor_copy(parts[:, :, 64:72], r[:]).then_inc(parts_ready, 1)
        gate_total[k + 1] = n[0]

    gate_total = {0: 0}

    def tensor2(pe, A):
        weights_in(pe, A)
        pe.wait_ge(gate_w_step, 7)
        pe.transpose(bank[4][0:16, 0:8], wgn[:], ident[0:8, 0:8]).then_inc(gate_w_step, 1)
        pe.wait_ge(gate_w_step, 9)
        pe.matmul(bank[5][:, 0:8], wredT[:], wgnT[:], start=True, stop=True).then_inc(gate_w_step, 1)
        norm_tensor(pe, A)
        pe.wait_ge(gate_w_step, 11)
        gate_tensor(pe, A)
        pe.wait_ge(b2_step, 6)

        def down(g, n):
            pe.wait_ge(gated_done[0], 16 * g + n + 1)
            pe.matmul(bank[6][:], F2[:, n, :], gated_ring[:, n % 4, :], start=False, stop=(n == 15))\
              .then_inc(down_done[0], 1)

        def body(g):
            if not known_zero(g):
                pe.wait_ge(outT_ready[2], g)
            for q in range(3):
                pe.matmul(bank[6][:], b2parts[:, q, :], gT[:, bass.ts(g, GROUP)], start=(q == 0), stop=False)
            for n in range(16):
                if n % 2 == 0:
                    if not (known_zero(g) and n < 4):
                        pe.wait_ge(gated_done[0], 16 * g + n - 2)
                    pe.matmul(bank[4 + n // 2 % 2][:], sel[:, n // 2, :], gT[:, bass.ts(g, GROUP)],
                              start=True, stop=True).then_inc(bc_done[0], 1)
                if not (known_zero(g) and n < 4):
                    pe.wait_ge(act_ready[2], 16 * g + n - 3)
                pe.matmul(bank[n % 4][:], F1[:, n // 2, (n % 2) * P:(n % 2 + 1) * P], xnT_all[:, bass.ts(g, GROUP)],
                          start=True, stop=True).then_inc(up_done[2], 1)
                if n >= 3:
                    down(g, n - 3)
            for n in range(13, 16):
                down(g, n)
            back_tensor(pe, A, g, bank[7])

        groups(pe, body)

    def scalar2(act, A):
        weights_in(act, A)
        act.wait_ge(gate_w_step, 2)
        act.activation(wnorm[:, 1:2], wnorm[:, 0:1], ACT.Sqrt).then_inc(gate_w_step, 1)
        norm_scalar(act, A)
        gate_scalar(act, A)

        def body(g):
            for n in range(16):
                act.wait_ge(up_done[2], 16 * g + n + 1)
                if not (known_zero(g) and n < 4):
                    act.wait_ge(gated_done[0], 16 * g + n - 3)
                act.activation(act_ring[:, n % 4, :], bank[n % 4][:], ACT.Gelu, bias=f1b[:, n:n + 1])\
                   .then_inc(act_ready[2], 1)
            act.wait_ge(down_done[0], 16 * g + 16)
            if not known_zero(g):
                act.wait_ge(back_done[2], g)
            act.activation(outT[:], bank[6][:], ACT.Copy).then_inc(outT_ready[2], 1)

        groups(act, body)

    def vector2(dve, A):
        weights_in(dve, A)
        dve.tensor_tensor(wsq[:], wg[:], wg[:], ALU.mult).then_inc(gate_w_step, 1)
        dve.wait_ge(gate_w_step, 1)
        dve.tensor_reduce(wnorm[:, 0:1], wsq[:], AX, ALU.add).then_inc(gate_w_step, 1)
        dve.wait_ge(gate_w_step, 3)
        dve.tensor_scalar(wnorm[:, 2:3], wnorm[:, 1:2], 1e-4, None, ALU.max).then_inc(gate_w_step, 1)
        dve.wait_ge(gate_w_step, 4)
        dve.reciprocal(wnorm[:, 3:4], wnorm[:, 2:3]).then_inc(gate_w_step, 1)
        dve.wait_ge(gate_w_step, 5)
        dve.tensor_scalar(wgn[:], wg[:], wnorm[:, 3:4], None, ALU.mult).then_inc(gate_w_step, 2)
        dve.wait_ge(gate_w_step, 8)
        dve.tensor_copy(wgnT[:], bank[4][0:16, 0:8]).then_inc(gate_w_step, 1)
        dve.tensor_copy(b2parts[:, 0, :], b2pad[:]).then_inc(b2_step, 1)
        dve.wait_ge(b2_step, 1)
        dve.tensor_tensor(b2pad[:], b2pad[:], b2parts[:, 0, :], ALU.subtract).then_inc(b2_step, 1)
        dve.wait_ge(b2_step, 2)
        dve.tensor_copy(b2parts[:, 1, :], b2pad[:]).then_inc(b2_step, 1)
        dve.wait_ge(b2_step, 3)
        dve.tensor_tensor(b2pad[:], b2pad[:], b2parts[:, 1, :], ALU.subtract).then_inc(b2_step, 1)
        dve.wait_ge(b2_step, 4)
        dve.tensor_copy(b2parts[:, 2, :], b2pad[:]).then_inc(b2_step, 2)
        dve.wait_ge(gate_w_step, 10)
        dve.tensor_copy(gateW[:, 0, :], bank[5][:, 0:8]).then_inc(gate_w_step, 1)
        norm_vector(dve, A)
        gate_vector(dve, A)

        def body(g):
            for n in range(16):
                dve.wait_ge(act_ready[2], 16 * g + n + 1)
                if n % 2 == 0:
                    dve.wait_ge(bc_done[0], 8 * g + n // 2 + 1)
                if not (known_zero(g) and n < 4):
                    dve.wait_ge(down_done[0], 16 * g + n - 3)
                dve.tensor_tensor(gated_ring[:, n % 4, :], bank[4 + n // 2 % 2][:], act_ring[:, n % 4, :],
                                  ALU.mult).then_inc(gated_done[0], 1)
            add_vector(dve, A, g, bank[7])

        groups(dve, body)

    UNITS = EXPERTS + 2

    def unit_weights(n):
        if n < EXPERTS:
            return WG[:, n, :], WU[:, n, :], WD[:, n, :]
        return SG[:, n - EXPERTS, :], SU[:, n - EXPERTS, :], SD[:, n - EXPERTS, :]

    def tensor3(pe, A):
        weights_in(pe, A)
        norm_tensor(pe, A)
        gate_tensor(pe, A)

        def down(g, n):
            pe.wait_ge(gated_done[1], UNITS * g + n + 1)
            pe.matmul(bank[6][:], unit_weights(n)[2], gated_ring[:, n % 4, :], start=(n == 0), stop=(n == UNITS - 1))\
              .then_inc(down_done[1], 1)

        def body(g):
            for n in range(UNITS):
                wgate, wup, _ = unit_weights(n)
                if n < EXPERTS:
                    if not (known_zero(g) and n < 2):
                        pe.wait_ge(gated_done[1], UNITS * g + (n - 1 if n >= 2 else n - 3))
                    pe.matmul(bank[4 + n % 2][:], sel[:, n, :], gT[:, bass.ts(g, GROUP)],
                              start=True, stop=True).then_inc(bc_done[1], 1)
                if not (known_zero(g) and n < 2):
                    pe.wait_ge(prod_step, UNITS * g + n - 1)
                pe.matmul(bank[2 * (n % 2)][:], wgate, xnT_all[:, bass.ts(g, GROUP)], start=True, stop=True)
                pe.matmul(bank[2 * (n % 2) + 1][:], wup, xnT_all[:, bass.ts(g, GROUP)],
                          start=True, stop=True).then_inc(up_done[3], 1)
                if n == 1 and not known_zero(g):
                    pe.wait_ge(outT_ready[3], g)
                if n >= 1:
                    down(g, n - 1)
            down(g, UNITS - 1)
            back_tensor(pe, A, g, bank[7])

        groups(pe, body)

    def scalar3(act, A):
        weights_in(act, A)
        norm_scalar(act, A)
        gate_scalar(act, A)

        def body(g):
            for n in range(UNITS):
                act.wait_ge(up_done[3], UNITS * g + n + 1)
                if not (known_zero(g) and n < 4):
                    act.wait_ge(prod_step, UNITS * g + n - 3)
                act.activation(act_ring[:, n % 4, :], bank[2 * (n % 2)][:], ACT.Silu).then_inc(act_ready[3], 1)
            act.wait_ge(down_done[1], UNITS * g + UNITS)
            if not known_zero(g):
                act.wait_ge(back_done[3], g)
            act.activation(outT[:], bank[6][:], ACT.Copy).then_inc(outT_ready[3], 1)

        groups(act, body)

    def vector3(dve, A):
        weights_in(dve, A)
        norm_vector(dve, A)
        gate_vector(dve, A)

        def body(g):
            for n in range(UNITS):
                dve.wait_ge(act_ready[3], UNITS * g + n + 1)
                if not (known_zero(g) and n < 4):
                    dve.wait_ge(down_done[1], UNITS * g + n - 3)
                up_bank = bank[2 * (n % 2) + 1]
                if n < EXPERTS:
                    dve.tensor_tensor(shared_u[:, n % 4, :], up_bank[:], act_ring[:, n % 4, :], ALU.mult)\
                       .then_inc(prod_step, 1)
                    dve.wait_ge(prod_step, UNITS * g + n + 1)
                    dve.wait_ge(bc_done[1], EXPERTS * g + n + 1)
                    dve.tensor_tensor(gated_ring[:, n % 4, :], bank[4 + n % 2][:], shared_u[:, n % 4, :],
                                      ALU.mult).then_inc(gated_done[1], 1)
                else:
                    dve.tensor_tensor(gated_ring[:, n % 4, :], up_bank[:], act_ring[:, n % 4, :], ALU.mult)\
                       .then_inc(prod_step, 1)
                    dve.wait_ge(prod_step, UNITS * g + n + 1)
                    dve.nop().then_inc(gated_done[1], 1)
            add_vector(dve, A, g, bank[7])

        groups(dve, body)

    def setup_vector(dve):
        dve.memset(onesB[:], 1.0).then_inc(setup_done, 1)
        dve.memset(onesF[:], 1.0).then_inc(setup_done, 1)

    def tensor(pe, A):
        pe.wait_ge(stage_done, A.stages)
        {"ffn0": tensor0, "ffn1": tensor1, "ffn2": tensor2, "ffn3": tensor3}[A.kind](pe, A)

    def scalar(act, A):
        act.wait_ge(stage_done, A.stages)
        {"ffn0": scalar0, "ffn1": scalar1, "ffn2": scalar2, "ffn3": scalar3}[A.kind](act, A)

    def vector(dve, A):
        {"ffn0": vector0, "ffn1": vector1, "ffn2": vector2, "ffn3": vector3}[A.kind](dve, A)
        dve.wait_ge(added[A.index], TILES if A.kind == "ffn1" else GROUPS)
        dve.nop().then_inc(stage_done, 1)

    def pool(pool_, A, rsqrt):
        pool_.wait_ge(stage_done, A.stages)
        rsqrt(pool_, TILES, A.ln)
        if A.kind == "ffn1":
            rsqrt(pool_, 1, A.ln + 1)
            pool1(pool_, A)
        pool_.wait_ge(stage_done, A.stages + 1)

    F.n_loads = lambda kind: len(lists[kind])
    F.loads, F.setup_vector, F.tensor, F.scalar, F.vector, F.pool = loads, setup_vector, tensor, scalar, vector, pool
    return F


def kernel(**inputs):
    import ml_dtypes
    import numpy as np
    import concourse.bacc as bacc
    from concourse.bass_utils import run_bass_kernel_spmd

    a, outs = lay_out(np, ml_dtypes, **{k: np.asarray(v) for k, v in inputs.items()})
    nc = bacc.Bacc("TRN2", target_bir_lowering=False, num_devices=1)
    w = {n: nc.dram_tensor("in_" + n, v.shape, mybir.dt.from_np(v.dtype), kind="ExternalInput").ap()
         for n, v in a.items()}
    out = nc.dram_tensor("out_x", outs, F32, kind="ExternalOutput").ap()
    build(nc, w, out, len(LAYERS))
    r = run_bass_kernel_spmd(nc, [{"in_" + n: v for n, v in a.items()}], core_ids=[0])
    y = r.results[0]["out_x"]
    return y.transpose(1, 0, 2).reshape(BATCH, SEQ, D)


def lay_out(np, ml_dtypes, **i):
    bf = ml_dtypes.bfloat16
    c = np.ascontiguousarray

    def col(v, n=1):
        return c(v.reshape(n, -1).T)

    tri = np.where(np.arange(P)[None, :] <= np.arange(P)[:, None], 0.0, -1e30)
    sel = np.zeros((P, EXPERTS, P), np.float32)
    for e in range(EXPERTS):
        sel[[e, 32 + e, 64 + e], e, :] = 1.0
    b2pad = np.zeros((P, D), np.float32)
    for r in (0, 32, 64):
        b2pad[r:r + EXPERTS] = i["L2_ffn_b2"]
    ctx = i["ctx_1024"]
    wkv = i["L1_xattn_Wkv"]
    a = dict(
        x=c(i["x"].reshape(TILES, P, D).transpose(1, 0, 2)),
        ctxT=c(ctx.reshape(TOKENS, D).T),
        ctx=c(ctx.reshape(BATCH, TPB, P, D).transpose(0, 2, 1, 3)),
        rowmask=c(i["mask_BxS_ik0"].reshape(TILES, P).T),
        keymask=c(i["mask_Bx1x1xS2_ff0"].reshape(1, TOKENS)),
        ident=np.eye(P, dtype=np.float32), identB=np.eye(P, dtype=np.float32).astype(bf),
        triB=c(np.stack([tri, tri], 1).astype(bf)),
        headmask=c((np.arange(P)[:, None] // 8 == np.arange(HEADS)[None, :]).astype(np.float32)),
        W1T=c(i["L0_ffn_W1"].T), b1c=col(i["L0_ffn_b1"], 4), b2c=col(i["L0_ffn_b2"]),
        W2T=c(i["L0_ffn_W2"].T.reshape(4, P, D).transpose(1, 0, 2).reshape(P, 512)),
        WQ1=c(i["L1_xattn_Wq"]), WK1=c(wkv[:, :1024]), WV1=c(wkv[:, 1024:]),
        WO1=c(i["L1_xattn_Wout"].reshape(PAIRS, P, D).transpose(1, 0, 2)), bo1=col(i["L1_xattn_bout"]),
        gamma=col(i["L1_ffn_bn_gamma"]), beta=col(i["L1_ffn_bn_beta"]),
        WKQ=c(i["L1_ffn_w_q"].reshape(16, P, D).transpose(1, 0, 2)),
        keysT=c(i["L1_ffn_keys_p"].transpose(3, 0, 2, 1).reshape(P, 512)),
        downT=c(i["L1_ffn_down"][:NE_USED].T), up=c(i["L1_ffn_up"][:NE_USED].reshape(CHUNKS, P, D).transpose(1, 0, 2)),
        WQ2=c(i["L2_xattn_Wq"].T), WK2=c(i["L2_xattn_Wk"].T), WV2=c(i["L2_xattn_Wv"].T), WO2=c(i["L2_xattn_Wo"].T),
        bq2=col(i["L2_xattn_bq"]), bk2=col(i["L2_xattn_bk"]), bo2=col(i["L2_xattn_bo"]),
        bv2=c(np.broadcast_to(i["L2_xattn_bv"], (P, D))),
        F1=c(i["L2_ffn_W1"].transpose(1, 0, 2)), f1b=c(i["L2_ffn_b1"].reshape(16, P).T),
        F2=c(i["L2_ffn_W2"].reshape(16, P, D).transpose(1, 0, 2)), b2pad=b2pad,
        wredT=c(i["L2_ffn_w_red"].T), wg=c(i["L2_ffn_wg"]),
        sel=sel.astype(bf), iota8=c(np.broadcast_to(np.arange(8, dtype=np.float32), (P, 8))),
        before=(np.arange(P)[:, None] < np.arange(P)[None, :]).astype(bf),
        WQ3=c(i["L3_xattn_Wq"]), WK3=c(i["L3_xattn_Wk"]), WV3=c(i["L3_xattn_Wv"]),
        WO3=c(i["L3_xattn_Wo"].reshape(PAIRS, P, D).transpose(1, 0, 2)),
        gateW3=c(i["L3_ffn_gate_w"].T), WG=c(i["L3_ffn_we_gate"].transpose(2, 0, 1)),
        WU=c(i["L3_ffn_we_up"].transpose(2, 0, 1)), WD=c(i["L3_ffn_we_down"].transpose(2, 0, 1)),
        SG=c(i["L3_ffn_ws_gate"].T.reshape(P, 2, P)), SU=c(i["L3_ffn_ws_up"].T.reshape(P, 2, P)),
        SD=c(i["L3_ffn_ws_down"].T.reshape(2, P, D).transpose(1, 0, 2)),
    )
    return a, (P, TILES, D)
```

```python
from contextlib import ExitStack

import concourse.bass as bass
from concourse import mybir
from concourse.alu_op_type import AluOpType as ALU

ACT = mybir.ActivationFunctionType
AX = mybir.AxisListType.X
F32 = mybir.dt.float32
BF16 = mybir.dt.bfloat16
I32 = mybir.dt.int32
U32 = mybir.dt.uint32

P = 128
D = 128
BATCH, SEQ = 8, 256
TOKENS = BATCH * SEQ
TILES = TOKENS // P
TPB = SEQ // P
HEADS = 16
PAIRS = HEADS // 2
GROUP = 512
GROUPS = TOKENS // GROUP
TPG = GROUP // P
EPS = 1e-5
PENALTY = 1.0e6
RSQRT_SEED = float(0x5F3759DF)
NEWTON = 3
LN_CHAIN = 4 * NEWTON


LAYERS = ["raw", "ffn0", "rows", "ffn1", "bias", "ffn2", "keys", "ffn3"]


def take_counts(layer, c):
    layer.scores, layer.exp, layer.rawmax, layer.negmax = c["scores"], c["exp"], c["rawmax"], c["negmax"]
    layer.rinv, layer.norm, layer.tp, layer.pt, layer.av = c["rinv"], c["norm"], c["tp"], c["pt"], c["av"]
    layer.ot, layer.km, layer.qt, layer.vc, layer.ctx = c["ot"], c["km"], c["qt"], c["vc"], c["ctx"]
    layer.xn, layer.ln, layer.stat, layer.nat = c["xn"], c["ln"], c["stat"], c["nat"]
    layer.stages = c["stages"]


class Attention:

    def __init__(self, kind, base):
        self.kind = kind
        self.wide = kind in ("rows", "keys")
        self.causal = not self.wide
        self.scale = 1.0 if self.wide else 8 ** -0.5
        self.slabs = PAIRS if self.wide else 1
        take_counts(self, base)
        self.uses = {part: [u for t in range(PAIRS) for slot in "ABC" for u in self.bank_uses(part, t, slot)]
                     for part in ("first", "loop", "last")}
        if self.wide:
            self.uses["pre"] = ["ln", "qk0", "qk1", "qk2", "qk3", "v0", "v1"]
        else:
            self.uses["pre"] = {"raw": ["ln"], "bias": ["k", "ln", "q"]}[kind]
        self.uses["epi"] = ["back"] if kind == "raw" else ["out", "back"]
        self.fill0, self.drain0 = {}, {}
        fills, drains = base["fill"], base["drain"]
        for part, times in (("pre", 1), ("first", 1), ("loop", BATCH - 2), ("last", 1), ("epi", 1)):
            self.fill0[part], self.drain0[part] = fills, drains
            fills += times * len(self.uses[part])
            drains += times * sum(self.drains_of(u) for u in self.uses[part])
        per = dict(scores=2, exp=2, rawmax=2, negmax=2, rinv=2, norm=2, tp=2, pt=1, av=1)
        self.after = {k: base[k] + v * BATCH * PAIRS for k, v in per.items()}
        self.after.update(
            ot=base["ot"] + (BATCH * PAIRS if self.wide else BATCH),
            km=base["km"] + (0 if self.wide else BATCH * PAIRS),
            qt=base["qt"] + (0 if self.wide else BATCH),
            vc=base["vc"] + (2 * BATCH if kind == "raw" else 0),
            ctx=base["ctx"] + BATCH, xn=base["xn"] + TPB * BATCH, ln=base["ln"] + BATCH,
            stat=base["stat"] + 7 * BATCH, nat=base["nat"] + (BATCH if kind == "raw" else 0),
            stages=base["stages"] + 1, fill=fills, drain=drains)

    def bank_uses(self, part, t, slot):
        before, after = part != "first", part != "last"
        out = []
        if self.wide:
            if slot == ("C" if t == 2 else "A") and (t < 4 or after):
                out.append(f"qk{(t + 4) % PAIRS}")
            if slot == "C" and t in (0, 1):
                out.append(f"v{t + 2}")
            if slot == "C" and t == 3 and after:
                out.append("ln")
            if slot == "C" and t in (4, 6) and after:
                out.append(f"v{(t - 4) // 2}")
            if slot == "C" and t == 5 and before:
                out.append("back")
        elif self.kind == "bias":
            if (t, slot) == (1, "B"):
                out.append("v")
            if (t, slot) == (2, "C") and after:
                out.append("k")
            if (t, slot) == (6, "B") and after:
                out.append("q")
        if (t, slot) == (5, "C") and after and not self.wide:
            out.append("ln")
        if (t, slot) == (2, "A") and before and self.kind != "raw":
            out.append("out")
        if (t, slot) == (4, "B") and before and not self.wide:
            out.append("back")
        return out

    def drains_of(self, use):
        if use.startswith("qk"):
            return 3
        return 2 if use.startswith("v") else 1

    def fills(self, part, b, use):
        n = self.fill0[part] + self.uses[part].index(use) + 1
        return n + (b - 1) * len(self.uses["loop"]) if part == "loop" else n

    def drained(self, part, b, use, whole=True):
        names = self.uses[part]
        n = self.drain0[part] + sum(self.drains_of(u) for u in names[:names.index(use) + whole])
        return n + (b - 1) * sum(self.drains_of(u) for u in self.uses["loop"]) if part == "loop" else n


def known_below(g, n):
    return isinstance(g, int) and g < n


def build(nc, w, out, layers):
    with ExitStack() as ctx:
        def sb(name, shape, dt=F32):
            return ctx.enter_context(nc.sbuf_tensor("sb_" + name, shape, dt))

        def sem(name):
            return ctx.enter_context(nc.semaphore(name))

        x = sb("x", [P, TILES, D])
        xn_all = sb("xn_all", [P, TILES, D])
        xnT_all = sb("xnT_all", [P, TOKENS])
        ident = sb("ident", [P, P])
        identB = sb("identB", [P, P], BF16)
        triB = sb("triB", [P, 2, P], BF16)
        onesB = sb("onesB", [P, P], BF16)
        headmask = sb("headmask", [P, HEADS])
        stats = sb("stats", [P, TILES, 6])
        mv = sb("mv", [P, TILES, 2])
        veps = sb("veps", [P, TILES])
        vhalf = sb("vhalf", [P, TILES])
        vbits = sb("vbits", [P, TILES], U32)
        c15 = sb("c15", [P, TILES])
        scratch = sb("scratch", [P, 2])
        rstd = sb("rstd", [P, TILES])
        ntmp = sb("ntmp", [P, TILES])
        ctxT_in = sb("ctxT_in", [P, SEQ])
        ctxT = sb("ctxT", [P, SEQ])
        xn = sb("xn", [P, TPB, D])
        xnT = sb("xnT", [P, SEQ])
        QT = sb("QT", [P, PAIRS, SEQ])
        KM = sb("KM", [P, PAIRS, 2, SEQ])
        VP = sb("VP", [P, TPB, HEADS, P])
        both = sb("both", [P, 4096])
        PR = both[:, 0:2048].rearrange("p (g i h k) -> p g i h k", g=2, i=TPB, h=2)
        PT = both[:, 2048:4096].rearrange("p (g h i q) -> p g h i q", g=2, h=2, i=TPB)
        rawmax = sb("rawmax", [P, 2, TPB, 2])
        negmax = sb("negmax", [P, 2, TPB, 2])
        rowsum = sb("rowsum", [P, 2, TPB, 2])
        rinv = sb("rinv", [P, 2, TPB, 2])
        OT = sb("OT", [P, PAIRS, SEQ])
        kT_all = OT[:, 1, :]
        qT_next = OT[:, 2, :]
        ctxN = OT[:, 3, :].rearrange("p (i d) -> p i d", i=TPB)
        outT = sb("outT", [P, GROUP])
        rowmask = sb("rowmask", [P, TILES], I32)
        rowpen = sb("rowpen", [P, TILES])
        keymask = xn_all[:].rearrange("p a b -> p (a b)")
        WQ1, WK1, WV1 = (sb(n, [P, 1024]) for n in ("WQ1", "WK1", "WV1"))
        WO1 = sb("WO1", [P, PAIRS, D])
        WQ3, WK3, WV3 = (sb(n, [P, 1024]) for n in ("WQ3", "WK3", "WV3"))
        WO3 = sb("WO3", [P, PAIRS, D])
        WQ2, WK2, WV2, WO2 = (sb(n, [P, D]) for n in ("WQ2", "WK2", "WV2", "WO2"))
        bq2, bk2, bo2, bo1 = (sb(n, [P, 1]) for n in ("bq2", "bk2", "bo2", "bo1"))
        bv2 = sb("bv2", [P, D])
        bank = [ctx.enter_context(nc.psum_tensor(f"bank{i}", [P, GROUP], F32)) for i in range(8)]

        x_in, x_rest_in = sem("x_in"), sem("x_rest_in")
        const_in = sem("const_in")
        rowmask_in, keymask_in = sem("rowmask_in"), sem("keymask_in")
        rowpen_ready = sem("rowpen_ready")
        masked = sem("masked")
        w_in = [sem(f"w_in{i}") for i in range(8)]
        ctx_in, nat_in = sem("ctx_in"), sem("nat_in")
        out_done = sem("out_done")
        setup_done = sem("setup_done")
        zeros_done = sem("zeros_done")
        stage_done = sem("stage_done")
        stat_step = sem("stat_step")
        seed_ready = sem("seed_ready")
        newton_step = sem("newton_step")
        xn_ready = sem("xn_ready")
        ctx_ready = sem("ctx_ready")
        fill_done, drain_done = sem("fill_done"), sem("drain_done")
        scores_ready = sem("scores_ready")
        rawmax_done, negmax_ready = sem("rawmax_done"), sem("negmax_ready")
        exp_done = sem("exp_done")
        rinv_ready = sem("rinv_ready")
        probs_ready = sem("probs_ready")
        tp_done = sem("tp_done")
        pt_ready = [sem("pt_ready0"), sem("pt_ready1")]
        av_done = sem("av_done")
        ot_ready = sem("ot_ready")
        km_ready = sem("km_ready")
        qt_ready = sem("qt_ready")
        vc_ready = sem("vc_ready")
        def own_wait(dve, cell=0):
            dve.memset(scratch[:, cell:cell + 1], 0.0)

        def seed(dve, variance, lo, hi, at):
            dve.tensor_scalar(veps[:, lo:hi], variance, EPS, None, ALU.add).then_inc(stat_step, 1)
            dve.tensor_scalar(vhalf[:, lo:hi], variance, EPS, -0.5, ALU.add, ALU.mult).then_inc(stat_step, 1)
            dve.wait_ge(stat_step, at + 2)
            dve.tensor_scalar(vbits[:, lo:hi], veps[:, lo:hi].bitcast(U32), 1, None,
                              ALU.logical_shift_right).then_inc(stat_step, 1)
            dve.wait_ge(stat_step, at + 3)
            dve.tensor_scalar(rstd[:, lo:hi].bitcast(I32), vbits[:, lo:hi], -1.0, RSQRT_SEED,
                              ALU.mult, ALU.add).then_inc(seed_ready, 1)

        S = dict(
            x=x, xn_all=xn_all, xnT_all=xnT_all, ident=ident, identB=identB, bank=bank, outT=outT, QT=QT, OT=OT,
            both=both, KM=KM, VP=VP, stats=stats, mv=mv, veps=veps, vbits=vbits, rstd=rstd,
            onesB=onesB, w_in=w_in, const_in=const_in, stat_step=stat_step,
            seed_ready=seed_ready, newton_step=newton_step, xn_ready=xn_ready, stage_done=stage_done,
            setup_done=setup_done, seed=seed, own_wait=own_wait)

        zero = {k: 0 for k in ("scores", "exp", "rawmax", "negmax", "rinv", "norm", "tp", "pt", "av", "ot",
                               "km", "qt", "vc", "ctx", "xn", "ln", "stat", "nat", "stages", "fill", "drain")}
        kinds = LAYERS
        plan, now = [], zero
        for kind in kinds[:layers]:
            plan.append(Attention(kind, now) if not kind.startswith("ffn") else FeedForward(kind, now))
            now = plan[-1].after
        zeros, narrow = 1, 0
        for A in plan:
            if isinstance(A, Attention):
                A.narrow = narrow
                narrow += 0 if A.wide else A.after["rawmax"] - A.rawmax
                zeros += 2 if A.wide else 1
                A.zeros = zeros
        ctxT_v = w["ctxT"]
        ctxN_v = w["ctx"]
        ffn = feed_forward(nc, ctx, sb, sem, S, w)
        block = ctx.enter_context(nc.Block())
        layer_of = {k: i for i, k in enumerate(kinds)}
        weights = {"rows": (WQ1, WK1, WV1, WO1), "keys": (WQ3, WK3, WV3, WO3), "bias": (WQ2, WK2, WV2, WO2)}

        @block.sync
        def _(sp):
            sp.dma_start(x[:, 0:TPB, :], w["x"][:, 0:TPB, :]).then_inc(x_in, 16)
            sp.dma_start(ctxT_in[:], ctxT_v[:, 0:SEQ]).then_inc(ctx_in, 16)
            for dst, name in ((headmask, "headmask"), (ident, "ident"), (identB, "identB"), (triB, "triB")):
                sp.dma_start(dst[:], w[name]).then_inc(const_in, 16)
            sp.dma_start(x[:, TPB:TILES, :], w["x"][:, TPB:TILES, :]).then_inc(x_rest_in, 16)
            sp.dma_start(ctxN, ctxN_v[0]).then_inc(nat_in, 16)
            ffn.loads(sp, "ffn0")
            sp.dma_start(rowmask[:], w["rowmask"]).then_inc(rowmask_in, 16)
            layer_weights = (
                ("rows", ((WQ1, "WQ1"), (WK1, "WK1"), (WV1, "WV1"), (WO1, "WO1"), (bo1, "bo1"))),
                ("ffn1", ()),
                ("bias", ((WQ2, "WQ2"), (WK2, "WK2"), (WV2, "WV2"), (WO2, "WO2"), (bq2, "bq2"),
                          (bk2, "bk2"), (bo2, "bo2"), (bv2, "bv2"))),
                ("ffn2", ()),
                ("keys", ((WQ3, "WQ3"), (WK3, "WK3"), (WV3, "WV3"), (WO3, "WO3"))),
                ("ffn3", ()))
            layers_attn = [A for A in plan if isinstance(A, Attention)]
            for A in layers_attn:
                more = A is not layers_attn[-1]
                if A.kind == "keys":
                    sp.wait_ge(ffn.lnT_done, 3 * GROUPS)
                    sp.dma_start(keymask, w["keymask"].broadcast_to([P, TOKENS])).then_inc(keymask_in, 16)
                with sp.Fori(0, BATCH - 1) as b:
                    sp.wait_ge(ctx_ready, A.ctx + b + 1)
                    sp.dma_start(ctxT_in[:], ctxT_v[:, bass.ts(b + 1, SEQ)]).then_inc(ctx_in, 16)
                    if A.kind == "raw":
                        sp.wait_ge(vc_ready, A.vc + 2 * b + 2)
                        sp.dma_start(ctxN, ctxN_v[b + 1]).then_inc(nat_in, 16)
                if more:
                    sp.wait_ge(ctx_ready, A.ctx + BATCH)
                    sp.dma_start(ctxT_in[:], ctxT_v[:, 0:SEQ]).then_inc(ctx_in, 16)
                if A is layers_attn[0]:
                    for kind, pairs in layer_weights:
                        if kind.startswith("ffn"):
                            ffn.loads(sp, kind)
                        for dst, name in pairs:
                            sp.dma_start(dst[:], w[name]).then_inc(w_in[layer_of[kind]], 16)
            for kind, pairs in layer_weights:
                sp.wait_ge(w_in[layer_of[kind]], 16 * (len(pairs) or ffn.n_loads(kind)))
            sp.wait_ge(w_in[1], 16 * ffn.n_loads("ffn0"))
            sp.wait_ge(rowmask_in, 16)
            if len(plan) > layer_of["keys"]:
                sp.wait_ge(keymask_in, 16)
            if plan[-1].kind == "ffn3":
                for g in range(GROUPS):
                    sp.wait_ge(ffn.added[3], g + 2)
                    tiles = slice(TPG * g, TPG * g + TPG)
                    sp.dma_start(out[:, tiles, :], x[:, tiles, :]).then_inc(out_done, 16)
                sp.wait_ge(out_done, 16 * GROUPS)
            else:
                sp.wait_ge(stage_done, len(plan))
                sp.dma_start(out, x[:]).then_inc(out_done, 16)
                sp.wait_ge(out_done, 16)

        pre_banks = (bank[7], bank[6], bank[5], bank[4])

        def home(A, part, use):
            if A.wide and part == "pre":
                return pre_banks[A.uses["pre"].index(use) % len(pre_banks)]
            return bank[7]

        def copy_pt(eng, A, b, t, qt):
            g = PAIRS * b + t
            if not known_below(g, 2):
                eng.wait_ge(av_done, A.av + g - 1)
            eng.wait_ge(tp_done, A.tp + 2 * g + qt + 1)
            kts = qt + 1 if A.causal else TPB
            src = bank[4 + qt][:].rearrange("p (h kt q) -> p h kt q", h=2, kt=TPB)[:, :, 0:kts, :]
            dst = PT[:, t % 2, :, 0:kts, qt * P:(qt + 1) * P]
            if pt_engine(A, qt) == "scalar":
                ins = eng.activation(dst, src, ACT.Copy)
            else:
                ins = eng.tensor_copy(dst, src)
            ins.then_inc(pt_ready[qt], 1)

        def pt_engine(A, qt):
            return "scalar" if A.wide and qt == 1 else "vector"

        def attention_tensor(pe, A):
            WQ, WK, WV, WO = weights.get(A.kind, (None,) * 4)

            def wait_bank(part, b, use):
                if A.wide and part == "pre":
                    k = A.uses["pre"].index(use)
                    if use == "qk0":
                        pe.wait_ge(drain_done, A.drained("pre", 0, "ln"))
                    if k >= len(pre_banks):
                        pe.wait_ge(drain_done, A.drained("pre", 0, A.uses["pre"][k - len(pre_banks)]))
                elif not (part == "pre" and A.drained(part, b, use, False) == 0):
                    pe.wait_ge(drain_done, A.drained(part, b, use, False))

            def put(part, b, use):
                wait_bank(part, b, use)
                shared = home(A, part, use)
                if use == "ln":
                    nxt = 0 if part == "pre" else b + 1
                    pe.wait_ge(xn_ready, A.xn + TPB * nxt + TPB)
                    for i in range(TPB):
                        last = pe.transpose(shared[:, i * P:(i + 1) * P], xn[:, i, :], ident[:])
                elif use.startswith("qk"):
                    j = int(use[2:])
                    if j == 0:
                        pe.wait_ge(ctx_ready, A.ctx + (1 if part == "pre" else b + 2))
                    pe.matmul(shared[:, 0:SEQ], WQ[:, j * P:(j + 1) * P], xnT[:], start=True, stop=True)
                    last = pe.matmul(shared[:, SEQ:2 * SEQ], WK[:, j * P:(j + 1) * P], ctxT[:],
                                     start=True, stop=True)
                elif use == "q":
                    last = pe.matmul(shared[:, 0:SEQ], WQ[:], xnT[:], start=True, stop=True)
                elif use == "k":
                    pe.wait_ge(ctx_ready, A.ctx + (1 if part == "pre" else b + 2))
                    last = pe.matmul(shared[:, 0:SEQ], WK[:], ctxT[:], start=True, stop=True)
                elif use == "v":
                    for kt in range(TPB):
                        last = pe.matmul(shared[:, kt * D:(kt + 1) * D], ctxT[:, kt * P:(kt + 1) * P], WV[:],
                                         start=True, stop=True)
                elif use.startswith("v"):
                    m = int(use[1:])
                    for kt in range(TPB):
                        last = pe.matmul(shared[:, kt * 256:(kt + 1) * 256], ctxT[:, kt * P:(kt + 1) * P],
                                         WV[:, m * 256:(m + 1) * 256], start=True, stop=True)
                elif use == "out":
                    if A.wide:
                        pe.wait_ge(ot_ready, A.ot + PAIRS * b)
                    else:
                        pe.wait_ge(ot_ready, A.ot + b)
                    for j in range(A.slabs):
                        wo = WO[:, j, :] if A.wide else WO[:]
                        last = pe.matmul(shared[:, 0:SEQ], wo, OT[:, j, :], start=(j == 0),
                                         stop=(j == A.slabs - 1))
                elif use == "back":
                    if A.kind == "raw":
                        pe.wait_ge(ot_ready, A.ot + b)
                    for i in range(TPB):
                        last = pe.transpose(shared[:, i * P:(i + 1) * P], outT[:, i * P:(i + 1) * P], ident[:])
                last.then_inc(fill_done, 1)

            def scores(b, t):
                g = PAIRS * b + t
                if not known_below(g, 2):
                    pe.wait_ge(exp_done, A.exp + 2 * g - 2)
                if not A.wide:
                    pe.wait_ge(km_ready, A.km + g + 1)
                    if t == 0:
                        pe.wait_ge(qt_ready, A.qt + b + 1)
                for qt in range(TPB):
                    keys = P if A.causal and qt == 0 else SEQ
                    s = bank[2 * (t % 2) + qt][:].rearrange("p (h k) -> p h k", h=2)
                    q = QT[:, t if A.wide else 0, qt * P:(qt + 1) * P]
                    last = pe.matmul(s[:, :, 0:keys], q, KM[:, t, :, 0:keys], start=True, stop=not A.causal)
                    if A.causal:
                        last = pe.matmul(s[:, :, qt * P:(qt + 1) * P], identB[:], triB[:], start=False, stop=True)
                    last.then_inc(scores_ready, 1)

            def transposes(b, t):
                g = PAIRS * b + t
                for qt in range(TPB):
                    pe.wait_ge(probs_ready, A.norm + 2 * g + qt + 1)
                    if not known_below(g, 1):
                        pe.wait_ge(pt_ready[qt], A.pt + g)
                    for h in range(2):
                        for kt in range(qt + 1 if A.causal else TPB):
                            n = h * TPB + kt
                            last = pe.transpose(bank[4 + qt][:, n * P:(n + 1) * P],
                                                PR[:, t % 2, qt, h, kt * P:(kt + 1) * P], ident[:])
                    last.then_inc(tp_done, 1)

            def weighted(part, b, t):
                g = PAIRS * b + t
                for qt in range(TPB):
                    pe.wait_ge(pt_ready[qt], A.pt + g + 1)
                if A.wide and not known_below(g, 1):
                    pe.wait_ge(ot_ready, A.ot + g)
                if not A.wide and t == 0:
                    if not known_below(b, 1):
                        pe.wait_ge(ot_ready, A.ot + b)
                    if A.kind == "raw":
                        pe.wait_ge(vc_ready, A.vc + 2 * b + 2)
                    else:
                        pe.wait_ge(drain_done, A.drained(part, b, "v"))
                if A.wide:
                    for kt in range(TPB):
                        for h in range(2):
                            rows = slice(64 * h, 64 * h + 64)
                            last = pe.matmul(bank[6][rows, 0:SEQ], VP[:, kt, 2 * t + h, rows], PT[:, t % 2, h, kt, :],
                                             start=kt == 0, stop=kt == TPB - 1)
                else:
                    rows = slice(32 * (t // 2), 32 * (t // 2) + 32)
                    for h in range(2):
                        for kt in range(TPB):
                            lo = P if kt == 1 else 0
                            last = pe.matmul(bank[6][rows, lo:SEQ], VP[:, kt, 2 * t + h, rows],
                                             PT[:, t % 2, h, kt, lo:SEQ], start=(h == 0 and kt == 0 and t % 2 == 0),
                                             stop=(h == 1 and kt == 1 and t % 2 == 1))
                last.then_inc(av_done, 1)

            def step(part, b, t):
                g = PAIRS * b + t
                scores(b, t)
                for use in A.bank_uses(part, t, "A"):
                    put(part, b, use)
                if not known_below(g, 2):
                    weighted(part, b if t >= 2 else b - 1, (t - 2) % PAIRS)
                for use in A.bank_uses(part, t, "B"):
                    put(part, b, use)
                if not known_below(g, 1):
                    transposes(b if t >= 1 else b - 1, (t - 1) % PAIRS)
                for use in A.bank_uses(part, t, "C"):
                    put(part, b, use)

            if A.stages:
                pe.wait_ge(stage_done, A.stages)
            else:
                pe.wait_ge(const_in, 16 * 4)
            if A.kind != "raw":
                n = {"rows": 5, "bias": 8, "keys": 4}[A.kind]
                pe.wait_ge(w_in[layer_of[A.kind]], 16 * n)
            pe.wait_ge(zeros_done, A.zeros)
            for use in A.uses["pre"]:
                put("pre", 0, use)
            pe.wait_ge(drain_done, A.drained("pre", 0, "qk1" if A.wide else A.uses["pre"][-1]))
            for t in range(PAIRS):
                step("first", 0, t)
            with pe.Fori(1, BATCH - 1) as b:
                for t in range(PAIRS):
                    step("loop", b, t)
            for t in range(PAIRS):
                step("last", BATCH - 1, t)
            weighted("last", BATCH - 1, PAIRS - 2)
            transposes(BATCH - 1, PAIRS - 1)
            weighted("last", BATCH - 1, PAIRS - 1)
            for use in A.uses["epi"]:
                put("epi", BATCH, use)

        @block.tensor
        def _(pe):
            for A in plan:
                if isinstance(A, Attention):
                    attention_tensor(pe, A)
                else:
                    ffn.tensor(pe, A)

        def attention_scalar(act, A):
            def take(part, b, use):
                if use not in ("ln", "q", "k", "out") and not use.startswith("qk"):
                    return
                act.wait_ge(fill_done, A.fills(part, b, use))
                shared = home(A, part, use)
                if use == "ln":
                    dst = qT_next if A.kind == "raw" else xnT[:]
                    if A.kind == "raw" and part != "pre":
                        act.wait_ge(qt_ready, A.qt + b + 1)
                    act.activation(dst, shared[:, 0:SEQ], ACT.Copy).then_inc(drain_done, 1)
                elif use == "q":
                    if part != "pre":
                        act.wait_ge(qt_ready, A.qt + b + 1)
                    act.activation(qT_next, shared[:, 0:SEQ], ACT.Identity, bias=bq2[:]).then_inc(drain_done, 1)
                elif use == "k":
                    if part != "pre":
                        act.wait_ge(km_ready, A.km + PAIRS * b + PAIRS)
                    act.activation(kT_all, shared[:, 0:SEQ], ACT.Identity, bias=bk2[:]).then_inc(drain_done, 1)
                elif use.startswith("qk"):
                    act.activation(QT[:, int(use[2:]), :], shared[:, 0:SEQ], ACT.Copy,
                                   scale=64 ** -0.5).then_inc(drain_done, 1)
                    for h in range(2):
                        act.activation(KM[64 * h:64 * h + 64, int(use[2:]), h, :],
                                       shared[64 * h:64 * h + 64, SEQ:2 * SEQ], ACT.Copy).then_inc(drain_done, 1)
                elif use == "out":
                    bias = {"rows": bo1, "bias": bo2}.get(A.kind)
                    if bias is None:
                        act.activation(outT[:, 0:SEQ], shared[:, 0:SEQ], ACT.Copy).then_inc(drain_done, 1)
                    else:
                        act.activation(outT[:, 0:SEQ], shared[:, 0:SEQ], ACT.Identity,
                                       bias=bias[:]).then_inc(drain_done, 1)

            def spread_keys(part, b, t):
                if A.kind == "raw":
                    act.wait_ge(ctx_ready, A.ctx + b + 1)
                else:
                    if isinstance(b, int) and b == 0:
                        act.wait_ge(drain_done, A.drained("pre", 0, "k"))
                    elif t >= PAIRS - 3:
                        pass
                    else:
                        act.wait_ge(drain_done, A.drained(part, b - 1, "k"))
                src = ctxT[:] if A.kind == "raw" else kT_all
                act.activation(KM[:, t, 0, :], src, ACT.Copy, scale=headmask[:, 2 * t:2 * t + 1])
                act.activation(KM[:, t, 1, :], src, ACT.Copy,
                               scale=headmask[:, 2 * t + 1:2 * t + 2]).then_inc(km_ready, 1)

            def exps(b, t):
                g = PAIRS * b + t
                for qt in range(TPB):
                    act.wait_ge(negmax_ready, A.negmax + 2 * g + qt + 1)
                    if not known_below(g, 2):
                        act.wait_ge(tp_done, A.tp + 2 * g - 4 + qt + 1)
                    keys = P if A.causal and qt == 0 else SEQ
                    s = bank[2 * (t % 2) + qt][:].rearrange("p (h k) -> p h k", h=2)
                    for h in range(2):
                        last = act.activation(PR[:, t % 2, qt, h, 0:keys], s[:, h, 0:keys], ACT.Exp,
                                              bias=negmax[:, t % 2, qt, h:h + 1], scale=A.scale,
                                              accum_out=rowsum[:, t % 2, qt, h:h + 1])
                    last.then_inc(exp_done, 1)

            def heads_out(part, b, t):
                g = PAIRS * b + t
                if not A.wide and t != PAIRS - 1:
                    return
                act.wait_ge(av_done, A.av + g + 1)
                if A.kind == "raw":
                    act.activation(outT[:, 0:SEQ], bank[6][:, 0:SEQ], ACT.Copy).then_inc(ot_ready, 1)
                else:
                    act.activation(OT[:, t if A.wide else 0, :], bank[6][:, 0:SEQ], ACT.Copy).then_inc(ot_ready, 1)

            def step(part, b, t):
                g = PAIRS * b + t
                if not known_below(g, 2) and pt_engine(A, 1) == "scalar":
                    copy_pt(act, A, b if t >= 2 else b - 1, (t - 2) % PAIRS, 1)
                for use in A.bank_uses(part, t, "A"):
                    take(part, b, use)
                exps(b, t)
                if not known_below(g, 2):
                    heads_out(part, b if t >= 2 else b - 1, (t - 2) % PAIRS)
                for use in A.bank_uses(part, t, "B"):
                    take(part, b, use)
                if not A.wide and (t < 3 or part != "last"):
                    spread_keys(part, b if t < 3 else b + 1, (t + 5) % PAIRS)
                for use in A.bank_uses(part, t, "C"):
                    take(part, b, use)

            if A.stages:
                act.wait_ge(stage_done, A.stages)
            else:
                act.wait_ge(const_in, 16 * 4)
            if A.kind != "raw":
                n = {"rows": 5, "bias": 8, "keys": 4}[A.kind]
                act.wait_ge(w_in[layer_of[A.kind]], 16 * n)
            act.wait_ge(zeros_done, A.zeros)
            if A.kind == "bias":
                take("pre", 0, "k")
            if not A.wide:
                for t in range(PAIRS - 3):
                    spread_keys("pre", 0, t)
                    if t == 0:
                        take("pre", 0, "ln")
                    if t == 2 and A.kind == "bias":
                        take("pre", 0, "q")
            else:
                for use in A.uses["pre"]:
                    take("pre", 0, use)
            for t in range(PAIRS):
                step("first", 0, t)
            with act.Fori(1, BATCH - 1) as b:
                for t in range(PAIRS):
                    step("loop", b, t)
            for t in range(PAIRS):
                step("last", BATCH - 1, t)
            for t in (PAIRS - 2, PAIRS - 1):
                if pt_engine(A, 1) == "scalar":
                    copy_pt(act, A, BATCH - 1, t, 1)
                heads_out("last", BATCH - 1, t)
            for use in A.uses["epi"]:
                take("epi", BATCH, use)

        @block.scalar
        def _(act):
            for A in plan:
                if isinstance(A, Attention):
                    attention_scalar(act, A)
                else:
                    ffn.scalar(act, A)

        def norm_stats(dve, A, b):
            base = A.stat + 7 * b
            for i in range(TPB):
                dve.bn_stats(stats[:, i, :], x[:, TPB * b + i, :]).then_inc(stat_step, 1)
            dve.wait_ge(stat_step, base + 2)
            own_wait(dve)
            for i in range(TPB):
                dve.bn_aggr(mv[:, i, :], stats[:, i, :]).then_inc(stat_step, 1)
            dve.wait_ge(stat_step, base + 4)
            seed(dve, mv[:, 0:TPB, 1], 0, TPB, base + 4)

        def take_context(dve, A, b):
            dve.wait_ge(ctx_in, 16 * (A.ctx + b + 1))
            dve.tensor_copy(ctxT[:], ctxT_in[:]).then_inc(ctx_ready, 1)

        def start_vector(dve, A):
            take_context(dve, A, 0)
            norm_stats(dve, A, 0)

        def attention_vector(dve, A, following):
            def normalise(b):
                dve.wait_ge(newton_step, LN_CHAIN * (A.ln + b + 1))
                for i in range(TPB):
                    dve.tensor_scalar(xn[:, i, :], x[:, TPB * b + i, :], mv[:, i, 0:1], rstd[:, i:i + 1],
                                      ALU.subtract, ALU.mult).then_inc(xn_ready, 1)

            def take(part, b, use):
                if not (use == "back" or use in ("v", "v0", "v1", "v2", "v3")):
                    return
                dve.wait_ge(fill_done, A.fills(part, b, use))
                if part == "pre":
                    dve.wait_ge(drain_done, A.drained("pre", 0, use, False))
                shared = home(A, part, use)
                if use == "v":
                    for kt in range(TPB):
                        dve.tensor_tensor(diagonal(kt), shared[:, kt * D:(kt + 1) * D].rearrange(
                            "p (h c) -> p h c", h=HEADS), bv2[:].rearrange("p (h c) -> p h c", h=HEADS),
                            ALU.add).then_inc(drain_done, 1)
                elif use.startswith("v"):
                    m = int(use[1:])
                    src = shared[:].rearrange("p (kt pp h c) -> p kt pp h c", kt=TPB, pp=2, h=2)
                    for h in range(2):
                        dst = VP[:, :, 4 * m + h:4 * m + 4:2, 64 * h:64 * h + 64]
                        dve.tensor_copy(dst, src[:, :, :, h, :]).then_inc(drain_done, 1)
                elif use == "back":
                    xb = x[:, bass.ds(TPB * (b - 1), TPB), :]
                    last = dve.tensor_tensor(xb, shared[:, 0:SEQ].rearrange("p (i d) -> p i d", i=TPB), xb, ALU.add)
                    last.then_inc(drain_done, 1)

            def diagonal(kt):
                flat = VP[:, kt, :, :].rearrange("p h c -> p (h c)")
                return bass.AP(tensor=flat.tensor, offset=flat.offset, ap=[list(flat.ap[0]), [P + 8, HEADS], [1, 8]])

            def values_raw(b):
                if not known_below(b, 1):
                    dve.wait_ge(av_done, A.av + PAIRS * b)
                dve.wait_ge(nat_in, 16 * (A.nat + b + 1))
                for kt in range(TPB):
                    dve.tensor_copy(diagonal(kt), ctxN[:, kt, :].rearrange("p (h c) -> p h c", h=HEADS))\
                       .then_inc(vc_ready, 1)

            def maxima(b, t):
                g = PAIRS * b + t
                for qt in range(TPB):
                    keys = P if A.causal and qt == 0 else SEQ
                    s = bank[2 * (t % 2) + qt][:].rearrange("p (h k) -> p h k", h=2)
                    dve.wait_ge(scores_ready, A.scores + 2 * g + qt + 1)
                    if A.wide:
                        if A.kind == "rows":
                            mask = rowpen[:, bass.ds(TPB * b + qt, 1)].unsqueeze(2).broadcast_to([P, 2, SEQ])
                        else:
                            mask = keymask[:, bass.ds(b * SEQ, SEQ)].unsqueeze(1).broadcast_to([P, 2, SEQ])
                        dve.tensor_tensor(s, s, mask, ALU.add).then_inc(masked, 1)
                        dve.wait_ge(masked, A.rawmax - A.narrow + 2 * g + qt + 1)
                    dve.tensor_reduce(rawmax[:, t % 2, qt, :], s[:, :, 0:keys], AX, ALU.max).then_inc(rawmax_done, 1)
                    dve.wait_ge(rawmax_done, A.rawmax + 2 * g + qt + 1)
                    dve.tensor_scalar(negmax[:, t % 2, qt, :], rawmax[:, t % 2, qt, :], -A.scale, None,
                                      ALU.mult).then_inc(negmax_ready, 1)

            def inverses(b, t, qts=range(TPB)):
                g = PAIRS * b + t
                for qt in qts:
                    dve.wait_ge(exp_done, A.exp + 2 * g + qt + 1)
                    dve.reciprocal(rinv[:, t % 2, qt, :], rowsum[:, t % 2, qt, :]).then_inc(rinv_ready, 1)

            def step(part, b, t):
                g = PAIRS * b + t
                more = part != "last"
                before, before2 = (b if t >= 1 else b - 1, (t - 1) % PAIRS), (b if t >= 2 else b - 1, (t - 2) % PAIRS)
                if not known_below(g, 1):
                    inverses(*before, [0])
                for qt in range(TPB):
                    if not known_below(g, 2) and pt_engine(A, qt) == "vector":
                        copy_pt(dve, A, *before2, qt)
                if not known_below(g, 1):
                    inverses(*before, [1])
                maxima(b, t)
                if t == 0 and more:
                    if part == "first" and not A.stages:
                        dve.wait_ge(x_rest_in, 16)
                    norm_stats(dve, A, b + 1)
                if t == 4 - A.wide and more:
                    normalise(b + 1)
                if A.kind == "bias" and t == 2 and more:
                    take_context(dve, A, b + 1)
                if A.kind == "raw" and t == 3 and more:
                    dve.wait_ge(km_ready, A.km + PAIRS * b + PAIRS)
                    take_context(dve, A, b + 1)
                if t == PAIRS - 1 and more and not A.wide:
                    dve.wait_ge(drain_done, A.drained(part, b, "ln" if A.kind == "raw" else "q"))
                    dve.tensor_copy(QT[:, 0, :], qT_next).then_inc(qt_ready, 1)
                for use in A.bank_uses(part, t, "A"):
                    take(part, b, use)
                if t == 3 and more and A.wide:
                    dve.wait_ge(fill_done, A.fills(part, b, "qk7"))
                    take_context(dve, A, b + 1)
                if t == 1 and A.kind == "raw":
                    values_raw(b)
                for use in A.bank_uses(part, t, "B"):
                    take(part, b, use)
                for use in A.bank_uses(part, t, "C"):
                    take(part, b, use)

            if not A.stages:
                dve.wait_ge(x_in, 16)
                start_vector(dve, A)
            normalise(0)
            if A.kind != "raw":
                n = {"rows": 5, "bias": 8, "keys": 4}[A.kind]
                dve.wait_ge(w_in[layer_of[A.kind]], 16 * n)
            dve.wait_ge(zeros_done, A.zeros)
            if A.kind == "rows":
                dve.wait_ge(rowmask_in, 16)
                dve.tensor_scalar(rowpen[:], rowmask[:], -1.0, PENALTY, ALU.add, ALU.mult).then_inc(rowpen_ready, 1)
                dve.wait_ge(rowpen_ready, 1)
            if A.kind == "keys":
                dve.wait_ge(keymask_in, 16)
            for use in A.uses["pre"]:
                take("pre", 0, use)
            if not A.wide:
                dve.wait_ge(drain_done, A.drained("pre", 0, "ln" if A.kind == "raw" else "q"))
                dve.tensor_copy(QT[:, 0, :], qT_next).then_inc(qt_ready, 1)
            for t in range(PAIRS):
                step("first", 0, t)
            with dve.Fori(1, BATCH - 1) as b:
                for t in range(PAIRS):
                    step("loop", b, t)
            for t in range(PAIRS):
                step("last", BATCH - 1, t)
            inverses(BATCH - 1, PAIRS - 1)
            for t in (PAIRS - 2, PAIRS - 1):
                for qt in range(TPB):
                    if pt_engine(A, qt) == "vector":
                        copy_pt(dve, A, BATCH - 1, t, qt)
            if following:
                dve.wait_ge(drain_done, A.drained("last", BATCH - 1, "back"))
                ffn.early_stats(dve, following)
            for use in A.uses["epi"]:
                take("epi", BATCH, use)
            dve.wait_ge(drain_done, A.after["drain"])
            dve.nop().then_inc(stage_done, 1)

        @block.vector
        def _(dve):
            ffn.setup_vector(dve)
            for A, following in zip(plan, plan[1:] + [None]):
                if isinstance(A, Attention):
                    attention_vector(dve, A, following)
                else:
                    ffn.vector(dve, A, lambda: following and start_vector(dve, following))

        def rsqrt(pool, lo, hi, ln, rounds=range(NEWTON)):
            step = LN_CHAIN * ln
            if 0 in rounds:
                pool.wait_ge(seed_ready, ln + 1)
            y, a = rstd[:, lo:hi], ntmp[:, lo:hi]
            for k in rounds:
                if k:
                    pool.wait_ge(newton_step, step + 4 * k)
                pool.tensor_tensor(a, y, y, ALU.mult).then_inc(newton_step, 1)
                pool.wait_ge(newton_step, step + 4 * k + 1)
                pool.tensor_tensor(a, a, vhalf[:, lo:hi], ALU.mult).then_inc(newton_step, 1)
                pool.wait_ge(newton_step, step + 4 * k + 2)
                pool.tensor_tensor(a, a, c15[:, lo:hi], ALU.add).then_inc(newton_step, 1)
                pool.wait_ge(newton_step, step + 4 * k + 3)
                pool.tensor_tensor(y, y, a, ALU.mult).then_inc(newton_step, 1)

        def attention_pool(pool, A):
            def step(part, b, t):
                g = PAIRS * b + t
                for qt in range(TPB):
                    keys = P if A.causal and qt == 0 else SEQ
                    pool.wait_ge(rinv_ready, A.rinv + 2 * g + qt + 1)
                    p = PR[:, t % 2, qt, :, 0:keys]
                    pool.tensor_tensor(p, p, rinv[:, t % 2, qt, :].unsqueeze(2).broadcast_to([P, 2, keys]),
                                       ALU.mult).then_inc(probs_ready, 1)
                if t < NEWTON and part != "last":
                    rsqrt(pool, 0, TPB, A.ln + b + 1, [t])

            if not A.stages:
                pool.memset(c15[:], 1.5).then_inc(zeros_done, 1)
                pool.wait_ge(zeros_done, 1)
                clear(pool, A)
            rsqrt(pool, 0, TPB, A.ln)
            for t in range(PAIRS):
                step("first", 0, t)
            with pool.Fori(1, BATCH - 1) as b:
                for t in range(PAIRS):
                    step("loop", b, t)
            for t in range(PAIRS):
                step("last", BATCH - 1, t)

        def clear(pool, A):
            pool.memset(VP[:], 0.0).then_inc(zeros_done, 1)
            if A.wide:
                pool.memset(KM[:], 0.0).then_inc(zeros_done, 1)

        @block.gpsimd
        def _(pool):
            for A, following in zip(plan, plan[1:] + [None]):
                if isinstance(A, Attention):
                    attention_pool(pool, A)
                else:
                    ffn.pool(pool, A, rsqrt, lambda: following and clear(pool, following))


class FeedForward:

    def __init__(self, kind, base):
        self.kind = kind
        take_counts(self, base)
        self.index = int(kind[3:])
        norms = 3 if kind == "ffn1" else 2
        self.after = dict(base, xn=base["xn"] + TILES, ln=base["ln"] + norms,
                          stat=base["stat"] + 2 * TILES + 6 + (GROUPS + 4 if norms == 3 else 0),
                          stages=base["stages"] + 1)


EARLY = TILES - TPB
NE_USED = 1024
CHUNKS = NE_USED // P
PK_HEADS, NK, TOPK = 8, 32, 8
EXPERTS = 8
CAPACITY = 640


def feed_forward(nc, ctx, sb, sem, S, w):
    x, xn_all, xnT_all, ident, identB = (S[n] for n in ("x", "xn_all", "xnT_all", "ident", "identB"))
    bank, outT, QT, OT, both, KM, VP = (S[n] for n in ("bank", "outT", "QT", "OT", "both", "KM", "VP"))
    stats, mv, veps, vbits, rstd = (S[n] for n in ("stats", "mv", "veps", "vbits", "rstd"))
    onesB, w_in, const_in = S["onesB"], S["w_in"], S["const_in"]
    stat_step, seed_ready, newton_step, xn_ready = (S[n] for n in ("stat_step", "seed_ready", "newton_step", "xn_ready"))
    stage_done, setup_done = S["stage_done"], S["setup_done"]

    W1T, W2T = sb("W1T", [P, 512]), sb("W2T", [P, 512])
    b1c, b2c = sb("b1c", [P, 4]), sb("b2c", [P, 1])
    abssum = sb("abssum", [P, 2])
    onesF = sb("onesF", [P, P])
    half, neghalf = sb("half", [P, 2]), sb("neghalf", [P, 2])
    above, below = OT[:, 0:2, :].rearrange("p a b -> p (a b)"), OT[:, 2:4, :].rearrange("p a b -> p (a b)")
    absjunk = OT[:, 4:6, :].rearrange("p a b -> p (a b)")
    hidden = QT[:].rearrange("p a b -> p (a b)").rearrange("p (s n) -> p s n", s=4)
    WKQ, keysT = sb("WKQ", [P, 16, P]), sb("keysT", [P, 512])
    AK = QT[:, 0:2, :].rearrange("p a b -> p (a b)")
    downT, up = sb("downT", [P, NE_USED]), sb("up", [P, CHUNKS, D])
    gamma, beta = sb("gamma", [P, 1]), sb("beta", [P, 1])
    bnstats, bnmv = sb("bnstats", [P, GROUPS, 6]), sb("bnmv", [P, 2])
    bn_a, bn_c = sb("bn_a", [P, 1]), sb("bn_c", [P, 1])
    xbT = QT[:, 2, :].rearrange("p (a b) -> p a b", a=2)
    sims = OT[:].rearrange("p a b -> p (a b)").rearrange("p (g n) -> p g n", g=4)
    top = sb("top", [P, 2, 16, TOPK])
    combos = QT[:, 4:6, :].rearrange("p a b -> p (a b)")
    best = sb("best", [P, 2, PK_HEADS, TOPK])
    pairsum = KM[:].rearrange("p a b c -> p (a b c)").rearrange("p (r n) -> p r n", r=4)
    gated = both[:].rearrange("p (r n) -> p r n", r=4)
    HG = xn_all[:].rearrange("p a b -> p (a b)").rearrange("p (r c n) -> p r c n", r=2, c=CHUNKS)
    F1, F2 = sb("F1", [P, EXPERTS, 256]), sb("F2", [P, 16, D])
    f1b = sb("f1b", [P, 16])
    b2pad = sb("b2pad", [P, D])
    b2parts = sb("b2parts", [P, 3, D], BF16)
    wredT, wg = sb("wredT", [16, P]), sb("wg", [8, 16])
    wgn, wgnT = sb("wgn", [8, 16]), sb("wgnT", [16, 8])
    wsq, wnorm = sb("wsq", [8, 16]), sb("wnorm", [8, 4])
    gateW = sb("gateW", [P, 2, EXPERTS])
    WG, WU, WD = (sb(n, [P, EXPERTS, P]) for n in ("WG", "WU", "WD"))
    SG, SU, SD = (sb(n, [P, 2, P]) for n in ("SG", "SU", "SD"))
    sel = sb("sel", [P, EXPERTS, P], BF16)
    iota8 = sb("iota8", [P, EXPERTS])
    before = sb("before", [P, P], BF16)
    gt = {n: sb("g_" + n, [P, TILES, EXPERTS]) for n in ("lg", "m8", "e8", "idxf", "oh1", "oh2", "comb", "t1", "pre", "r")}
    idx8 = sb("idx8", [P, TILES, EXPERTS], U32)
    gs = {n: sb("gs_" + n, [P, TILES]) for n in ("z", "zi", "p1", "p2", "den", "di", "w1", "w2")}
    picks = sb("picks", [P, TILES, EXPERTS], BF16)
    parts = QT[:].rearrange("p a b -> p (a b)").bitcast(BF16)[:, 0:TILES * P].rearrange("p (t c) -> p t c", t=TILES)
    gT = sb("gT", [P, TOKENS], BF16)
    act_ring = both[:, 0:2048].rearrange("p (r n) -> p r n", r=4)
    gated_ring = both[:, 2048:4096].rearrange("p (r n) -> p r n", r=4)
    shared_u = VP[:].rearrange("p a b c -> p (a b c)")[:, 0:2048].rearrange("p (r n) -> p r n", r=4)

    abs_ready, abs_sum, scale_ready = sem("abs_ready"), sem("abs_sum"), sem("scale_ready")
    tern_step = sem("tern_step")
    lnT_done, xnT_ready = sem("lnT_done"), sem("xnT_ready")
    up_done = [sem(f"up_done{i}") for i in range(4)]
    act_ready = [sem(f"act_ready{i}") for i in range(4)]
    out_ready = sem("out_ready")
    outT_ready = [sem(f"outT_ready{i}") for i in range(4)]
    back_done = [sem(f"back_done{i}") for i in range(4)]
    added = [sem(f"added{i}") for i in range(4)]
    ak_done, ak_ready = sem("ak_done"), sem("ak_ready")
    bn_step, bn_ready = sem("bn_step"), sem("bn_ready")
    xb_ready, sim_done, sims_ready = sem("xb_ready"), sem("sim_done"), sem("sims_ready")
    top_done, combos_done, best_done = sem("top_done"), sem("combos_done"), sem("best_done")
    sum_ready = sem("sum_ready")
    sig_ready = sem("sig_ready")
    gated_ready = sem("gated_ready")
    wT_done = sem("wT_done")
    mixed = sem("mixed")
    gate_w_step = sem("gate_w_step")
    lg_done = sem("lg_done")
    gate_step = sem("gate_step")
    gexp_go, gexp_done = sem("gexp_go"), sem("gexp_done")
    count_done = sem("count_done")
    parts_ready, gT_done, gT_ready = sem("parts_ready"), sem("gT_done"), sem("gT_ready")
    b2_step = sem("b2_step")
    bc_done = [sem("bc_done2"), sem("bc_done3")]
    prod_step = sem("prod_step")
    gated_done = [sem("gated_done2"), sem("gated_done3")]
    down_done = [sem("down_done2"), sem("down_done3")]

    class Programs:
        pass

    F = Programs()
    F.lnT_done, F.added = lnT_done, added
    lists = {
        "ffn0": ((W1T, "W1T"), (W2T, "W2T"), (b1c, "b1c"), (b2c, "b2c")),
        "ffn1": ((WKQ, "WKQ"), (keysT, "keysT"), (downT, "downT"), (up, "up"), (gamma, "gamma"), (beta, "beta")),
        "ffn2": ((F1, "F1"), (F2, "F2"), (f1b, "f1b"), (b2pad, "b2pad"), (wredT, "wredT"), (wg, "wg"),
                 (sel, "sel"), (iota8, "iota8")),
        "ffn3": ((gateW[:, 1, :], "gateW3"), (WG, "WG"), (WU, "WU"), (WD, "WD"), (SG, "SG"), (SU, "SU"), (SD, "SD"),
                 (before, "before")),
    }
    layer_no = {"ffn0": 1, "ffn1": 3, "ffn2": 5, "ffn3": 7}

    def loads(sp, kind):
        for dst, name in lists[kind]:
            sp.dma_start(dst if name == "gateW3" else dst[:], w[name]).then_inc(w_in[layer_no[kind]], 16)

    def weights_in(eng, A):
        eng.wait_ge(w_in[layer_no[A.kind]], 16 * len(lists[A.kind]))

    def tile_stats(dve, lo, hi, at):
        for i in range(lo, hi):
            dve.bn_stats(stats[:, i, :], x[:, i, :]).then_inc(stat_step, 1)
        dve.wait_ge(stat_step, at + hi - lo)
        for i in range(lo, hi):
            dve.bn_aggr(mv[:, i, :], stats[:, i, :]).then_inc(stat_step, 1)
        dve.wait_ge(stat_step, at + 2 * (hi - lo))
        S["seed"](dve, mv[:, lo:hi, 1], lo, hi, at + 2 * (hi - lo))

    def early_stats(dve, A):
        tile_stats(dve, 0, EARLY, A.stat)

    def norm_vector(dve, A):
        tile_stats(dve, EARLY, TILES, A.stat + 2 * EARLY + 3)
        for n, (lo, hi) in enumerate(((0, EARLY), (EARLY, TILES))):
            dve.wait_ge(newton_step, LN_CHAIN * (A.ln + n + 1))
            for i in range(lo, hi):
                dve.tensor_scalar(xn_all[:, i, :], x[:, i, :], mv[:, i, 0:1], rstd[:, i:i + 1],
                                  ALU.subtract, ALU.mult).then_inc(xn_ready, 1)

    def norm_tensor(pe, A):
        for g in range(GROUPS):
            pe.wait_ge(xn_ready, A.xn + TPG * (g + 1))
            for i in range(TPG):
                last = pe.transpose(bank[g][:, i * P:(i + 1) * P], xn_all[:, TPG * g + i, :], ident[:])
            last.then_inc(lnT_done, 1)

    def norm_scalar(act, A):
        for g in range(GROUPS):
            act.wait_ge(lnT_done, GROUPS * A.index + g + 1)
            act.activation(xnT_all[:, g * GROUP:(g + 1) * GROUP], bank[g][:], ACT.Copy).then_inc(xnT_ready, 1)

    def back_tensor(pe, A, g, home):
        pe.wait_ge(outT_ready[A.index], g + 1)
        pe.wait_ge(added[A.index], g + 1)
        for i in range(TPG):
            last = pe.transpose(home[:, i * P:(i + 1) * P], outT[:, i * P:(i + 1) * P], ident[:])
        last.then_inc(back_done[A.index], 1)

    def add_vector(dve, A, g, home):
        dve.wait_ge(back_done[A.index], g + 1)
        xg = x[:, bass.ds(TPG * g, TPG), :]
        dve.tensor_tensor(xg, home[:].rearrange("p (i d) -> p i d", i=TPG), xg, ALU.add).then_inc(added[A.index], 1)

    def known_zero(g):
        return isinstance(g, int) and g == 0

    def groups(eng, body):
        body(0)
        with eng.Fori(1, GROUPS) as g:
            body(g)

    def with_adds(dve, A, home, body, before_last):
        dve.nop().then_inc(added[A.index], 1)
        groups(dve, body)
        before_last()
        add_vector(dve, A, GROUPS - 1, home)

    def tensor0(pe, A):
        pe.wait_ge(setup_done, 2)
        pe.wait_ge(abs_ready, 2)
        pe.matmul(bank[6][:, 0:2], onesF[:], abssum[:], start=True, stop=True).then_inc(abs_sum, 1)
        norm_tensor(pe, A)
        pe.wait_ge(tern_step, 4)

        def body(g):
            if known_zero(g):
                pe.wait_ge(xnT_ready, GROUPS * A.index + GROUPS)
            for s in range(4):
                if not known_zero(g):
                    pe.wait_ge(act_ready[0], 4 * g - 4 + s + 1)
                pe.matmul(bank[s][:], W1T[:, s * P:(s + 1) * P], xnT_all[:, bass.ts(g, GROUP)],
                          start=True, stop=True).then_inc(up_done[0], 1)
            if not known_zero(g):
                back_tensor(pe, A, g - 1, bank[5])
            if known_zero(g):
                pe.wait_ge(tern_step, 8)
            else:
                pe.wait_ge(outT_ready[0], g)
            for s in range(4):
                pe.wait_ge(act_ready[0], 4 * g + s + 1)
                last = pe.matmul(bank[4][:], W2T[:, s * P:(s + 1) * P], hidden[:, s, :], start=(s == 0), stop=(s == 3))
            last.then_inc(out_ready, 1)

        groups(pe, body)
        back_tensor(pe, A, GROUPS - 1, bank[5])

    def scalar0(act, A):
        weights_in(act, A)
        act.activation(absjunk, W1T[:], ACT.Abs, accum_out=abssum[:, 0:1]).then_inc(abs_ready, 1)
        act.wait_ge(abs_ready, 1)
        act.activation(absjunk, W2T[:], ACT.Abs, accum_out=abssum[:, 1:2]).then_inc(abs_ready, 1)
        norm_scalar(act, A)

        def body(g):
            for s in range(4):
                act.wait_ge(up_done[0], 4 * g + s + 1)
                if not known_zero(g):
                    act.wait_ge(out_ready, g)
                act.activation(hidden[:, s, :], bank[s][:], ACT.Gelu, bias=b1c[:, s:s + 1]).then_inc(act_ready[0], 1)
            if not known_zero(g):
                act.wait_ge(back_done[0], g)
            act.wait_ge(out_ready, g + 1)
            act.activation(outT[:], bank[4][:], ACT.Identity, bias=b2c[:]).then_inc(outT_ready[0], 1)

        groups(act, body)

    def vector0(dve, A, before_last):
        def ternary():
            dve.wait_ge(abs_sum, 1)
            dve.tensor_scalar(half[:], bank[6][:, 0:2], 1.0 / (512 * D), 1e-8, ALU.mult, ALU.max)\
               .then_inc(scale_ready, 1)
            dve.wait_ge(scale_ready, 1)
            dve.tensor_scalar(neghalf[:], half[:], -0.5, None, ALU.mult).then_inc(scale_ready, 1)
            dve.wait_ge(scale_ready, 2)
            dve.tensor_scalar(half[:], half[:], 0.5, None, ALU.mult).then_inc(scale_ready, 1)
            dve.wait_ge(scale_ready, 3)
            for n, wt in enumerate((W1T, W2T)):
                dve.tensor_scalar(below, wt[:], neghalf[:, n:n + 1], None, ALU.is_lt).then_inc(tern_step, 1)
                dve.wait_ge(tern_step, 4 * n + 1)
                dve.scalar_tensor_tensor(out=above, in0=wt[:], scalar=half[:, n:n + 1], in1=below,
                                         op0=ALU.is_gt, op1=ALU.subtract).then_inc(tern_step, 1)
                dve.wait_ge(tern_step, 4 * n + 2)
                dve.tensor_tensor(below, above, wt[:], ALU.subtract).then_inc(tern_step, 1)
                dve.wait_ge(tern_step, 4 * n + 3)
                dve.tensor_tensor(wt[:], wt[:], below, ALU.add).then_inc(tern_step, 1)
                dve.wait_ge(tern_step, 4 * n + 4)

        norm_vector(dve, A)
        ternary()

        def body(g):
            if not known_zero(g):
                add_vector(dve, A, g - 1, bank[5])

        with_adds(dve, A, bank[5], body, before_last)

    def steps1(eng, step):
        far = TILES
        for t in range(TPG):
            step(t, far, t, t)
        with eng.Fori(1, GROUPS - 1) as g:
            for t in range(TPG):
                step(far, far, TPG * g + t, t)
        for t in range(TPG):
            step(far, TPG - 1 - t, TILES - TPG + t, t)

    def weight_bank(t, c):
        return bank[(2, 6)[t % 2] + c // 4][:, (c % 4) * P:(c % 4 + 1) * P]

    def tensor1(pe, A):
        weights_in(pe, A)
        for p in range(2):
            for h in range(PK_HEADS):
                c = (2 * h + p) * NK
                last = pe.matmul(bank[4][:, c:c + NK], WKQ[:, p * PK_HEADS + h, :], keysT[:, c:c + NK],
                                 start=True, stop=True)
        last.then_inc(ak_done, 1)
        norm_tensor(pe, A)
        pe.wait_ge(ak_ready, 1)

        def similar(first, i, t):
            pe.wait_ge(xb_ready, i + 1)
            if first > 0:
                pe.wait_ge(sims_ready, i)
            pe.matmul(bank[0][:], xbT[:, t % 2, :], AK, start=True, stop=True).then_inc(sim_done, 1)

        def lower(first, i):
            for half_ in range(2):
                if first > 0:
                    pe.wait_ge(act_ready[1], 2 * i + half_ - 1)
                for c in range(4):
                    last = pe.matmul(bank[4 + half_][:, c * P:(c + 1) * P],
                                     downT[:, (4 * half_ + c) * P:(4 * half_ + c + 1) * P],
                                     xnT_all[:, bass.ds(i * P, P)], start=True, stop=True)
                last.then_inc(up_done[1], 1)

        def upper(first, i, t):
            pe.wait_ge(mixed, 2 * i + 2)
            if first > 0:
                pe.wait_ge(added[1], i)
            for c in range(CHUNKS):
                last = pe.matmul(bank[1][:, 0:D], HG[:, t % 2, c, :], up[:, c, :],
                                 start=(c == 0), stop=(c == CHUNKS - 1))
            last.then_inc(back_done[1], 1)

        def step(first, last_, i, t):
            if first > 0:
                upper(first - 1, i - 1, t - 1)
            for h in range(PK_HEADS):
                pe.wait_ge(gated_ready, PK_HEADS * i + h + 1)
                if h == 0 and first > 1:
                    pe.wait_ge(mixed, 2 * i - 2)
                for c in range(CHUNKS):
                    last = pe.matmul(weight_bank(t, c), gated[:, h % 4, c * P:(c + 1) * P], ident[:],
                                     is_transpose=True, start=(h == 0 and c % 4 == 0),
                                     stop=(h == PK_HEADS - 1 and c % 4 == 3), skip_group_check=True)
                last.then_inc(wT_done, 1)
                if h == 1 and last_ > 1:
                    similar(first + 2, i + 2, t)
                if h == 3 and last_ > 0:
                    lower(first + 1, i + 1)

        pe.wait_ge(xnT_ready, GROUPS * A.index + GROUPS)
        lower(0, 0)
        similar(0, 0, 0)
        similar(1, 1, 1)
        steps1(pe, step)
        prepare_tensor(pe)
        upper(TILES, TILES - 1, TPG - 1)
        prepare_tensor_end(pe)

    def scalar1(act, A):
        weights_in(act, A)
        act.wait_ge(ak_done, 1)
        act.activation(AK, bank[4][:], ACT.Copy).then_inc(ak_ready, 1)
        norm_scalar(act, A)
        prepare_scalar(act)
        act.wait_ge(bn_ready, 1)

        def inputs(first, i, t):
            if first > 1:
                act.wait_ge(sim_done, i - 1)
            act.activation(xbT[:, t % 2, :], xnT_all[:, bass.ds(i * P, P)], ACT.Identity, bias=bn_c[:], scale=bn_a[:])\
               .then_inc(xb_ready, 1)

        def copy_sims(first, i, t):
            act.wait_ge(sim_done, i + 1)
            if first > 3:
                act.wait_ge(top_done, 16 * (i - 3))
                act.wait_ge(gated_ready, PK_HEADS * (i - 3))
            act.activation(sims[:, t % 4, :], bank[0][:], ACT.Copy).then_inc(sims_ready, 1)

        def step(first, last_, i, t):
            if last_ > 1:
                inputs(first + 2, i + 2, t)
            if last_ > 0:
                copy_sims(first + 1, i + 1, t + 1)
            for half_ in range(2):
                act.wait_ge(up_done[1], 2 * i + half_ + 1)
                if half_ == 0 and first > 1:
                    act.wait_ge(back_done[1], i - 1)
                act.activation(HG[:, t % 2, 4 * half_:4 * half_ + 4, :],
                               bank[4 + half_][:].rearrange("p (c n) -> p c n", c=4), ACT.Gelu).then_inc(act_ready[1], 1)
            for h in range(PK_HEADS):
                n = PK_HEADS * i + h
                act.wait_ge(sum_ready, n + 1)
                if first > 0 or h >= 4:
                    act.wait_ge(wT_done, n - 3)
                act.activation(gated[:, h % 4, :], pairsum[:, h % 4, :], ACT.Sigmoid).then_inc(sig_ready, 1)

        inputs(0, 0, 0)
        inputs(1, 1, 1)
        copy_sims(0, 0, 0)
        steps1(act, step)

    def pool1(pool, A):
        def step(first, last_, i, t):
            pool.wait_ge(sims_ready, i + 1)
            s = sims[:, t % 4, :].rearrange("p (h q k) -> p h q k", h=PK_HEADS, q=2)
            for h in range(PK_HEADS):
                if first > 0 or h >= 4:
                    pool.wait_ge(gated_ready, PK_HEADS * i + h - 3)
                dst = pairsum[:, h % 4, :].rearrange("p (i j) -> p i j", i=NK)
                pool.tensor_tensor(dst, s[:, h, 0, :].unsqueeze(2).broadcast_to([P, NK, NK]),
                                   s[:, h, 1, :].unsqueeze(1).broadcast_to([P, NK, NK]), ALU.add)\
                    .then_inc(sum_ready, 1)

        steps1(pool, step)

    def vector1(dve, A, before_last):
        norm_vector(dve, A)
        dve.wait_ge(xnT_ready, GROUPS * A.index + GROUPS)
        for g in range(GROUPS):
            dve.bn_stats(bnstats[:, g, :], xnT_all[:, g * GROUP:(g + 1) * GROUP]).then_inc(stat_step, 1)
        at = A.stat + 2 * TILES + 6
        dve.wait_ge(stat_step, at + GROUPS)
        dve.bn_aggr(bnmv[:], bnstats[:].rearrange("p g s -> p (g s)")).then_inc(stat_step, 1)
        dve.wait_ge(stat_step, at + GROUPS + 1)
        S["seed"](dve, bnmv[:, 1:2], 0, 1, at + GROUPS + 1)
        prepare_vector(dve)
        dve.wait_ge(newton_step, LN_CHAIN * (A.ln + 3))
        weights_in(dve, A)
        dve.tensor_tensor(bn_a[:], rstd[:, 0:1], gamma[:], ALU.mult).then_inc(bn_step, 1)
        dve.wait_ge(bn_step, 1)
        dve.tensor_tensor(bn_c[:], bnmv[:, 0:1], bn_a[:], ALU.mult).then_inc(bn_step, 1)
        dve.wait_ge(bn_step, 2)
        dve.tensor_tensor(bn_c[:], beta[:], bn_c[:], ALU.subtract).then_inc(bn_ready, 1)

        def choose(i, t):
            dve.wait_ge(sims_ready, i + 1)
            S["own_wait"](dve)
            for n in range(16):
                last = dve.max(top[:, t % 2, n, :], sims[:, t % 4, n * NK:(n + 1) * NK])
                last.then_inc(top_done, 1)
            dve.wait_ge(top_done, 16 * i + 16)
            pair = top[:, t % 2].rearrange("p (h q) k -> p h q k", q=2)
            dve.tensor_tensor(combos.rearrange("p (h a b) -> p h a b", h=PK_HEADS, a=TOPK),
                              pair[:, :, 0, :].unsqueeze(3).broadcast_to([P, PK_HEADS, TOPK, TOPK]),
                              pair[:, :, 1, :].unsqueeze(2).broadcast_to([P, PK_HEADS, TOPK, TOPK]), ALU.add)\
               .then_inc(combos_done, 1)
            dve.wait_ge(combos_done, i + 1)
            S["own_wait"](dve, 1)
            for h in range(PK_HEADS):
                dve.max(best[:, t % 2, h, :], combos[:, h * 64:(h + 1) * 64]).then_inc(best_done, 1)

        def mix(i, t):
            dve.wait_ge(wT_done, PK_HEADS * i + PK_HEADS)
            dve.wait_ge(act_ready[1], 2 * i + 2)
            for half_ in range(2):
                hg = HG[:, t % 2, 4 * half_:4 * half_ + 4, :]
                wt = bank[(2, 6)[t % 2] + half_][:].rearrange("p (c n) -> p c n", c=4)
                dve.tensor_tensor(hg, wt, hg, ALU.mult).then_inc(mixed, 1)

        def add_tile(i):
            dve.wait_ge(back_done[1], i + 1)
            xi = x[:, bass.ds(i, 1), :].rearrange("p a d -> p (a d)")
            dve.tensor_tensor(xi, bank[1][:, 0:D], xi, ALU.add).then_inc(added[1], 1)

        def step(first, last_, i, t):
            if last_ > 0:
                choose(i + 1, t + 1)
            if first > 0:
                mix(i - 1, t - 1)
            dve.wait_ge(best_done, PK_HEADS * i + PK_HEADS)
            for h in range(PK_HEADS):
                dve.wait_ge(sig_ready, PK_HEADS * i + h + 1)
                dve.scalar_tensor_tensor(out=gated[:, h % 4, :], in0=pairsum[:, h % 4, :],
                                         scalar=best[:, t % 2, h, TOPK - 1:TOPK], in1=gated[:, h % 4, :],
                                         op0=ALU.is_ge, op1=ALU.mult).then_inc(gated_ready, 1)
                if h == 3 and first > 0:
                    add_tile(i - 1)

        choose(0, 0)
        steps1(dve, step)
        mix(TILES - 1, TPG - 1)
        prepare_turned_vector(dve)
        before_last()
        add_tile(TILES - 1)
        prepare_gate_vector(dve)

    UPS_AHEAD2, UNITS_AHEAD3 = 4, 2
    UNITS = EXPERTS + 2

    def unit_weights(n):
        if n < EXPERTS:
            return WG[:, n, :], WU[:, n, :], WD[:, n, :]
        return SG[:, n - EXPERTS, :], SU[:, n - EXPERTS, :], SD[:, n - EXPERTS, :]

    def up2(pe, g, n):
        if not (known_zero(g) and n < 4):
            pe.wait_ge(act_ready[2], 16 * g + n - 3)
        pe.matmul(bank[n % 4][:], F1[:, n // 2, (n % 2) * P:(n % 2 + 1) * P], xnT_all[:, bass.ts(g, GROUP)],
                  start=True, stop=True).then_inc(up_done[2], 1)

    def up3(pe, g, n):
        if not (known_zero(g) and n < 2):
            pe.wait_ge(prod_step, UNITS * g + n - 1)
        wgate, wup, _ = unit_weights(n)
        pe.matmul(bank[2 * (n % 2)][:], wgate, xnT_all[:, bass.ts(g, GROUP)], start=True, stop=True)
        pe.matmul(bank[2 * (n % 2) + 1][:], wup, xnT_all[:, bass.ts(g, GROUP)],
                  start=True, stop=True).then_inc(up_done[3], 1)

    def gate_tensor(pe, A):
        k = A.index - 2
        for i in range(TILES):
            if i % TPG == 0:
                pe.wait_ge(xnT_ready, GROUPS * A.index + i // TPG + 1)
            last = pe.matmul(bank[6][:, i * EXPERTS:(i + 1) * EXPERTS], xnT_all[:, i * P:(i + 1) * P], gateW[:, k, :],
                             start=True, stop=True)
        last.then_inc(lg_done, 1)
        if k == 1:
            pe.wait_ge(count_done, 1)
            flat = picks[:].rearrange("p t e -> p (t e)")
            width = TILES * EXPERTS
            pe.matmul(bank[7][:, 0:width], before[:], flat, start=True, stop=True)
            for n in range(1, TILES):
                last = pe.matmul(bank[7][:, n * EXPERTS:width], onesB[:], flat[:, 0:width - n * EXPERTS],
                                 start=False, stop=True, skip_group_check=True)
            last.then_inc(count_done, 1)
        if k == 0:
            for n in range(UPS_AHEAD2):
                up2(pe, 0, n)
        else:
            for n in range(UNITS_AHEAD3):
                up3(pe, 0, n)
        pe.wait_ge(parts_ready, k + 1)
        for i in range(TILES):
            home = bank[4 + i // 8][:].bitcast(BF16)
            last = pe.transpose(home[:, (i % 8) * P:(i % 8 + 1) * P], parts[:, i, :], identB[:])
            if i % 8 == 7:
                last.then_inc(gT_done, 1)
        pe.wait_ge(gT_ready, 2 * k + 2)

    def gate_scalar(act, A):
        k = A.index - 2
        act.wait_ge(gexp_go, k + 1)
        act.activation(gt["e8"][:], gt["t1"][:], ACT.Exp).then_inc(gexp_done, 1)
        for half_ in range(2):
            act.wait_ge(gT_done, 2 * k + half_ + 1)
            act.activation(gT[:, half_ * 1024:(half_ + 1) * 1024], bank[4 + half_][:].bitcast(BF16), ACT.Copy)\
               .then_inc(gT_ready, 1)

    def gate_vector(dve, A):
        k = A.index - 2
        n = [gate_total[k]]

        def link(ins):
            n[0] += 1
            ins.then_inc(gate_step, 1)
            dve.wait_ge(gate_step, n[0])

        def wide(a):
            return a.unsqueeze(2).broadcast_to([P, TILES, EXPERTS])

        lg, m8, e8, oh1, oh2, comb, t1 = (gt[q] for q in ("lg", "m8", "e8", "oh1", "oh2", "comb", "t1"))
        link(dve.memset(parts, 0.0))
        dve.wait_ge(lg_done, k + 1)
        link(dve.tensor_copy(lg[:].rearrange("p t e -> p (t e)"), bank[6][:, 0:TILES * EXPERTS]))
        for i in range(TILES):
            ins = dve.max(m8[:, i, :], lg[:, i, :])
            n[0] += 1
            ins.then_inc(gate_step, 1)
        dve.wait_ge(gate_step, n[0])
        for i in range(TILES):
            ins = dve.max_index(idx8[:, i, :], m8[:, i, :], lg[:, i, :])
            n[0] += 1
            ins.then_inc(gate_step, 1)
        dve.tensor_tensor(t1[:], m8[:], wide(m8[:, :, 0]), ALU.subtract).then_inc(gexp_go, 1)
        dve.wait_ge(gate_step, n[0])
        link(dve.tensor_copy(gt["idxf"][:], idx8[:]))
        iota = iota8[:].unsqueeze(1).broadcast_to([P, TILES, EXPERTS])
        link(dve.tensor_tensor(oh1[:], wide(gt["idxf"][:, :, 0]), iota, ALU.is_equal))
        if k == 1:
            link(dve.tensor_tensor(oh2[:], wide(gt["idxf"][:, :, 1]), iota, ALU.is_equal))
            dve.tensor_tensor(picks[:], oh1[:], oh2[:], ALU.add).then_inc(count_done, 1)
        dve.wait_ge(gexp_done, k + 1)
        link(dve.tensor_reduce(gs["z"][:], e8[:], AX, ALU.add))
        link(dve.reciprocal(gs["zi"][:], gs["z"][:]))
        if k == 0:
            link(dve.tensor_tensor(comb[:], oh1[:], wide(gs["zi"][:]), ALU.mult))
        else:
            link(dve.tensor_tensor(gs["p1"][:], e8[:, :, 0], gs["zi"][:], ALU.mult))
            link(dve.tensor_tensor(gs["p2"][:], e8[:, :, 1], gs["zi"][:], ALU.mult))
            link(dve.tensor_tensor(gs["den"][:], gs["p1"][:], gs["p2"][:], ALU.add))
            link(dve.tensor_scalar(gs["den"][:], gs["den"][:], 1e-20, None, ALU.add))
            link(dve.reciprocal(gs["di"][:], gs["den"][:]))
            link(dve.tensor_tensor(gs["w1"][:], gs["p1"][:], gs["di"][:], ALU.mult))
            link(dve.tensor_tensor(gs["w2"][:], gs["p2"][:], gs["di"][:], ALU.mult))
            link(dve.tensor_tensor(oh1[:], oh1[:], wide(gs["w1"][:]), ALU.mult))
            link(dve.tensor_tensor(oh2[:], oh2[:], wide(gs["w2"][:]), ALU.mult))
            link(dve.tensor_tensor(comb[:], oh1[:], oh2[:], ALU.add))
            dve.wait_ge(count_done, 2)
            pre = gt["pre"]
            link(dve.tensor_scalar(pre[:], bank[7][:, 0:P].rearrange("p (t e) -> p t e", t=TILES),
                                   float(CAPACITY), None, ALU.is_lt))
            link(dve.tensor_tensor(comb[:], comb[:], pre[:], ALU.mult))
        r = gt["r"]
        link(dve.tensor_copy(parts[:, :, 0:8], comb[:]))
        link(dve.tensor_tensor(r[:], comb[:], parts[:, :, 0:8], ALU.subtract))
        link(dve.tensor_copy(parts[:, :, 32:40], r[:]))
        link(dve.tensor_tensor(r[:], r[:], parts[:, :, 32:40], ALU.subtract))
        dve.tensor_copy(parts[:, :, 64:72], r[:]).then_inc(parts_ready, 1)
        gate_total[k + 1] = n[0]

    gate_total = {0: 0}

    def prepare_tensor(pe):
        pe.wait_ge(w_in[5], 16 * len(lists["ffn2"]))
        pe.wait_ge(gate_w_step, 7)
        pe.transpose(bank[0][0:16, 0:8], wgn[:], ident[0:8, 0:8]).then_inc(gate_w_step, 1)

    def prepare_tensor_end(pe):
        pe.wait_ge(gate_w_step, 9)
        pe.matmul(bank[4][:, 0:8], wredT[:], wgnT[:], start=True, stop=True).then_inc(gate_w_step, 1)

    def prepare_scalar(act):
        act.wait_ge(gate_w_step, 2)
        act.activation(wnorm[:, 1:2], wnorm[:, 0:1], ACT.Sqrt).then_inc(gate_w_step, 1)

    def prepare_vector(dve):
        dve.wait_ge(w_in[5], 16 * len(lists["ffn2"]))
        dve.tensor_tensor(wsq[:], wg[:], wg[:], ALU.mult).then_inc(gate_w_step, 1)
        dve.wait_ge(gate_w_step, 1)
        dve.tensor_reduce(wnorm[:, 0:1], wsq[:], AX, ALU.add).then_inc(gate_w_step, 1)
        dve.wait_ge(gate_w_step, 3)
        dve.tensor_scalar(wnorm[:, 2:3], wnorm[:, 1:2], 1e-4, None, ALU.max).then_inc(gate_w_step, 1)
        dve.wait_ge(gate_w_step, 4)
        dve.reciprocal(wnorm[:, 3:4], wnorm[:, 2:3]).then_inc(gate_w_step, 1)
        dve.wait_ge(gate_w_step, 5)
        dve.tensor_scalar(wgn[:], wg[:], wnorm[:, 3:4], None, ALU.mult).then_inc(gate_w_step, 2)
        dve.tensor_copy(b2parts[:, 0, :], b2pad[:]).then_inc(b2_step, 1)
        dve.wait_ge(b2_step, 1)
        dve.tensor_tensor(b2pad[:], b2pad[:], b2parts[:, 0, :], ALU.subtract).then_inc(b2_step, 1)
        dve.wait_ge(b2_step, 2)
        dve.tensor_copy(b2parts[:, 1, :], b2pad[:]).then_inc(b2_step, 1)
        dve.wait_ge(b2_step, 3)
        dve.tensor_tensor(b2pad[:], b2pad[:], b2parts[:, 1, :], ALU.subtract).then_inc(b2_step, 1)
        dve.wait_ge(b2_step, 4)
        dve.tensor_copy(b2parts[:, 2, :], b2pad[:]).then_inc(b2_step, 2)

    def prepare_turned_vector(dve):
        dve.wait_ge(gate_w_step, 8)
        dve.tensor_copy(wgnT[:], bank[0][0:16, 0:8]).then_inc(gate_w_step, 1)

    def prepare_gate_vector(dve):
        dve.wait_ge(gate_w_step, 10)
        dve.tensor_copy(gateW[:, 0, :], bank[4][:, 0:8]).then_inc(gate_w_step, 1)

    def tensor2(pe, A):
        weights_in(pe, A)
        norm_tensor(pe, A)
        gate_tensor(pe, A)
        pe.wait_ge(b2_step, 6)

        def down(g, n):
            pe.wait_ge(gated_done[0], 16 * g + n + 1)
            pe.matmul(bank[6][:], F2[:, n, :], gated_ring[:, n % 4, :], start=False, stop=(n == 15))\
              .then_inc(down_done[0], 1)

        def body(g):
            for n in range(16):
                if n % 2 == 0:
                    if not (known_zero(g) and n < 4):
                        pe.wait_ge(gated_done[0], 16 * g + n - 2)
                    pe.matmul(bank[4 + n // 2 % 2][:], sel[:, n // 2, :], gT[:, bass.ts(g, GROUP)],
                              start=True, stop=True).then_inc(bc_done[0], 1)
                if not (known_zero(g) and n < UPS_AHEAD2):
                    up2(pe, g, n)
                if n == 2:
                    if not known_zero(g):
                        back_tensor(pe, A, g - 1, bank[7])
                    for q in range(3):
                        pe.matmul(bank[6][:], b2parts[:, q, :], gT[:, bass.ts(g, GROUP)], start=(q == 0), stop=False)
                if n >= 3:
                    down(g, n - 3)
            for n in range(13, 16):
                down(g, n)

        groups(pe, body)
        back_tensor(pe, A, GROUPS - 1, bank[7])

    def scalar2(act, A):
        weights_in(act, A)
        norm_scalar(act, A)
        gate_scalar(act, A)

        def body(g):
            for n in range(16):
                act.wait_ge(up_done[2], 16 * g + n + 1)
                if not (known_zero(g) and n < 4):
                    act.wait_ge(gated_done[0], 16 * g + n - 3)
                act.activation(act_ring[:, n % 4, :], bank[n % 4][:], ACT.Gelu, bias=f1b[:, n:n + 1])\
                   .then_inc(act_ready[2], 1)
            act.wait_ge(down_done[0], 16 * g + 16)
            if not known_zero(g):
                act.wait_ge(back_done[2], g)
            act.activation(outT[:], bank[6][:], ACT.Copy).then_inc(outT_ready[2], 1)

        groups(act, body)

    def vector2(dve, A, before_last):
        weights_in(dve, A)
        norm_vector(dve, A)
        gate_vector(dve, A)

        def body(g):
            for n in range(16):
                dve.wait_ge(act_ready[2], 16 * g + n + 1)
                if n % 2 == 0:
                    dve.wait_ge(bc_done[0], 8 * g + n // 2 + 1)
                if not (known_zero(g) and n < 4):
                    dve.wait_ge(down_done[0], 16 * g + n - 3)
                dve.tensor_tensor(gated_ring[:, n % 4, :], bank[4 + n // 2 % 2][:], act_ring[:, n % 4, :],
                                  ALU.mult).then_inc(gated_done[0], 1)
                if n == 2 and not known_zero(g):
                    add_vector(dve, A, g - 1, bank[7])

        with_adds(dve, A, bank[7], body, before_last)

    def tensor3(pe, A):
        weights_in(pe, A)
        norm_tensor(pe, A)
        gate_tensor(pe, A)

        def down(g, n):
            pe.wait_ge(gated_done[1], UNITS * g + n + 1)
            pe.matmul(bank[6][:], unit_weights(n)[2], gated_ring[:, n % 4, :], start=(n == 0), stop=(n == UNITS - 1))\
              .then_inc(down_done[1], 1)

        def body(g):
            for n in range(UNITS):
                if n < EXPERTS:
                    if not (known_zero(g) and n < 2):
                        pe.wait_ge(gated_done[1], UNITS * g + (n - 1 if n >= 2 else n - 3))
                    pe.matmul(bank[4 + n % 2][:], sel[:, n, :], gT[:, bass.ts(g, GROUP)],
                              start=True, stop=True).then_inc(bc_done[1], 1)
                if not (known_zero(g) and n < UNITS_AHEAD3):
                    up3(pe, g, n)
                if n == 1 and not known_zero(g):
                    back_tensor(pe, A, g - 1, bank[7])
                if n >= 1:
                    down(g, n - 1)
            down(g, UNITS - 1)

        groups(pe, body)
        back_tensor(pe, A, GROUPS - 1, bank[7])

    def scalar3(act, A):
        weights_in(act, A)
        norm_scalar(act, A)
        gate_scalar(act, A)

        def body(g):
            for n in range(UNITS):
                act.wait_ge(up_done[3], UNITS * g + n + 1)
                if not (known_zero(g) and n < 4):
                    act.wait_ge(prod_step, UNITS * g + n - 3)
                act.activation(act_ring[:, n % 4, :], bank[2 * (n % 2)][:], ACT.Silu).then_inc(act_ready[3], 1)
            act.wait_ge(down_done[1], UNITS * g + UNITS)
            if not known_zero(g):
                act.wait_ge(back_done[3], g)
            act.activation(outT[:], bank[6][:], ACT.Copy).then_inc(outT_ready[3], 1)

        groups(act, body)

    def vector3(dve, A, before_last):
        weights_in(dve, A)
        norm_vector(dve, A)
        gate_vector(dve, A)

        def body(g):
            for n in range(UNITS):
                dve.wait_ge(act_ready[3], UNITS * g + n + 1)
                if not (known_zero(g) and n < 4):
                    dve.wait_ge(down_done[1], UNITS * g + n - 3)
                up_bank = bank[2 * (n % 2) + 1]
                if n < EXPERTS:
                    dve.tensor_tensor(shared_u[:, n % 4, :], up_bank[:], act_ring[:, n % 4, :], ALU.mult)\
                       .then_inc(prod_step, 1)
                    dve.wait_ge(prod_step, UNITS * g + n + 1)
                    dve.wait_ge(bc_done[1], EXPERTS * g + n + 1)
                    dve.tensor_tensor(gated_ring[:, n % 4, :], bank[4 + n % 2][:], shared_u[:, n % 4, :],
                                      ALU.mult).then_inc(gated_done[1], 1)
                else:
                    dve.tensor_tensor(gated_ring[:, n % 4, :], up_bank[:], act_ring[:, n % 4, :], ALU.mult)\
                       .then_inc(prod_step, 1)
                    dve.wait_ge(prod_step, UNITS * g + n + 1)
                    dve.nop().then_inc(gated_done[1], 1)
                if n == 1 and not known_zero(g):
                    add_vector(dve, A, g - 1, bank[7])

        with_adds(dve, A, bank[7], body, before_last)

    def setup_vector(dve):
        dve.memset(onesB[:], 1.0).then_inc(setup_done, 1)
        dve.memset(onesF[:], 1.0).then_inc(setup_done, 1)

    def tensor(pe, A):
        pe.wait_ge(stage_done, A.stages)
        {"ffn0": tensor0, "ffn1": tensor1, "ffn2": tensor2, "ffn3": tensor3}[A.kind](pe, A)

    def scalar(act, A):
        act.wait_ge(stage_done, A.stages)
        {"ffn0": scalar0, "ffn1": scalar1, "ffn2": scalar2, "ffn3": scalar3}[A.kind](act, A)

    def vector(dve, A, before_last):
        {"ffn0": vector0, "ffn1": vector1, "ffn2": vector2, "ffn3": vector3}[A.kind](dve, A, before_last)
        dve.wait_ge(added[A.index], TILES if A.kind == "ffn1" else GROUPS + 1)
        dve.nop().then_inc(stage_done, 1)

    def pool(pool_, A, rsqrt, clear_next):
        rsqrt(pool_, 0, EARLY, A.ln)
        rsqrt(pool_, EARLY, TILES, A.ln + 1)
        pool_.wait_ge(stage_done, A.stages)
        clear_next()
        if A.kind == "ffn1":
            rsqrt(pool_, 0, 1, A.ln + 2)
            pool1(pool_, A)

    F.early_stats = early_stats
    F.n_loads = lambda kind: len(lists[kind])
    F.loads, F.setup_vector, F.tensor, F.scalar, F.vector, F.pool = loads, setup_vector, tensor, scalar, vector, pool
    return F


def kernel(**inputs):
    import ml_dtypes
    import numpy as np
    import concourse.bacc as bacc
    from concourse.bass_utils import run_bass_kernel_spmd

    a, outs = lay_out(np, ml_dtypes, **{k: np.asarray(v) for k, v in inputs.items()})
    nc = bacc.Bacc("TRN2", target_bir_lowering=False, num_devices=1)
    w = {n: nc.dram_tensor("in_" + n, v.shape, mybir.dt.from_np(v.dtype), kind="ExternalInput").ap()
         for n, v in a.items()}
    out = nc.dram_tensor("out_x", outs, F32, kind="ExternalOutput").ap()
    build(nc, w, out, len(LAYERS))
    r = run_bass_kernel_spmd(nc, [{"in_" + n: v for n, v in a.items()}], core_ids=[0])
    y = r.results[0]["out_x"]
    return y.transpose(1, 0, 2).reshape(BATCH, SEQ, D)


def lay_out(np, ml_dtypes, **i):
    bf = ml_dtypes.bfloat16
    c = np.ascontiguousarray

    def col(v, n=1):
        return c(v.reshape(n, -1).T)

    tri = np.where(np.arange(P)[None, :] <= np.arange(P)[:, None], 0.0, -1e30)
    sel = np.zeros((P, EXPERTS, P), np.float32)
    for e in range(EXPERTS):
        sel[[e, 32 + e, 64 + e], e, :] = 1.0
    b2pad = np.zeros((P, D), np.float32)
    for r in (0, 32, 64):
        b2pad[r:r + EXPERTS] = i["L2_ffn_b2"]
    ctx = i["ctx_1024"]
    wkv = i["L1_xattn_Wkv"]
    a = dict(
        x=c(i["x"].reshape(TILES, P, D).transpose(1, 0, 2)),
        ctxT=c(ctx.reshape(TOKENS, D).T),
        ctx=c(ctx.reshape(BATCH, TPB, P, D).transpose(0, 2, 1, 3)),
        rowmask=c(i["mask_BxS_ik0"].reshape(TILES, P).T),
        keymask=c(i["mask_Bx1x1xS2_ff0"].reshape(1, TOKENS)),
        ident=np.eye(P, dtype=np.float32), identB=np.eye(P, dtype=np.float32).astype(bf),
        triB=c(np.stack([tri, tri], 1).astype(bf)),
        headmask=c((np.arange(P)[:, None] // 8 == np.arange(HEADS)[None, :]).astype(np.float32)),
        W1T=c(i["L0_ffn_W1"].T), b1c=col(i["L0_ffn_b1"], 4), b2c=col(i["L0_ffn_b2"]),
        W2T=c(i["L0_ffn_W2"].T.reshape(4, P, D).transpose(1, 0, 2).reshape(P, 512)),
        WQ1=c(i["L1_xattn_Wq"]), WK1=c(wkv[:, :1024]), WV1=c(wkv[:, 1024:]),
        WO1=c(i["L1_xattn_Wout"].reshape(PAIRS, P, D).transpose(1, 0, 2)), bo1=col(i["L1_xattn_bout"]),
        gamma=col(i["L1_ffn_bn_gamma"]), beta=col(i["L1_ffn_bn_beta"]),
        WKQ=c(i["L1_ffn_w_q"].reshape(16, P, D).transpose(1, 0, 2)),
        keysT=c(i["L1_ffn_keys_p"].transpose(3, 0, 2, 1).reshape(P, 512)),
        downT=c(i["L1_ffn_down"][:NE_USED].T), up=c(i["L1_ffn_up"][:NE_USED].reshape(CHUNKS, P, D).transpose(1, 0, 2)),
        WQ2=c(i["L2_xattn_Wq"].T), WK2=c(i["L2_xattn_Wk"].T), WV2=c(i["L2_xattn_Wv"].T), WO2=c(i["L2_xattn_Wo"].T),
        bq2=col(i["L2_xattn_bq"]), bk2=col(i["L2_xattn_bk"]), bo2=col(i["L2_xattn_bo"]),
        bv2=c(np.broadcast_to(i["L2_xattn_bv"], (P, D))),
        F1=c(i["L2_ffn_W1"].transpose(1, 0, 2)), f1b=c(i["L2_ffn_b1"].reshape(16, P).T),
        F2=c(i["L2_ffn_W2"].reshape(16, P, D).transpose(1, 0, 2)), b2pad=b2pad,
        wredT=c(i["L2_ffn_w_red"].T), wg=c(i["L2_ffn_wg"]),
        sel=sel.astype(bf), iota8=c(np.broadcast_to(np.arange(8, dtype=np.float32), (P, 8))),
        before=(np.arange(P)[:, None] < np.arange(P)[None, :]).astype(bf),
        WQ3=c(i["L3_xattn_Wq"]), WK3=c(i["L3_xattn_Wk"]), WV3=c(i["L3_xattn_Wv"]),
        WO3=c(i["L3_xattn_Wo"].reshape(PAIRS, P, D).transpose(1, 0, 2)),
        gateW3=c(i["L3_ffn_gate_w"].T), WG=c(i["L3_ffn_we_gate"].transpose(2, 0, 1)),
        WU=c(i["L3_ffn_we_up"].transpose(2, 0, 1)), WD=c(i["L3_ffn_we_down"].transpose(2, 0, 1)),
        SG=c(i["L3_ffn_ws_gate"].T.reshape(P, 2, P)), SU=c(i["L3_ffn_ws_up"].T.reshape(P, 2, P)),
        SD=c(i["L3_ffn_ws_down"].T.reshape(2, P, D).transpose(1, 0, 2)),
    )
    return a, (P, TILES, D)
```
